# Optimizing a Trainium2 kernel written in Bass

```python
import numpy as np
import jax
import jax.numpy as jnp

def _softmax(x, axis=-1):
    return jax.nn.softmax(x, axis=axis)

def _gelu(x):
    return jax.nn.gelu(x, approximate=True)

def _silu(x):
    return jax.nn.silu(x)

def _sigmoid(x):
    return jax.nn.sigmoid(x)

def _layernorm(x, axis=-1, eps=1e-05):
    m = jnp.mean(x, axis=axis, keepdims=True)
    v = jnp.var(x, axis=axis, keepdims=True)
    return (x - m) / jnp.sqrt(v + eps)

def _scatter_add(tgt, idx, src, axis=0):
    return tgt.at[idx].add(src)

def _segment_sum(src, seg, n):
    return jax.ops.segment_sum(src, seg, n)
kernel_name = 'mk_gnn_resnorm_d4_gnn_r32_8551e0'

def setup_inputs(seed: int=0):
    np.random.seed(seed)
    _w = jnp.asarray

    def _rec_inputs():
        import jax
        import jax.numpy as jnp
        _gk = jax.random.key(seed)
        x = -0.000202 + 1 * jax.random.normal(jax.random.fold_in(_gk, 1), (50000, 128), jnp.float32)
        src = jax.random.randint(jax.random.fold_in(_gk, 2), (50000,), 0, 50000, jnp.int32)
        dst = jax.random.randint(jax.random.fold_in(_gk, 3), (50000,), 0, 50000, jnp.int32)
        _o = jnp.argsort(dst, stable=True)
        src = src[_o]
        dst = dst[_o]
        return (x, src, dst)
    x, src, dst = _rec_inputs()

    def _L0_gnn_setup():
        import jax, jax.numpy as jnp
        import numpy as np
        N_NODES = 50000
        N_EDGES = 25000
        IN_FEAT = 128
        OUT_FEAT = 128
        key = jax.random.key(seed)
        ks = jax.random.split(key, 9)
        s = 1.0 / np.sqrt(IN_FEAT)
        return {'x': jax.random.normal(ks[0], (N_NODES, IN_FEAT), dtype=jnp.float32), 'src': jax.random.randint(ks[1], (N_EDGES,), 0, N_NODES), 'dst': jax.random.randint(ks[2], (N_EDGES,), 0, N_NODES), 'W1': jax.random.uniform(ks[3], (IN_FEAT, OUT_FEAT), jnp.float32, -s, s), 'b1': jax.random.uniform(ks[4], (OUT_FEAT,), jnp.float32, -s, s), 'W2': jax.random.uniform(ks[5], (OUT_FEAT, 1), jnp.float32, -s, s), 'b2': jax.random.uniform(ks[6], (1,), jnp.float32, -s, s), 'W4': jax.random.uniform(ks[7], (IN_FEAT, OUT_FEAT), jnp.float32, -s, s), 'b4': jax.random.uniform(ks[8], (OUT_FEAT,), jnp.float32, -s, s)}
    _L0_gnn_all = _L0_gnn_setup()
    _L0_gnn_in = {k: v for k, v in _L0_gnn_all.items() if k in ('W1', 'b1', 'W2', 'b2', 'W4', 'b4')}
    del _L0_gnn_all

    def _L1_gnn_setup():
        import jax, jax.numpy as jnp
        import numpy as np

        def _gcn_conv(x, src, dst, deg_inv_sqrt, W, b):
            norm = deg_inv_sqrt[src] * deg_inv_sqrt[dst]
            h = x @ W
            msgs = h[src] * norm[:, None]
            out = jax.ops.segment_sum(msgs, dst, num_segments=x.shape[0])
            return out + b
        key = jax.random.key(seed)
        ks = jax.random.split(key, 6)
        N, E, C = (3125, 50000, 128)
        scale = 1.0 / np.sqrt(C)
        return {'x': jax.random.normal(ks[0], (N, C), dtype=jnp.float32), 'edge_index': jax.random.randint(ks[1], (2, E), 0, N, dtype=jnp.int64), 'W1': jax.random.normal(ks[2], (C, C), dtype=jnp.float32) * scale, 'b1': jnp.zeros((C,), dtype=jnp.float32), 'W2': jax.random.normal(ks[3], (C, C), dtype=jnp.float32) * scale, 'b2': jnp.zeros((C,), dtype=jnp.float32)}
    _L1_gnn_all = _L1_gnn_setup()
    _L1_gnn_in = {k: v for k, v in _L1_gnn_all.items() if k in ('W1', 'b1', 'W2', 'b2')}
    del _L1_gnn_all

    def _L2_gnn_setup():
        import jax, jax.numpy as jnp
        import numpy as np
        N_NODES = 50000
        N_EDGES = 18750
        IN_CH = 128
        HEADS = 4
        OUT_CH = 32
        NEG_SLOPE = 0.2
        key = jax.random.key(seed)
        k1, k2, k3, k4, k5 = jax.random.split(key, 5)
        x = jax.random.normal(k1, (N_NODES, IN_CH), dtype=jnp.float32)
        src = jax.random.randint(k2, (N_EDGES,), 0, N_NODES)
        dst = jax.random.randint(k3, (N_EDGES,), 0, N_NODES)
        dst = jnp.where(src == dst, (dst + 1) % N_NODES, dst)
        edge_index = jnp.stack([src, dst]).astype(jnp.int32)
        weight = jax.random.normal(k4, (IN_CH, HEADS * OUT_CH), dtype=jnp.float32) / np.sqrt(IN_CH)
        att = jax.random.normal(k5, (1, HEADS, 2 * OUT_CH), dtype=jnp.float32) * 0.1
        bias = jnp.zeros((HEADS * OUT_CH,), dtype=jnp.float32)
        return {'x': x, 'edge_index': edge_index, 'weight': weight, 'att': att, 'bias': bias}
    _L2_gnn_all = _L2_gnn_setup()
    _L2_gnn_in = {k: v for k, v in _L2_gnn_all.items() if k in ('weight', 'att', 'bias')}
    del _L2_gnn_all

    def _L3_gnn_setup():
        import jax, jax.numpy as jnp
        import numpy as np
        import math
        N_NODES = 3125
        N_EDGES = 50000
        DIM = 128
        key = jax.random.key(seed)
        ks = jax.random.split(key, 6)
        x = jax.random.normal(ks[0], (N_NODES, DIM), dtype=jnp.float32)
        edge_index = jax.random.randint(ks[1], (2, N_EDGES), 0, N_NODES, dtype=jnp.int64)
        limit = 0.1 * math.sqrt(6.0 / (DIM + DIM))
        Wqk = jax.random.uniform(ks[2], (DIM, DIM), dtype=jnp.float32, minval=-limit, maxval=limit)
        Wv = jax.random.uniform(ks[3], (DIM, DIM), dtype=jnp.float32, minval=-limit, maxval=limit)
        Wo = jax.random.uniform(ks[4], (DIM, DIM), dtype=jnp.float32, minval=-limit, maxval=limit)
        return {'x': x, 'edge_index': edge_index, 'Wqk': Wqk, 'bqk': jnp.zeros((DIM,), jnp.float32), 'Wv': Wv, 'bv': jnp.zeros((DIM,), jnp.float32), 'Wo': Wo, 'bo': jnp.zeros((DIM,), jnp.float32), 'gamma': jnp.ones((DIM,), jnp.float32), 'beta': jnp.zeros((DIM,), jnp.float32)}
    _L3_gnn_all = _L3_gnn_setup()
    _L3_gnn_in = {k: v for k, v in _L3_gnn_all.items() if k in ('Wqk', 'bqk', 'Wv', 'bv', 'Wo', 'bo', 'gamma', 'beta')}
    del _L3_gnn_all
    return {'x': x, 'src': src, 'dst': dst, 'L0_gnn_W1': _L0_gnn_in['W1'], 'L0_gnn_b1': _L0_gnn_in['b1'], 'L0_gnn_W2': _L0_gnn_in['W2'], 'L0_gnn_b2': _L0_gnn_in['b2'], 'L0_gnn_W4': _L0_gnn_in['W4'], 'L0_gnn_b4': _L0_gnn_in['b4'], 'L1_gnn_W1': _L1_gnn_in['W1'], 'L1_gnn_b1': _L1_gnn_in['b1'], 'L1_gnn_W2': _L1_gnn_in['W2'], 'L1_gnn_b2': _L1_gnn_in['b2'], 'L2_gnn_weight': _L2_gnn_in['weight'], 'L2_gnn_att': _L2_gnn_in['att'], 'L2_gnn_bias': _L2_gnn_in['bias'], 'L3_gnn_Wqk': _L3_gnn_in['Wqk'], 'L3_gnn_bqk': _L3_gnn_in['bqk'], 'L3_gnn_Wv': _L3_gnn_in['Wv'], 'L3_gnn_bv': _L3_gnn_in['bv'], 'L3_gnn_Wo': _L3_gnn_in['Wo'], 'L3_gnn_bo': _L3_gnn_in['bo'], 'L3_gnn_gamma': _L3_gnn_in['gamma'], 'L3_gnn_beta': _L3_gnn_in['beta']}

def reference(x, src, dst, L0_gnn_W1, L0_gnn_b1, L0_gnn_W2, L0_gnn_b2, L0_gnn_W4, L0_gnn_b4, L1_gnn_W1, L1_gnn_b1, L1_gnn_W2, L1_gnn_b2, L2_gnn_weight, L2_gnn_att, L2_gnn_bias, L3_gnn_Wqk, L3_gnn_bqk, L3_gnn_Wv, L3_gnn_bv, L3_gnn_Wo, L3_gnn_bo, L3_gnn_gamma, L3_gnn_beta):
    import jax
    import jax.numpy as jnp

    def _L0_gnn_ref(x, src, dst, W1, b1, W2, b2, W4, b4):
        import jax, jax.numpy as jnp
        import numpy as np
        N_NODES = 50000
        N_EDGES = 25000
        IN_FEAT = 128
        OUT_FEAT = 128
        n_nodes = x.shape[0]
        theta = x[dst] - x[src]
        w = jax.nn.sigmoid(jax.nn.relu(theta @ W1 + b1) @ W2 + b2)
        w_theta = w * theta
        agg = jax.ops.segment_sum(w_theta, dst, num_segments=n_nodes)
        indeg = jax.ops.segment_sum(jnp.ones((dst.shape[0], 1), x.dtype), dst, num_segments=n_nodes)
        return agg + indeg * (x @ W4 + b4)

    def _L1_gnn_ref(x, edge_index, W1, b1, W2, b2):
        import jax, jax.numpy as jnp
        import numpy as np

        def _gcn_conv(x, src, dst, deg_inv_sqrt, W, b):
            norm = deg_inv_sqrt[src] * deg_inv_sqrt[dst]
            h = x @ W
            msgs = h[src] * norm[:, None]
            out = jax.ops.segment_sum(msgs, dst, num_segments=x.shape[0])
            return out + b
        N = x.shape[0]
        self_loops = jnp.arange(N, dtype=edge_index.dtype)
        src = jnp.concatenate([edge_index[0], self_loops])
        dst = jnp.concatenate([edge_index[1], self_loops])
        deg = jax.ops.segment_sum(jnp.ones_like(src, dtype=x.dtype), dst, num_segments=N)
        deg_inv_sqrt = jnp.where(deg > 0, jax.lax.rsqrt(deg), 0.0)
        h = jax.nn.relu(_gcn_conv(x, src, dst, deg_inv_sqrt, W1, b1))
        h = jax.nn.relu(_gcn_conv(h, src, dst, deg_inv_sqrt, W2, b2))
        return h

    def _L2_gnn_ref(x, edge_index, weight, att, bias):
        import jax, jax.numpy as jnp
        import numpy as np
        N_NODES = 50000
        N_EDGES = 18750
        IN_CH = 128
        HEADS = 4
        OUT_CH = 32
        NEG_SLOPE = 0.2
        n = x.shape[0]
        h = (x @ weight).reshape(n, HEADS, OUT_CH)
        loop = jnp.arange(n, dtype=edge_index.dtype)
        row = jnp.concatenate([edge_index[0], loop])
        col = jnp.concatenate([edge_index[1], loop])
        x_i = h[row]
        x_j = h[col]
        wl = att[:, :, :OUT_CH]
        wr = att[:, :, OUT_CH:]
        alpha = (x_i * wl).sum(-1) + (x_j * wr).sum(-1)
        alpha = jax.nn.leaky_relu(alpha, NEG_SLOPE)
        amax = jax.ops.segment_max(alpha, row, num_segments=n)
        alpha = jnp.exp(alpha - amax[row])
        denom = jax.ops.segment_sum(alpha, row, num_segments=n)
        alpha = alpha / (denom[row] + 1e-16)
        out = jax.ops.segment_sum(x_j * alpha[:, :, None], row, num_segments=n)
        return out.reshape(n, HEADS * OUT_CH) + bias

    def _L3_gnn_ref(x, edge_index, Wqk, bqk, Wv, bv, Wo, bo, gamma, beta):
        import jax, jax.numpy as jnp
        import numpy as np
        import math
        N_NODES = 3125
        N_EDGES = 50000
        DIM = 128
        N, D = x.shape
        qk = x @ Wqk + bqk
        v = x @ Wv + bv
        src = edge_index[0]
        dst = edge_index[1]
        scores = jnp.sum(qk[dst] * qk[src], axis=-1) / jnp.sqrt(jnp.float32(D))
        scores = jnp.clip(scores, -5.0, 5.0)
        m = jax.ops.segment_max(scores, dst, num_segments=N)
        e = jnp.exp(scores - m[dst])
        s = jax.ops.segment_sum(e, dst, num_segments=N)
        attn = e / s[dst]
        out = jax.ops.segment_sum(attn[:, None] * v[src], dst, num_segments=N)
        out = out @ Wo + bo
        h = out + x
        mu = jnp.mean(h, axis=-1, keepdims=True)
        var = jnp.mean(jnp.square(h - mu), axis=-1, keepdims=True)
        return gamma * (h - mu) / jnp.sqrt(var + 1e-05) + beta
    edge_index = jnp.stack([src, dst])
    x = _layernorm(x + _L0_gnn_ref(x, src, dst, L0_gnn_W1, L0_gnn_b1, L0_gnn_W2, L0_gnn_b2, L0_gnn_W4, L0_gnn_b4), axis=-1)
    x = _layernorm(x + _L1_gnn_ref(x, edge_index, L1_gnn_W1, L1_gnn_b1, L1_gnn_W2, L1_gnn_b2), axis=-1)
    x = _layernorm(x + _L2_gnn_ref(x, edge_index, L2_gnn_weight, L2_gnn_att, L2_gnn_bias), axis=-1)
    x = _layernorm(x + _L3_gnn_ref(x, edge_index, L3_gnn_Wqk, L3_gnn_bqk, L3_gnn_Wv, L3_gnn_bv, L3_gnn_Wo, L3_gnn_bo, L3_gnn_gamma, L3_gnn_beta), axis=-1)
    return x

_drawn_inputs = setup_inputs


def setup_inputs(seed=0):
    import zlib

    import numpy as np

    out = dict(_drawn_inputs(seed))
    spreads = {'L1_gnn_b1': (0.0, 0.1),
     'L1_gnn_b2': (0.0, 0.1),
     'L2_gnn_bias': (0.0, 0.1),
     'L3_gnn_bqk': (0.0, 2.0),
     'L3_gnn_bv': (0.0, 0.8),
     'L3_gnn_bo': (0.0, 0.1),
     'L3_gnn_gamma': (1.0, 0.2),
     'L3_gnn_beta': (0.0, 0.1)}
    factors = {'L0_gnn_b1': 43.706, 'L3_gnn_Wqk': 64.0, 'L3_gnn_Wv': 8.0, 'L3_gnn_Wo': 8.0}
    for name, (base, spread) in spreads.items():
        noise = np.random.default_rng([zlib.crc32(name.encode()), seed]).standard_normal(out[name].shape)
        drawn = base * np.exp(spread * noise) if base else spread * noise
        out[name] = jnp.asarray(drawn.astype(out[name].dtype))
    for name, factor in factors.items():
        out[name] = (out[name] * factor).astype(out[name].dtype)
    return out
```

```python
from contextlib import ExitStack

import numpy as np
import concourse.bass as bass
from concourse import mybir
from concourse.alu_op_type import AluOpType as ALU

F32, I32 = mybir.dt.float32, mybir.dt.int32
F16, BF16 = mybir.dt.float16, mybir.dt.bfloat16
ACT = mybir.ActivationFunctionType
AX = mybir.AxisListType

N = 50000
E = 50000
D = 128
HEADS, HC = 4, 32
NT = 100
TILES = N // NT
W = 128
EP = 125
CH = E // EP
B = 4
MAIN = 504
PLACE = 512
MAXI = 896
MAGIC = 12582912.0
BIG = 131072.0
HI, LO = 25, 20
SPLIT = 2048
KEYS = ("dst", "src")
EPS = 1e-5
NRING = 4


def wait(eng, sem, value):
    if not isinstance(value, int) or value > 0:
        eng.wait_ge(sem, value)


def turns(eng, first, last, lag, body):
    head = first + lag + NRING
    head += (-head) % NRING
    tail = head + (last - 1 - head) // NRING * NRING

    def peeled(s):
        body(s, s % NRING, lambda k: first <= s - k < last)

    for s in range(first, head):
        peeled(s)
    with eng.Fori(head // NRING, tail // NRING) as r:
        for q in range(NRING):
            body(r * NRING + q, q, lambda k: True)
    for s in range(tail, last + lag):
        peeled(s)


def lap(t):
    return t // NRING + 1


def waits_apart(eng, passed, pairs):
    for sem, value in pairs:
        wait(eng, sem, value)
    eng.sem_inc(passed, 1)


class Steps:

    def __init__(self, eng, sem, per):
        self.eng, self.sem, self.per = eng, sem, per

    def begin(self, t):
        self.base, self.n = t * self.per, 0

    def mark(self, ins):
        self.n += 1
        assert self.n <= self.per
        return ins.then_inc(self.sem, 1)

    def sync(self):
        self.eng.wait_ge(self.sem, self.base + self.n)

    def end(self):
        assert self.n == self.per, (self.n, self.per)


def both_ranges(eng, total_ap, run):
    run(0, MAIN // B)
    total = eng.value_load(total_ap, min_val=0, max_val=MAXI)
    with eng.If(total > MAIN):
        run(MAIN // B, MAXI // B)
    with eng.Else():
        pass


class Mem:

    def __init__(self, nc, ctx, tag):
        self.nc, self.ctx, self.tag, self.held = nc, ctx, tag, []
        ctx.callback(self.release)

    def release(self):
        if self.held:
            self.nc.clear_and_free_semaphores(self.held)
            self.nc.all_engine_barrier()

    def sb(self, name, shape, dt=F32):
        return self.ctx.enter_context(self.nc.sbuf_tensor(f"{self.tag}_{name}", shape, dt))

    def ps(self, name, shape, dt=F32):
        return self.ctx.enter_context(self.nc.psum_tensor(f"{self.tag}_bank_{name}", shape, dt))

    def sems(self, name):
        return [self.sem(f"{name}_{q}") for q in range(NRING)]

    def sem(self, name):
        self.held.append(self.nc.alloc_semaphore(f"{self.tag}_{name}"))
        return self.held[-1]



def sort_edges(nc, keep, key_dram, hist_dram, rows_dram, const):
    tab = {k: {} for k in KEYS}
    for k in KEYS:
        t = tab[k]
        t["other"] = keep.sb(f"other_{k}", [W, MAXI], I32)
        t["local"] = keep.sb(f"local_{k}", [W, MAXI])
        t["total"] = keep.sb(f"total_{k}", [1, 1], I32)
        t["keep"] = keep.sb(f"keep_{k}", [128, MAXI])
        t["first"] = keep.sb(f"first_{k}", [128, MAXI])
        t["row"] = keep.sb(f"row_{k}", [1, MAXI], I32)
        t["last"] = keep.sb(f"last_{k}", [1, MAXI], I32)
        t["plain"] = keep.sb(f"plain_{k}", [1, MAXI // B], I32)
        t["carry"] = keep.sb(f"carry_{k}", [1, MAXI // B], I32)
        t["again"] = keep.sb(f"again_{k}", [1, MAXI // B], I32)

    with ExitStack() as outer:
        m = Mem(nc, outer, "sort")
        iota_i = m.sb("iota_i", [128, MAXI], I32)
        iota_h = m.sb("iota_h", [128, MAXI], F16)
        iota_f = m.sb("iota_f", [128, HI])
        item_no = m.sb("item_no", [128, MAXI // 128])
        item_no_i = m.sb("item_no_i", [128, MAXI // 128], I32)
        diff_i = m.sb("diff_i", [128, 128], I32)
        earlier = m.sb("earlier", [EP, EP], F16)
        not_earlier = m.sb("not_earlier", [EP, EP], F16)
        big_eye = m.sb("big_eye", [EP, EP], BF16)
        neg_big_eye = m.sb("neg_big_eye", [EP, EP], BF16)
        ones_row = m.sb("ones_row", [1, EP])
        neg_big = m.sb("neg_big", [128, 1])
        node_i = {k: m.sb(f"node_i_{k}", [EP, CH], I32) for k in KEYS}
        node = {k: m.sb(f"node_{k}", [EP, CH]) for k in KEYS}
        tile = {k: m.sb(f"tile_{k}", [EP, CH]) for k in KEYS}
        low = {k: m.sb(f"low_{k}", [EP, CH]) for k in KEYS}
        high = {k: m.sb(f"high_{k}", [EP, CH]) for k in KEYS}
        pos = {k: m.sb(f"pos_{k}", [EP, CH]) for k in KEYS}
        item = {k: m.sb(f"item_{k}", [EP, CH]) for k in KEYS}
        start = {k: m.sb(f"start_{k}", [128, TILES]) for k in KEYS}
        end = {k: m.sb(f"end_{k}", [128, TILES]) for k in KEYS}
        base = {k: m.sb(f"base_{k}", [128, TILES]) for k in KEYS}

        G = 20
        with ExitStack() as inner:
            p = Mem(nc, inner, "hist")
            thi = {k: p.sb(f"thi_{k}", [EP, CH]) for k in KEYS}
            tlo = {k: p.sb(f"tlo_{k}", [EP, CH]) for k in KEYS}
            hot_hi = {k: p.sb(f"hot_hi_{k}", [EP, 2, G, HI]) for k in KEYS}
            hot_lo = {k: p.sb(f"hot_lo_{k}", [EP, 2, G, LO]) for k in KEYS}
            hist = {k: p.ps(f"hist_{k}", [HI, LO]) for k in KEYS}
            hist_sb = p.sb("hist_sb", [HI, 2, LO])
            iotas, loaded, step = p.sem("iotas_ready"), p.sem("edges_loaded"), p.sem("vector_step")
            hot_ready, counted = p.sem("one_hots_ready"), p.sem("chunks_counted")
            hist_ready, stored, spread = p.sem("histogram_ready"), p.sem("histogram_stored"), p.sem("histogram_spread")
            with nc.Block() as block:

                @block.sync
                def _(sp):
                    for k in KEYS:
                        sp.dma_start(node_i[k][:, :], key_dram[k].rearrange("(p c) -> p c", c=CH)).then_inc(loaded, 16)
                    sp.wait_ge(hist_ready, 1)
                    for n, k in enumerate(KEYS):
                        sp.dma_start(hist_dram[k].rearrange("(h l) -> h l", l=LO), hist_sb[:, n, :]).then_inc(stored, 16)
                    sp.wait_ge(stored, 32)
                    for k in KEYS:
                        row = hist_dram[k].rearrange("(a t) -> a t", a=1)
                        sp.dma_start(base[k][:, :], row.broadcast_to([128, TILES])).then_inc(spread, 16)

                @block.gpsimd
                def _(pool):
                    pool.iota(iota_i[:, :], [[1, MAXI]], base=0, channel_multiplier=0)
                    pool.iota(item_no_i[:, :], [[128, MAXI // 128]], base=0, channel_multiplier=1)
                    pool.iota(diff_i[:, :], [[1, 128]], base=0, channel_multiplier=-1).then_inc(iotas, 1)

                @block.vector
                def _(dve):
                    c = Steps(dve, step, 10 ** 6)
                    c.begin(0)

                    def do(ins):
                        c.mark(ins)
                        c.sync()

                    def rounded(out, in_, scale, shift):
                        do(dve.tensor_scalar(out, in_, scale, shift, ALU.mult, ALU.add))
                        do(dve.tensor_scalar(out, out, MAGIC, MAGIC, ALU.add, ALU.subtract))

                    dve.wait_ge(iotas, 1)
                    dve.tensor_copy(iota_h[:, :], iota_i[:, :])
                    dve.tensor_copy(iota_f[:, :], iota_i[:, 0:HI])
                    dve.tensor_copy(item_no[:, :], item_no_i[:, :])
                    below = diff_i[0:EP, 0:EP]
                    dve.tensor_scalar(earlier[:, :], below, 0.0, None, ALU.is_gt)
                    dve.tensor_scalar(not_earlier[:, :], below, 0.0, None, ALU.is_le)
                    dve.tensor_scalar(big_eye[:, :], below, 0.0, BIG, ALU.is_equal, ALU.mult)
                    dve.tensor_scalar(neg_big_eye[:, :], below, 0.0, -BIG, ALU.is_equal, ALU.mult)
                    dve.tensor_scalar(const["eye"][:, :], diff_i[:, :], 0.0, None, ALU.is_equal)
                    dve.tensor_scalar(const["neg_eye"][:, :], diff_i[:, :], 0.0, -1.0, ALU.is_equal, ALU.mult)
                    dve.tensor_copy(const["iota"][:, :], iota_i[:, 0:NT])
                    dve.memset(neg_big[:, :], -BIG)
                    do(dve.memset(ones_row[:, :], 1.0))
                    dve.wait_ge(loaded, 32)
                    for k in KEYS:
                        do(dve.tensor_copy(node[k][:, :], node_i[k][:, :]))
                    for k, o in zip(KEYS, reversed(KEYS)):
                        rounded(tile[k][:, :], node[k][:, :], 1.0 / NT, -0.495)
                        rounded(thi[k][:, :], tile[k][:, :], 1.0 / LO, -0.475)
                        do(dve.scalar_tensor_tensor(tlo[k][:, :], thi[k][:, :], -float(LO), tile[k][:, :], ALU.mult, ALU.add))
                        rounded(item[k][:, :], node[o][:, :], 1.0 / SPLIT, -0.49975)
                        do(dve.scalar_tensor_tensor(low[k][:, :], item[k][:, :], -float(SPLIT), node[o][:, :], ALU.mult, ALU.add))
                        do(dve.tensor_scalar(low[k][:, :], low[k][:, :], 1.0, None, ALU.add))
                        do(dve.scalar_tensor_tensor(pos[k][:, :], tile[k][:, :], -float(NT), node[k][:, :], ALU.mult, ALU.add))
                        do(dve.tensor_scalar(pos[k][:, :], pos[k][:, :], NT / 2.0, float(HI), ALU.subtract, ALU.mult))
                        do(dve.tensor_tensor(high[k][:, :], pos[k][:, :], item[k][:, :], ALU.add))
                    for s in range(CH // G):
                        wait(dve, counted, 2 * (s - 1))
                        for k in KEYS:
                            at = slice(s * G, (s + 1) * G)
                            dve.tensor_tensor(hot_hi[k][:, s % 2], iota_f[0:EP, :].unsqueeze(1).broadcast_to([EP, G, HI]),
                                              thi[k][:, at].unsqueeze(2).broadcast_to([EP, G, HI]), ALU.is_equal)
                            dve.tensor_tensor(hot_lo[k][:, s % 2], iota_f[0:EP, 0:LO].unsqueeze(1).broadcast_to([EP, G, LO]),
                                              tlo[k][:, at].unsqueeze(2).broadcast_to([EP, G, LO]), ALU.is_equal).then_inc(hot_ready, 1)
                    dve.wait_ge(counted, 2 * (CH // G))
                    dve.tensor_copy(hist_sb[:, 0, :], hist["dst"][:, :])
                    dve.tensor_copy(hist_sb[:, 1, :], hist["src"][:, :]).then_inc(hist_ready, 1)

                    dve.wait_ge(spread, 32)
                    for n, k in enumerate(KEYS):
                        rounded(start[k][:, :], base[k][:, :], 1.0 / W, (W - 1) / W - 0.498)
                        do(dve.tensor_scalar(start[k][:, :], start[k][:, :], 1.0, None, ALU.max))
                        do(dve.tensor_tensor_scan(end[k][:, :], start[k][:, :], start[k][:, :], 0.0, ALU.add, ALU.bypass))
                        do(dve.tensor_tensor(start[k][:, :], end[k][:, :], start[k][:, :], ALU.subtract))
                        do(dve.tensor_scalar(base[k][:, :], start[k][:, :], float(W), None, ALU.mult))
                        do(dve.tensor_copy(tab[k]["total"][:, :], end[k][0:1, TILES - 1:TILES]))

                @block.tensor
                def _(pe):
                    for s in range(CH // G):
                        for n, k in enumerate(KEYS):
                            pe.wait_ge(hot_ready, 2 * s + n + 1)
                            for g in range(G):
                                last = pe.matmul(hist[k][:, :], hot_hi[k][:, s % 2, g, :], hot_lo[k][:, s % 2, g, :],
                                                 start=(s == 0 and g == 0), stop=(s == CH // G - 1 and g == G - 1))
                            last.then_inc(counted, 1)

        with ExitStack() as inner:
            p = Mem(nc, inner, "flags")
            NG = MAXI // 128
            junk = p.sb("junk", [128, TILES])
            col = {k: p.sb(f"col_{k}", [128, 3, NG]) for k in KEYS}
            tiles = {k: p.sb(f"tiles_{k}", [1, MAXI]) for k in KEYS}
            lasts = {k: p.sb(f"lasts_{k}", [1, MAXI]) for k in KEYS}
            f1 = p.sb("f1", [1, MAXI // B])
            f2 = p.sb("f2", [1, MAXI // B])
            step, cols, stored, spread = p.sem("vector_step"), p.sem("columns_ready"), p.sem("stored"), p.sem("spread")
            with nc.Block() as block:

                @block.sync
                def _(sp):
                    for n, k in enumerate(KEYS):
                        sp.wait_ge(cols, n + 1)
                        for w in range(3):
                            sp.dma_start(rows_dram[k][w].rearrange("(g p) -> p g", p=128), col[k][:, w, :],
                                         allow_slow_non_contiguous=True).then_inc(stored, 16)
                    sp.wait_ge(stored, 96)
                    for k in KEYS:
                        row = [rows_dram[k][w].rearrange("(a t) -> a t", a=1) for w in range(3)]
                        sp.dma_start(tiles[k][:, :], row[0]).then_inc(spread, 16)
                        sp.dma_start(tab[k]["first"][:, :], row[1].broadcast_to([128, MAXI])).then_inc(spread, 16)
                        sp.dma_start(lasts[k][:, :], row[2]).then_inc(spread, 16)

                @block.vector
                def _(dve):
                    c = Steps(dve, step, 10 ** 6)
                    c.begin(0)

                    def do(ins):
                        c.mark(ins)
                        c.sync()

                    for k in KEYS:
                        do(dve.tensor_scalar(end[k][:, :], end[k][:, :], 1.0, None, ALU.subtract))
                        for g in range(NG):
                            for w, (row, op) in enumerate(((start, ALU.is_le), (start, ALU.is_equal), (end, ALU.is_equal))):
                                do(dve.tensor_scalar(junk[:, :], row[k][:, :], item_no[:, g:g + 1], 0.0, op, ALU.add,
                                                     accum_out=col[k][:, w, g:g + 1]))
                        do(dve.tensor_scalar(col[k][:, 0, :], col[k][:, 0, :], 1.0, None, ALU.subtract))
                        dve.sem_inc(cols, 1)
                    dve.wait_ge(spread, 96)
                    for k in KEYS:
                        t = tab[k]
                        by4 = tiles[k][:, :].rearrange("a (b j) -> a b j", j=B)
                        last4 = lasts[k][:, :].rearrange("a (b j) -> a b j", j=B)
                        do(dve.tensor_scalar(t["keep"][:, :], t["first"][:, :], -1.0, 1.0, ALU.mult, ALU.add))
                        do(dve.tensor_scalar(t["row"][:, :], tiles[k][:, :], float(NT), None, ALU.mult))
                        do(dve.tensor_copy(t["last"][:, :], lasts[k][:, :]))
                        do(dve.tensor_tensor(f1[:, :], by4[:, :, B - 1], by4[:, :, 0], ALU.subtract))
                        do(dve.scalar_tensor_tensor(f1[:, :], f1[:, :], float(B - 1), last4[:, :, B - 1], ALU.is_equal, ALU.mult))
                        do(dve.tensor_copy(t["plain"][:, :], f1[:, :]))
                        keep4 = t["keep"][0:1, :].rearrange("a (b j) -> a b j", j=B)
                        do(dve.tensor_reduce(f1[:, :], keep4, AX.X, ALU.max))
                        do(dve.tensor_copy(t["carry"][:, :], f1[:, :]))
                        do(dve.tensor_copy(f2[:, 0:2], f1[:, 0:2]))
                        do(dve.tensor_tensor(f2[:, 2:], f1[:, 2:], f1[:, :MAXI // B - 2], ALU.max))
                        do(dve.tensor_copy(t["again"][:, :], f2[:, :]))

        with ExitStack() as inner:
            p = Mem(nc, inner, "rank")
            hot = {k: p.sb(f"hot_{k}", [EP, NRING, TILES], F16) for k in KEYS}
            rank = {k: p.ps(f"rank_{k}", [EP, TILES]) for k in KEYS}
            junk = {k: p.sb(f"junk_{k}", [EP, TILES], F16 if k == "dst" else F32) for k in KEYS}
            got = {k: p.sb(f"got_{k}", [EP, 2, NRING]) for k in KEYS}
            hot_ready = p.sem("one_hots_ready")
            added = {k: p.sem(f"earlier_added_{k}") for k in KEYS}
            picked = {k: p.sem(f"position_picked_{k}") for k in KEYS}
            moved = {k: p.sem(f"positions_moved_{k}") for k in KEYS}
            counted = p.sem("chunk_counted")
            with nc.Block() as block:

                @block.vector
                def _(dve):
                    def body(s, q, on):
                        if on(0):
                            wait(dve, counted, 2 * (s - NRING + 1))
                            for k in KEYS:
                                last = dve.tensor_scalar(hot[k][:, q], iota_h[0:EP, 0:TILES], tile[k][:, bass.ds(s, 1)],
                                                         None, ALU.is_equal)
                            last.then_inc(hot_ready, 1)
                        if on(2):
                            t, r = s - 2, (q - 2) % NRING
                            dve.wait_ge(added["dst"], t + 1)
                            dve.tensor_tensor_reduce(out=junk["dst"][:, :], in0=rank["dst"][:, :], in1=hot["dst"][:, r],
                                                     scale=1.0, scalar=0.0, op0=ALU.mult, op1=ALU.add,
                                                     accum_out=got["dst"][:, 0, r:r + 1]).then_inc(picked["dst"], 1)
                            if r == NRING - 1:
                                dve.wait_ge(picked["dst"], t + 1)
                                dve.tensor_copy(pos["dst"][:, bass.ds(t - (NRING - 1), NRING)], got["dst"][:, 0]).then_inc(moved["dst"], 1)
                                dve.wait_ge(moved["dst"], (t + 1) // NRING)
                    turns(dve, 0, CH, 2, body)

                @block.scalar
                def _(act):
                    def body(s, q, on):
                        if on(0):
                            act.wait_ge(added["src"], s + 1)
                            act.activation(junk["src"][:, :], rank["src"][:, :], ACT.Relu, bias=neg_big[0:EP, :],
                                           accum_out=got["src"][:, 0, q:q + 1]).then_inc(picked["src"], 1)
                            if q == NRING - 1:
                                act.wait_ge(picked["src"], s + 1)
                                act.activation(pos["src"][:, bass.ds(s - (NRING - 1), NRING)], got["src"][:, 0], ACT.Copy).then_inc(moved["src"], 1)
                                act.wait_ge(moved["src"], (s + 1) // NRING)
                    turns(act, 0, CH, 0, body)

                @block.tensor
                def _(pe):
                    for k in KEYS:
                        pe.matmul(rank[k][:, :], ones_row[:, :], base[k][0:1, :], start=True, stop=True)

                    def body(s, q, on):
                        if on(0):
                            pe.wait_ge(hot_ready, s + 1)
                        for k in KEYS:
                            if on(1):
                                r = (q - 1) % NRING
                                pe.wait_ge(picked[k], s)
                                last = pe.matmul(rank[k][:, :], not_earlier[:, :], hot[k][:, r], start=False, stop=True, skip_group_check=True)
                                if k == "src":
                                    last = pe.matmul(rank[k][:, :], neg_big_eye[:, :], hot[k][:, r], start=False, stop=True, skip_group_check=True)
                                last.then_inc(counted, 1)
                            if on(0):
                                last = pe.matmul(rank[k][:, :], earlier[:, :], hot[k][:, q], start=False, stop=True, skip_group_check=True)
                                if k == "src":
                                    last = pe.matmul(rank[k][:, :], big_eye[:, :], hot[k][:, q], start=False, stop=True, skip_group_check=True)
                                last.then_inc(added[k], 1)
                    turns(pe, 0, CH, 1, body)
                    pe.wait_ge(counted, 2 * CH)

        with ExitStack() as inner:
            p = Mem(nc, inner, "place")
            in_item = {k: p.sb(f"in_item_{k}", [EP, NRING, PLACE], F16) for k in KEYS}
            in_slot = {k: p.sb(f"in_slot_{k}", [EP, NRING, 2, W], F16) for k in KEYS}
            plane = {k: [p.ps(f"plane{n}_{k}", [W, PLACE]) for n in range(2)] for k in KEYS}
            v1 = p.sb("v1", [W, PLACE])
            v2 = p.sb("v2", [W, PLACE])
            v3 = p.sb("v3", [W, PLACE])
            v4 = p.sb("v4", [W, PLACE])
            step, hot_ready, placed = p.sem("vector_step"), p.sem("one_hots_ready"), p.sem("chunk_placed")
            filled, tstep = p.sem("empty_slots_set"), p.sem("table_step")
            with nc.Block() as block:

                @block.vector
                def _(dve):
                    c = Steps(dve, step, 10 ** 6)
                    c.begin(0)

                    def do(ins):
                        c.mark(ins)
                        c.sync()

                    for k in KEYS:
                        t = tab[k]
                        dve.memset(t["other"][:, MAIN:], 0)
                        dve.memset(t["local"][:, MAIN:], -1.0)
                        do(dve.tensor_scalar(item[k][:, :], pos[k][:, :], 1.0 / W, -0.496, ALU.mult, ALU.add))
                        do(dve.tensor_scalar(item[k][:, :], item[k][:, :], MAGIC, MAGIC, ALU.add, ALU.subtract))
                        do(dve.scalar_tensor_tensor(pos[k][:, :], item[k][:, :], -float(W), pos[k][:, :], ALU.mult, ALU.add))

                    def place(n, lo, width):
                        def body(s, q, on):
                            wait(dve, placed, n * CH + s - NRING + 1 if n else s - NRING + 1)
                            at = bass.ds(s, 1)
                            for k in KEYS:
                                for w, pay in enumerate((low[k], high[k])):
                                    dve.tensor_scalar(in_slot[k][:, q, w, :], iota_h[0:EP, 0:W], pos[k][:, at], pay[:, at],
                                                      ALU.is_equal, ALU.mult)
                                last = dve.tensor_scalar(in_item[k][:, q, 0:width], iota_h[0:EP, lo:lo + width], item[k][:, at],
                                                         None, ALU.is_equal)
                            last.then_inc(hot_ready, 1)
                        turns(dve, 0, CH, 0, body)
                        dve.wait_ge(placed, (n + 1) * CH)
                        for i, k in enumerate(KEYS):
                            t = tab[k]
                            o = t["other"][:, lo:lo + width]
                            l = t["local"][:, lo:lo + width]
                            a, b, used, hi = v1[:, 0:width], v2[:, 0:width], v3[:, 0:width], v4[:, 0:width]
                            do(dve.tensor_copy(a, plane[k][0][:, 0:width]))
                            do(dve.tensor_copy(b, plane[k][1][:, 0:width]))
                            do(dve.tensor_scalar(used, a, 0.0, None, ALU.is_gt))
                            do(dve.tensor_scalar(b, b, NT / 2.0 * HI, None, ALU.add))
                            do(dve.tensor_scalar(hi, b, 1.0 / HI, -0.48, ALU.mult, ALU.add))
                            do(dve.tensor_scalar(hi, hi, MAGIC, MAGIC, ALU.add, ALU.subtract))
                            do(dve.scalar_tensor_tensor(b, hi, -float(HI), b, ALU.mult, ALU.add))
                            do(dve.tensor_scalar(hi, hi, 1.0, None, ALU.add))
                            do(dve.tensor_tensor(hi, hi, used, ALU.mult))
                            do(dve.tensor_scalar(l, hi, 1.0, None, ALU.subtract))
                            do(dve.scalar_tensor_tensor(b, b, float(SPLIT), a, ALU.mult, ALU.add))
                            do(dve.tensor_scalar(b, b, 1.0, 0.0, ALU.subtract, ALU.max))
                            do(dve.tensor_copy(o, b))
                        dve.sem_inc(filled, 1)

                    dve.drain()
                    place(0, 0, PLACE)
                    total = {k: dve.value_load(tab[k]["total"][0:1, 0:1], min_val=0, max_val=MAXI) for k in KEYS}
                    with dve.If((total["dst"] > PLACE) | (total["src"] > PLACE)):
                        place(1, PLACE, MAXI - PLACE)
                    with dve.Else():
                        pass

                @block.tensor
                def _(pe):
                    def place(n, width):
                        def chunk(s, q, start, stop):
                            pe.wait_ge(hot_ready, n * CH + s + 1)
                            for k in KEYS:
                                for w in range(2):
                                    last = pe.matmul(plane[k][w][:, 0:width], in_slot[k][:, q, w, :], in_item[k][:, q, 0:width],
                                                     start=start, stop=stop)
                            last.then_inc(placed, 1)
                        turns(pe, 0, CH, 0, lambda s, q, on: chunk(s, q, isinstance(s, int) and s == 0,
                                                                     isinstance(s, int) and s == CH - 1))
                    place(0, PLACE)
                    total = {k: pe.value_load(tab[k]["total"][0:1, 0:1], min_val=0, max_val=MAXI) for k in KEYS}
                    with pe.If((total["dst"] > PLACE) | (total["src"] > PLACE)):
                        pe.wait_ge(filled, 1)
                        place(1, MAXI - PLACE)
                    with pe.Else():
                        pass
    return tab



def own_rows(sp, tab, t, q, pairs, sems, part, store):
    sem = sems[q]
    plain = sp.value_load(tab["plain"][0:1, bass.ds(t, 1)], min_val=0, max_val=1)
    with sp.If(plain > 0):
        row = sp.value_load(tab["row"][0:1, bass.ds(t * B, 1)], min_val=0, max_val=N - B * NT)
        for dram, buf in pairs:
            rows = dram[bass.ds(row, B * NT), :].rearrange("(j n) f -> n j f", n=NT)
            src, dst = (buf, rows) if store else (rows, buf)
            sp.dma_start(dst, src).then_inc(sem, 16)
    with sp.Else():
        wait(sp, sem, 16 * len(pairs) * (lap(t) - 1))
        for j in range(B):
            last = sp.value_load(tab["last"][0:1, bass.ds(t * B + j, 1)], min_val=0, max_val=1) if store else 1
            row = sp.value_load(tab["row"][0:1, bass.ds(t * B + j, 1)], min_val=0, max_val=N - NT)

            def move():
                for dram, buf in pairs:
                    src, dst = dram[bass.ds(row, NT), :], buf[:, j, :]
                    src, dst = (dst, src) if store else (src, dst)
                    sp.dma_start(dst, src).then_inc(part, 16)
            if store:
                with sp.If(last > 0):
                    move()
                with sp.Else():
                    sp.sem_inc(part, 16 * len(pairs))
            else:
                move()
        sp.wait_ge(part, 16 * B * len(pairs))
        sp.sem_clear(part)
        sp.sem_inc(sem, 16 * len(pairs))


def all_stored(sp, stored, each, batches):
    for q in range(NRING):
        sp.wait_ge(stored[q], each * len(range(q, batches, NRING)))


def gather_rows(pool, tab, t, q, table, idx, rows, width, idx_ready, gathered, free, free_at, ready):
    par = q % 2
    wait(pool, gathered[(q - 2) % NRING], 16 * B * lap(t - 2))
    pool.tensor_copy(idx[:, par, :], tab["other"][:, bass.ds(t * B, B)]).then_inc(idx_ready, 1)
    wait(pool, free, free_at)
    pool.wait_ge(idx_ready, t + 1)
    pool.sem_inc(ready, 1)
    for j in range(B):
        pool.indirect_dma_start(rows[:, q, j, 0:width], None, table,
                                bass.IndirectOffsetOnAxis(idx[:, par, j:j + 1], 0)).then_inc(gathered[q], 16)


def one_hot(dve, const, tab, t, out):
    return dve.tensor_tensor(out, const["iota"][:, :].unsqueeze(1).broadcast_to([W, B, NT]),
                             tab["local"][:, bass.ds(t * B, B)].unsqueeze(2).broadcast_to([W, B, NT]), ALU.is_equal)


def if_set(eng, flags, t, then):
    flag = eng.value_load(flags[0:1, bass.ds(t, 1)], min_val=0, max_val=1)
    with eng.If(flag > 0):
        then()
    with eng.Else():
        pass


def mark_firsts(dve, const, tab, t, out, used, used_at):
    def build():
        wait(dve, used, used_at)
        dve.tensor_tensor(out, const["eye"][0:NT, 0:NT].unsqueeze(1).broadcast_to([NT, B, NT]),
                          tab["first"][0:NT, bass.ds(t * B, B)].unsqueeze(2).broadcast_to([NT, B, NT]), ALU.mult)
        dve.drain()
    if_set(dve, tab["again"], t, build)


def pass_on(dve, tab, t, acc, q, keep):
    def add():
        dve.tensor_copy(keep, tab["keep"][:keep.shape[0], bass.ds(t * B, B)])
        dve.drain()
        for j in range(B):
            before = acc[:, q, j - 1] if j else acc[:, (q - 1) % NRING, B - 1]
            dve.scalar_tensor_tensor(acc[:, q, j], before, keep[:, j:j + 1], acc[:, q, j], ALU.mult, ALU.add)
            dve.drain()
    if_set(dve, tab["carry"], t, add)


def norm_stats(dve, settled, c, u, stats, mv):
    for j in range(B):
        last = dve.bn_stats(stats[:, j, :], u[:, j, :])
    c.mark(last)
    waits_apart(dve, settled, [(c.sem, c.base + c.n)])
    for j in range(B):
        last = dve.bn_aggr(mv[:, j, :], stats[:, j, :])
    return last


def rstd(act, var, logs, out, eps, log_step, t):
    act.activation(logs, var, ACT.Ln, bias=eps).then_inc(log_step, 1)
    act.wait_ge(log_step, t + 1)
    return act.activation(out, logs, ACT.Exp, scale=-0.5)


def normalise(dve, c, u, mv, rs, shift, out):
    c.mark(dve.scalar_tensor_tensor(shift, mv[:, :, 0], -1.0, rs, ALU.mult, ALU.mult))
    c.sync()
    for j in range(B):
        last = dve.tensor_scalar(out[:, j, :], u[:, j, :], rs[:, j:j + 1], shift[:, j:j + 1], ALU.mult, ALU.add)
    return last


def col(v):
    return v.rearrange("(p a) -> p a", a=1)


def row(v):
    return v.rearrange("(a p) -> a p", a=1)



def load_weights(nc, keep, ins, const):
    w = {n: keep.sb(n, [D, D]) for n in ("L0_gnn_W1", "L0_gnn_W4", "L1_gnn_W1", "L1_gnn_W2", "L3_gnn_Wo")}
    w["W2"] = keep.sb("W2", [D, 1])
    w["b1"] = keep.sb("b1", [D, 1])
    w["neg_b2"] = keep.sb("neg_b2", [W, 1])
    w["gat"] = keep.sb("gat", [D, D + 2 * HEADS])
    w["qv"] = keep.sb("qv", [D, 2 * D])
    rows = ("L1_gnn_b1", "L1_gnn_b2", "L2_gnn_bias", "L3_gnn_bo", "L3_gnn_gamma", "L3_gnn_beta")
    for n in rows:
        w["row_" + n] = keep.sb("row_" + n, [128, D])
    parts = ("L0_gnn_b4", "L3_gnn_bqk", "L3_gnn_bv")
    w["parts"] = keep.sb("parts", [3, len(parts) * D], BF16)
    w["ones3"] = keep.sb("ones3", [3, NT], BF16)
    w["eps"] = keep.sb("eps", [128, 1])
    with ExitStack() as ctx:
        p = Mem(nc, ctx, "load")
        att = p.sb("att", [128, HEADS, 2 * HC])
        prod = p.sb("prod", [D, 2, D])
        full = p.sb("full", [1, len(parts) * D])
        left = p.sb("left", [1, len(parts) * D])
        piece = p.sb("piece", [1, 3, len(parts) * D], BF16)
        loaded, step, split, spread = p.sem("loaded"), p.sem("vector_step"), p.sem("split"), p.sem("spread")
        with nc.Block() as block:

            @block.sync
            def _(sp):
                loads = [(w[n][:, :], ins[n]) for n in ("L0_gnn_W1", "L0_gnn_W4", "L1_gnn_W1", "L1_gnn_W2", "L3_gnn_Wo")]
                loads += [(w["W2"][:, :], ins["L0_gnn_W2"]), (w["b1"][:, :], col(ins["L0_gnn_b1"])),
                          (w["neg_b2"][:, :], row(ins["L0_gnn_b2"]).broadcast_to([W, 1])),
                          (w["gat"][:, 0:D], ins["L2_gnn_weight"]), (w["qv"][:, 0:D], ins["L3_gnn_Wqk"]),
                          (w["qv"][:, D:], ins["L3_gnn_Wv"]),
                          (att[:, :, :], ins["L2_gnn_att"].broadcast_to([128, HEADS, 2 * HC]))]
                loads += [(w["row_" + n][:, :], row(ins[n]).broadcast_to([128, D])) for n in rows]
                loads += [(full[:, i * D:(i + 1) * D], row(ins[n])) for i, n in enumerate(parts)]
                for dst, src in loads:
                    sp.dma_start(dst, src).then_inc(loaded, 16)
                sp.wait_ge(split, 1)
                for i in range(3):
                    sp.dma_start(w["parts"][i:i + 1, :], piece[:, i, :]).then_inc(spread, 16)
                sp.wait_ge(spread, 48)
                sp.wait_ge(loaded, 16 * len(loads))

            @block.vector
            def _(dve):
                c = Steps(dve, step, 10 ** 6)
                c.begin(0)

                def do(ins_):
                    c.mark(ins_)
                    c.sync()
                dve.memset(w["ones3"][:, :], 1.0)
                dve.memset(w["eps"][:, :], EPS)
                dve.wait_ge(loaded, 16 * 21)
                do(dve.tensor_scalar(w["neg_b2"][:, :], w["neg_b2"][:, :], -1.0, None, ALU.mult))
                wt = w["gat"][:, 0:D].rearrange("p (h c) -> p h c", h=HEADS)
                for i, half in enumerate((slice(HC, 2 * HC), slice(0, HC))):
                    pr = prod[:, i, :].rearrange("p (h c) -> p h c", h=HEADS)
                    do(dve.tensor_tensor(pr, wt, att[:, :, half], ALU.mult))
                    do(dve.tensor_reduce(w["gat"][:, D + i * HEADS:D + (i + 1) * HEADS], pr, AX.X, ALU.add))
                do(dve.tensor_copy(piece[:, 0, :], full[:, :]))
                do(dve.tensor_tensor(left[:, :], full[:, :], piece[:, 0, :], ALU.subtract))
                do(dve.tensor_copy(piece[:, 1, :], left[:, :]))
                do(dve.tensor_tensor(left[:, :], left[:, :], piece[:, 1, :], ALU.subtract))
                dve.tensor_copy(piece[:, 2, :], left[:, :]).then_inc(split, 1)
    return w



def gated_layer(nc, tab, const, w, dis, x, x1, y1):
    with ExitStack() as ctx:
        m = Mem(nc, ctx, "l0")
        idx = m.sb("idx", [W, 2, B], I32)
        G = m.sb("gathered", [W, NRING, B, D + 1])
        X = m.sb("own", [NT, NRING, B, D])
        S = m.sb("one_hot", [W, NRING, B, NT])
        ST = m.sb("one_hot_T", [NT, 2, B, W])
        XT = m.sb("own_T", [D, NRING, B, NT])
        TH = m.sb("theta_T", [D, 2, B * W])
        R = m.sb("hidden_T", [D, 2, B * W])
        EX = m.sb("exp_logit", [W, 2, B])
        WE = m.sb("edge_weight", [W, 2, B])
        SW = m.sb("weighted_one_hot", [W, 2, B, NT])
        A = m.sb("sums", [NT, NRING, B, D + 2])
        W1 = m.sb("weight_sum_plus_1", [NT, B])
        V = m.sb("partial", [NT, B, D])
        U = m.sb("summed", [NT, 2, B, D])
        stats = m.sb("stats", [NT, B, 6])
        mv = m.sb("mean_var", [NT, 2, 2, B, 2])
        lg = m.sb("logs", [NT, 2, B])
        rs = m.sb("rstd", [NT, 2, 2, B])
        shift = m.sb("shift", [NT, B])
        keep4 = m.sb("keep4", [NT, B])
        X1 = m.sb("x1", [NT, 2, B, D])
        Y1 = m.sb("y1", [NT, 2, B, D])
        pST = m.ps("one_hot_T", [NT, B, W])
        pX = m.ps("own_T", [D, B, NT])
        pTH = m.ps("theta_T", [D, B, W])
        pH = m.ps("hidden_T", [D, B * W])
        pZ = m.ps("logit", [W, B])
        pA = m.ps("sums", [NT, B, 256])
        pW = m.ps("x_W4", [NT, B, D])
        ready, passed, sp_passed = m.sem("constants_set"), m.sem("waits_passed"), m.sem("sync_waits_passed")
        own, idx_ready, gathered = m.sems("own_loaded"), m.sem("indices_ready"), m.sems("gathered")
        s_ready, st_made, st_ready = m.sem("one_hot_ready"), m.sem("one_hot_T_made"), m.sem("one_hot_T_ready")
        xt_made, xt_ready = m.sem("own_T_made"), m.sem("own_T_ready")
        th_made, th_ready = m.sem("theta_made"), m.sem("theta_ready")
        h_made, h_ready = m.sem("hidden_made"), m.sem("hidden_ready")
        z_made, e_ready, w_step, sw_ready = m.sem("logit_made"), m.sem("exp_ready"), m.sem("weight_step"), m.sem("weighted_ready")
        a_made, a_ready, w4_made, u_step, u_ready = (m.sem("sums_made"), m.sem("sums_ready"), m.sem("x_W4_made"),
                                                     m.sem("epilogue_step"), m.sem("summed_ready"))
        log_step, rs_ready, n_step, x1_ready, y1_ready = (m.sem("log_step"), m.sem("rstd_ready"), m.sem("normalise_step"),
                                                          m.sem("x1_ready"), m.sem("y1_ready"))
        stored, part, stat_step = m.sems("stored"), m.sem("tiles_moved"), m.sem("stat_step")
        with nc.Block() as block:

            @block.sync
            def _(sp):
                def body(s, q, on):
                    if on(0):
                        waits_apart(sp, sp_passed, [(u_ready, s - 3)])
                        own_rows(sp, tab, s, q, [(x, X[:, q])], own, part, False)
                    if on(4):
                        t, r = s - 4, q % 2
                        waits_apart(sp, sp_passed, [(x1_ready, t + 1), (y1_ready, t + 1)])
                        own_rows(sp, tab, t, q, [(x1, X1[:, r]), (y1, Y1[:, r])], stored, part, True)

                def run(first, last):
                    turns(sp, first, last, 4, body)
                    all_stored(sp, stored, 32, last)
                both_ranges(sp, tab["total"][0:1, 0:1], run)

            @block.gpsimd
            def _(pool):
                def body(s, q, on):
                    gather_rows(pool, tab, s, q, x, idx, G, D, idx_ready, gathered, a_made, s - 3, passed)
                both_ranges(pool, tab["total"][0:1, 0:1], lambda a, b: turns(pool, a, b, 0, body))

            @block.vector
            def _(dve):
                wstep, ustep, nstep = Steps(dve, w_step, 2), Steps(dve, u_step, 3), Steps(dve, n_step, 1)
                dve.memset(mv[:, :, :, :, :], 1.0)
                dve.memset(A[:, NRING - 1, B - 1, :], 0.0)
                dve.memset(G[:, :, :, D:D + 1], 1.0).then_inc(ready, 1)
                dve.wait_ge(ready, 1)

                def body(s, q, on):
                    if on(0):
                        wait(dve, a_made, s - 3)
                        one_hot(dve, const, tab, s, S[:, q]).then_inc(s_ready, 1)
                    if on(3):
                        t, r = s - 3, (q - 3) % 2
                        dve.wait_ge(rs_ready, t + 1)
                        wait(dve, stored[(q - 5) % NRING], 32 * lap(t - 2))
                        wait(dve, x1_ready, t)
                        nstep.begin(t)
                        dve.tensor_copy(dis[:, bass.ds(t * B, B)], rs[:, r, 1])
                        normalise(dve, nstep, U[:, r], mv[:, r, 0], rs[:, r, 0], shift[:, :], X1[:, r]).then_inc(x1_ready, 1)
                        nstep.end()
                    if on(1):
                        t, r, rq = s - 1, (q - 1) % 2, (q - 1) % NRING
                        dve.wait_ge(e_ready, t + 1)
                        wait(dve, a_made, t - 1)
                        wstep.begin(t)
                        wstep.mark(dve.tensor_scalar(EX[:, r], EX[:, r], 1.0, None, ALU.add))
                        wstep.sync()
                        wstep.mark(dve.reciprocal(WE[:, r], EX[:, r]))
                        wstep.sync()
                        wstep.end()
                        dve.tensor_tensor(SW[:, r], S[:, rq], WE[:, r].unsqueeze(2).broadcast_to([W, B, NT]),
                                          ALU.mult).then_inc(sw_ready, 1)
                    if on(2):
                        t, r, rq = s - 2, (q - 2) % 2, (q - 2) % NRING
                        dve.wait_ge(a_ready, t + 1)
                        wait(dve, x1_ready, t - 1)
                        wait(dve, u_ready, t)
                        pass_on(dve, tab, t, A, rq, keep4[:, :])
                        ustep.begin(t)
                        dve.tensor_scalar(mv[:, r, 1, :, 1], A[:, rq, :, D + 1], 1.0, None, ALU.add)
                        ustep.mark(dve.tensor_scalar(W1[:, :], A[:, rq, :, D], 1.0, None, ALU.add))
                        ustep.sync()
                        for j in range(B):
                            last = dve.scalar_tensor_tensor(V[:, j, :], X[:, rq, j, :], W1[:, j:j + 1], A[:, rq, j, 0:D],
                                                            ALU.mult, ALU.subtract)
                        ustep.mark(last)
                        dve.wait_ge(w4_made, t + 1)
                        ustep.sync()
                        for j in range(B):
                            last = dve.scalar_tensor_tensor(U[:, r, j, :], pW[:, j, :], A[:, rq, j, D + 1:D + 2], V[:, j, :],
                                                            ALU.mult, ALU.add)
                        ustep.mark(last)
                        ustep.sync()
                        ustep.end()
                        sstep = Steps(dve, stat_step, 1)
                        sstep.begin(t)
                        norm_stats(dve, ready, sstep, U[:, r], stats, mv[:, r, 0]).then_inc(u_ready, 1)
                both_ranges(dve, tab["total"][0:1, 0:1], lambda a, b: turns(dve, a, b, 3, body))

            @block.scalar
            def _(act):
                def body(s, q, on):
                    if on(3):
                        t, r = s - 3, (q - 3) % 2
                        act.wait_ge(u_ready, t + 1)
                        wait(act, x1_ready, t - 1)
                        wait(act, y1_ready, t - 1)

                        wait(act, rs_ready, t)
                        act.activation(lg[:, 0], mv[:, r, 0, :, 1], ACT.Ln, bias=w["eps"][0:NT, :])
                        act.activation(lg[:, 1], mv[:, r, 1, :, 1], ACT.Ln).then_inc(log_step, 1)
                        act.wait_ge(log_step, t + 1)
                        act.activation(rs[:, r], lg[:, :, :], ACT.Exp, scale=-0.5).then_inc(rs_ready, 1)
                    if on(0):
                        act.wait_ge(st_made, s + 1)
                        wait(act, th_made, s - 1)
                        act.activation(ST[:, q % 2], pST[:, :, :], ACT.Copy).then_inc(st_ready, 1)
                        act.wait_ge(xt_made, s + 1)
                        wait(act, w4_made, s - 3)
                        act.activation(XT[:, q], pX[:, :, :], ACT.Copy).then_inc(xt_ready, 1)
                    if on(1):
                        t, r = s - 1, (q - 1) % 2
                        act.wait_ge(h_made, t + 1)
                        wait(act, z_made, t - 1)
                        act.activation(R[:, r], pH[:, :], ACT.Relu, bias=w["b1"][:, :]).then_inc(h_ready, 1)
                    if on(0):
                        act.wait_ge(th_made, s + 1)
                        wait(act, h_made, s - 1)
                        act.activation(TH[:, q % 2], pTH[:, :, :], ACT.Copy).then_inc(th_ready, 1)
                    if on(1):
                        t, r = s - 1, (q - 1) % 2
                        act.wait_ge(z_made, t + 1)
                        wait(act, sw_ready, t - 1)
                        act.activation(EX[:, r], pZ[:, :], ACT.Exp, bias=w["neg_b2"][:, :], scale=-1.0).then_inc(e_ready, 1)
                    if on(2):
                        t, rq = s - 2, (q - 2) % NRING
                        act.wait_ge(a_made, t + 1)
                        wait(act, u_ready, t - 2)
                        act.activation(A[:, rq], pA[:, :, 0:D + 2], ACT.Copy).then_inc(a_ready, 1)
                    if on(3):
                        t, r = s - 3, (q - 3) % 2
                        act.wait_ge(x1_ready, t + 1)
                        wait(act, stored[(q - 5) % NRING], 32 * lap(t - 2))
                        for j in range(B):
                            last = act.activation(Y1[:, r, j, :], X1[:, r, j, :], ACT.Copy, scale=rs[:, r, 1, j:j + 1])
                        last.then_inc(y1_ready, 1)
                both_ranges(act, tab["total"][0:1, 0:1], lambda a, b: turns(act, a, b, 3, body))

            @block.tensor
            def _(pe):
                eye, neg_eye = const["eye"], const["neg_eye"]
                b4 = w["parts"][:, 0:D].unsqueeze(1).broadcast_to([3, B, D])

                def body(s, q, on):
                    if on(0):
                        pe.wait_ge(s_ready, s + 1)
                        wait(pe, st_ready, s)
                        for j in range(B):
                            last = pe.transpose(pST[:, j, :], S[:, q, j, :], eye[:, :])
                        last.then_inc(st_made, 1)
                        pe.wait_ge(own[q], 16 * lap(s))
                        wait(pe, xt_ready, s)
                        for j in range(B):
                            last = pe.transpose(pX[:, j, :], X[:, q, j, :], eye[0:NT, 0:NT])
                        last.then_inc(xt_made, 1)
                    if on(1):
                        t, r = s - 1, (q - 1) % 2
                        pe.wait_ge(th_ready, t + 1)
                        wait(pe, h_ready, t)
                        pe.matmul(pH[:, :], w["L0_gnn_W1"][:, :], TH[:, r], start=True, stop=True).then_inc(h_made, 1)
                    if on(0):
                        pe.wait_ge(st_ready, s + 1)
                        pe.wait_ge(gathered[q], 16 * B * lap(s))
                        wait(pe, th_ready, s)
                        for j in range(B):
                            pe.matmul(pTH[:, j, :], X[:, q, j, :], ST[:, q % 2, j, :], start=True, stop=False)
                            last = pe.matmul(pTH[:, j, :], G[:, q, j, 0:D], neg_eye[:, :], start=False, stop=True)
                        last.then_inc(th_made, 1)
                    if on(1):
                        t, r = s - 1, (q - 1) % 2
                        pe.wait_ge(h_ready, t + 1)
                        wait(pe, e_ready, t)
                        for j in range(B):
                            last = pe.matmul(pZ[:, j:j + 1], R[:, r, j * W:(j + 1) * W], w["W2"][:, :], start=True, stop=True)
                        last.then_inc(z_made, 1)
                    if on(2):
                        t, r, rq = s - 2, (q - 2) % 2, (q - 2) % NRING
                        pe.wait_ge(xt_ready, t + 1)
                        wait(pe, u_ready, t)
                        pe.matmul(pW[:, :, :], w["ones3"][:, :], b4, start=True, stop=False)
                        for j in range(B):
                            last = pe.matmul(pW[:, j, :], XT[:, rq, j, :], w["L0_gnn_W4"][:, :], start=False, stop=(j == B - 1))
                        last.then_inc(w4_made, 1)
                        pe.wait_ge(sw_ready, t + 1)
                        wait(pe, a_ready, t)
                        for j in range(B):
                            pe.matmul(pA[:, j, 0:D + 1], SW[:, r, j, :], G[:, rq, j, :], start=True, stop=True)
                            last = pe.matmul(pA[:, j, D + 1:D + 2], S[:, rq, j, :], G[:, rq, j, D:D + 1], start=True, stop=True)
                        last.then_inc(a_made, 1)
                both_ranges(pe, tab["total"][0:1, 0:1], lambda a, b: turns(pe, a, b, 2, body))



def convolution(nc, tab, const, w, dis, tag, weight, bias, y_in, y_out=None, x_in=None, x_out=None, gat=None):
    second = x_in is not None
    HW = D + 2 * HEADS
    with ExitStack() as ctx:
        m = Mem(nc, ctx, tag)
        idx = m.sb("idx", [W, 2, B], I32)
        G = m.sb("gathered", [W, NRING, B, D])
        Y = m.sb("own", [NT, NRING, B, D])
        S = m.sb("one_hot", [W, NRING, B, NT])
        F = m.sb("firsts", [NT, 2, B, NT])
        AT = m.sb("sums_T", [D, NRING, B, NT])
        dl = m.sb("dis", [NT, NRING, B])
        keep4 = m.sb("keep4", [D, B])
        T = m.sb("before_relu", [NT, 2, B, D])
        O = m.sb("out", [NT, 2, B, D])
        pT = m.ps("sums_T", [D, B, NT])
        pZ = m.ps("product", [NT, B, D])
        ready, passed, sp_passed = m.sem("constants_set"), m.sem("waits_passed"), m.sem("sync_waits_passed")
        own, idx_ready, gathered = m.sems("own_loaded"), m.sem("indices_ready"), m.sems("gathered")
        s_ready, t_made, t_copied, t_ready = (m.sem("one_hot_ready"), m.sem("sums_made"), m.sem("sums_copied"),
                                              m.sem("sums_ready"))
        z_made, b_ready, o_ready = m.sem("product_made"), m.sem("biased_ready"), m.sem("out_ready")
        stored, part = m.sems("stored"), m.sem("tiles_moved")
        if second:
            X = m.sb("own_x", [NT, NRING, B, D])
            U = m.sb("summed", [NT, 2, B, D])
            stats = m.sb("stats", [NT, B, 6])
            mv = m.sb("mean_var", [NT, 2, B, 2])
            lg = m.sb("logs", [NT, B])
            rs = m.sb("rstd", [NT, 2, B])
            shift = m.sb("shift", [NT, B])
            OT = m.sb("out_T", [D, 2, B, NT])
            H = m.sb("gat_rows", [NT, 2, B, HW])
            pOT = m.ps("out_T", [D, B, NT])
            pH = m.ps("gat_rows", [NT, B, 256])
            own_x = m.sems("own_x_loaded")
            u_step, u_ready, log_step, rs_ready, n_step = (m.sem("summed_step"), m.sem("summed_ready"), m.sem("log_step"),
                                                           m.sem("rstd_ready"), m.sem("normalise_step"))
            ot_made, ot_ready, h_made, h_ready = (m.sem("out_T_made"), m.sem("out_T_ready"), m.sem("gat_made"),
                                                  m.sem("gat_ready"))
        with nc.Block() as block:

            @block.sync
            def _(sp):
                def body(s, q, on):
                    if on(0):
                        waits_apart(sp, sp_passed, [(t_made, s - 3)])
                        own_rows(sp, tab, s, q, [(y_in, Y[:, q])], own, part, False)
                        if second:
                            waits_apart(sp, sp_passed, [(u_ready, s - 3)])
                            own_rows(sp, tab, s, q, [(x_in, X[:, q])], own_x, part, False)
                    if second and on(4):
                        t, r = s - 4, q % 2
                        waits_apart(sp, sp_passed, [(o_ready, t + 1), (h_ready, t + 1)])
                        own_rows(sp, tab, t, q, [(x_out, O[:, r]), (gat, H[:, r])], stored, part, True)
                    if not second and on(2):
                        t, r, tq = s - 2, q % 2, (q - 2) % NRING
                        waits_apart(sp, sp_passed, [(o_ready, t + 1)])
                        own_rows(sp, tab, t, tq, [(y_out, O[:, r])], stored, part, True)

                def run(first, last):
                    turns(sp, first, last, 4 if second else 2, body)
                    all_stored(sp, stored, 32 if second else 16, last)
                both_ranges(sp, tab["total"][0:1, 0:1], run)

            @block.gpsimd
            def _(pool):
                def body(s, q, on):
                    gather_rows(pool, tab, s, q, y_in, idx, G, D, idx_ready, gathered, t_made, s - 3, passed)
                both_ranges(pool, tab["total"][0:1, 0:1], lambda a, b: turns(pool, a, b, 0, body))

            @block.vector
            def _(dve):
                dve.memset(AT[:, NRING - 1, B - 1, :], 0.0)
                dve.tensor_copy(F[:, 0], const["eye"][0:NT, 0:NT].unsqueeze(1).broadcast_to([NT, B, NT]))
                dve.tensor_copy(F[:, 1], const["eye"][0:NT, 0:NT].unsqueeze(1).broadcast_to([NT, B, NT])).then_inc(ready, 1)
                dve.wait_ge(ready, 1)

                def body(s, q, on):
                    if on(0):
                        mark_firsts(dve, const, tab, s, F[:, q % 2], t_made, s - 1)
                        wait(dve, t_made, s - 3)
                        one_hot(dve, const, tab, s, S[:, q]).then_inc(s_ready, 1)
                    if second and on(2):
                        t, r, tq = s - 2, q % 2, (q - 2) % NRING
                        dve.wait_ge(rs_ready, t + 1)
                        wait(dve, stored[tq - 2], 32 * lap(t - 2))
                        wait(dve, ot_made, t - 1)
                        wait(dve, o_ready, t)
                        nstep = Steps(dve, n_step, 1)
                        nstep.begin(t)
                        normalise(dve, nstep, U[:, r], mv[:, r], rs[:, r], shift[:, :], O[:, r]).then_inc(o_ready, 1)
                    if on(0):
                        dve.wait_ge(t_copied, s + 1)
                        dve.tensor_copy(dl[:, q], dis[:, bass.ds(s * B, B)])
                        pass_on(dve, tab, s, AT, q, keep4[:, :])
                        dve.sem_inc(t_ready, 1)
                    if on(1):
                        t, r, tq = s - 1, (q - 1) % 2, (q - 1) % NRING
                        dve.wait_ge(z_made, t + 1)
                        wait(dve, u_ready if second else o_ready, t - 1)
                        for j in range(B):
                            last = dve.scalar_tensor_tensor(T[:, r, j, :], pZ[:, j, :], dl[:, tq, j:j + 1],
                                                            w["row_" + bias][0:NT, :], ALU.mult, ALU.add)
                        last.then_inc(b_ready, 1)
                        if second:
                            ustep = Steps(dve, u_step, 2)
                            ustep.begin(t)
                            dve.wait_ge(b_ready, t + 1)
                            dve.wait_ge(own_x[tq], 16 * lap(t))
                            wait(dve, o_ready, t - 1)
                            wait(dve, u_ready, t)
                            ustep.mark(dve.scalar_tensor_tensor(U[:, r], T[:, r], 0.0, X[:, tq], ALU.max, ALU.add))
                            ustep.sync()
                            norm_stats(dve, ready, ustep, U[:, r], stats, mv[:, r]).then_inc(u_ready, 1)
                            ustep.end()
                both_ranges(dve, tab["total"][0:1, 0:1], lambda a, b: turns(dve, a, b, 2 if second else 1, body))

            @block.scalar
            def _(act):
                def body(s, q, on):
                    if second and on(2):
                        t, r = s - 2, q % 2
                        act.wait_ge(u_ready, t + 1)
                        wait(act, o_ready, t - 1)
                        wait(act, rs_ready, t)
                        rstd(act, mv[:, r, :, 1], lg[:, :], rs[:, r], w["eps"][0:NT, :], log_step, t).then_inc(rs_ready, 1)
                    if on(0):
                        act.wait_ge(t_made, s + 1)
                        wait(act, z_made, s - 3)
                        wait(act, t_ready, s - 2)
                        act.activation(AT[:, q], pT[:, :, :], ACT.Copy).then_inc(t_copied, 1)
                    if not second and on(1):
                        t, r, tq = s - 1, (q - 1) % 2, (q - 1) % NRING
                        act.wait_ge(b_ready, t + 1)
                        wait(act, stored[tq - 2], 16 * lap(t - 2))
                        for j in range(B):
                            last = act.activation(O[:, r, j, :], T[:, r, j, :], ACT.Relu, scale=dl[:, tq, j:j + 1])
                        last.then_inc(o_ready, 1)
                    if second and on(3):
                        t, r, tq = s - 3, (q - 3) % 2, (q - 3) % NRING
                        act.wait_ge(ot_made, t + 1)
                        wait(act, h_made, t - 1)
                        act.activation(OT[:, r], pOT[:, :, :], ACT.Copy).then_inc(ot_ready, 1)
                        act.wait_ge(h_made, t + 1)
                        wait(act, stored[tq - 2], 32 * lap(t - 2))
                        act.activation(H[:, r], pH[:, :, 0:HW], ACT.Copy).then_inc(h_ready, 1)
                both_ranges(act, tab["total"][0:1, 0:1], lambda a, b: turns(act, a, b, 3 if second else 1, body))

            @block.tensor
            def _(pe):
                def body(s, q, on):
                    if second and on(3):
                        t, r = s - 3, (q - 3) % 2
                        pe.wait_ge(o_ready, t + 1)
                        wait(pe, ot_ready, t)
                        for j in range(B):
                            last = pe.transpose(pOT[:, j, :], O[:, r, j, :], const["eye"][0:NT, 0:NT])
                        last.then_inc(ot_made, 1)
                    if on(0):
                        pe.wait_ge(s_ready, s + 1)
                        pe.wait_ge(own[q], 16 * lap(s))
                        pe.wait_ge(gathered[q], 16 * B * lap(s))
                        wait(pe, t_copied, s)
                        for j in range(B):
                            pe.matmul(pT[:, j, :], G[:, q, j, :], S[:, q, j, :], start=True, stop=False)
                            last = pe.matmul(pT[:, j, :], Y[:, q, j, :], F[:, q % 2, j, :], start=False, stop=True)
                        last.then_inc(t_made, 1)
                    if second and on(3):
                        t, r = s - 3, (q - 3) % 2
                        pe.wait_ge(ot_ready, t + 1)
                        wait(pe, h_ready, t)
                        for j in range(B):
                            last = pe.matmul(pH[:, j, 0:HW], OT[:, r, j, :], w["gat"][:, :], start=True, stop=True)
                        last.then_inc(h_made, 1)
                    if on(1):
                        t, tq = s - 1, (q - 1) % NRING
                        pe.wait_ge(t_ready, t + 1)
                        wait(pe, b_ready, t)
                        for j in range(B):
                            last = pe.matmul(pZ[:, j, :], AT[:, tq, j, :], w[weight][:, :], start=True, stop=True)
                        last.then_inc(z_made, 1)
                both_ranges(pe, tab["total"][0:1, 0:1], lambda a, b: turns(pe, a, b, 3 if second else 1, body))



def leaky(dve, out, in_):
    return dve.scalar_tensor_tensor(out, in_, 0.2, in_, ALU.mult, ALU.max)


def by_head(rows):
    return rows.rearrange("p j (h c) -> p j h c", h=HEADS)


def per_channel(heads, parts):
    return heads.unsqueeze(3).broadcast_to([parts, B, HEADS, HC])


def gat_layer(nc, tab, const, w, h_rows, x2, x3_out, qv_out):
    HW = D + 2 * HEADS
    RW = D + HEADS
    with ExitStack() as ctx:
        m = Mem(nc, ctx, "gat")
        idx = m.sb("idx", [W, 2, B], I32)
        G = m.sb("gathered", [W, NRING, B, HW])
        H = m.sb("own", [NT, NRING, B, HW])
        X = m.sb("own_x", [NT, NRING, B, D])
        S = m.sb("one_hot", [W, NRING, B, NT])
        F = m.sb("firsts", [NT, 2, B, NT])
        ST = m.sb("one_hot_T", [NT, NRING, B, W])
        dif = m.sb("ar_above_own", [W, B, HEADS])
        lin = m.sb("logit_linear", [W, B, HEADS])
        LG = m.sb("logit", [W, 2, B, HEADS])
        arg = m.sb("exp_argument", [W, B, HEADS])
        V = m.sb("values_by_node", [W, B, HEADS, NT])
        TOP = m.sb("top_above_own", [NT, NRING, B, HEADS])
        own_lin = m.sb("own_linear", [NT, B, HEADS])
        own_lg = m.sb("own_logit", [NT, B, HEADS])
        AM = m.sb("logit_max", [NT, NRING, B, HEADS])
        ES = m.sb("own_arguments", [NT, 2, 2, B, HEADS])
        EE = m.sb("own_exp", [NT, NRING, 2, B, HEADS])
        R = m.sb("weighted", [W, 2, B, RW])
        HS = m.sb("own_weighted", [NT, 2, B, RW])
        A = m.sb("sums", [NT, NRING, B, RW])
        tmp = m.sb("before_scaled", [NT, RW])
        den = m.sb("denominator", [NT, B, HEADS])
        T = m.sb("mean_by_head", [NT, B, D])
        TB = m.sb("with_bias", [NT, B, D])
        U = m.sb("summed", [NT, 2, B, D])
        stats = m.sb("stats", [NT, B, 6])
        mv = m.sb("mean_var", [NT, 2, B, 2])
        lg = m.sb("logs", [NT, B])
        rs = m.sb("rstd", [NT, 2, B])
        shift = m.sb("shift", [NT, B])
        keep4 = m.sb("keep4", [NT, B])
        keep4e = m.sb("keep4_late", [NT, B])
        X3 = m.sb("x3", [NT, NRING, B, D])
        XT = m.sb("x3_T", [D, 2, B, NT])
        QV = m.sb("qv", [NT, 2, B, 2 * D])
        pST = m.ps("one_hot_T", [NT, B, W])
        pL = m.ps("looked_up", [W, 2, 256])
        pV = [m.ps(f"values_T_{i}", [NT, HEADS, W]) for i in range(2)]
        pA = m.ps("sums", [NT, B, 256])
        pXT = m.ps("x3_T", [D, B, NT])
        pQV = m.ps("qv", [NT, 2, 2 * D])
        ready, passed, sp_passed = m.sem("constants_set"), m.sem("waits_passed"), m.sem("sync_waits_passed")
        own, own_x, idx_ready, gathered = (m.sems("own_loaded"), m.sems("own_x_loaded"), m.sem("indices_ready"),
                                           m.sems("gathered"))
        s_ready, st_made, st_ready, l1_made, l2_made = (m.sem("one_hot_ready"), m.sem("one_hot_T_made"),
                                                        m.sem("one_hot_T_ready"), m.sem("centre_looked_up"),
                                                        m.sem("max_looked_up"))
        v_step, v_ready, vt_made, vt_read = m.sem("logit_step"), m.sem("values_ready"), m.sem("values_T_made"), m.sem("values_T_read")
        m_step, am_ready, e_ready = m.sem("max_step"), m.sem("max_ready"), m.sem("own_exp_ready")
        a_step, a_ready, p_ready, r_ready = m.sem("argument_step"), m.sem("argument_ready"), m.sem("exp_ready"), m.sem("weighted_ready")
        pa_made, pa_ready, u_step, u_ready = m.sem("sums_made"), m.sem("sums_ready"), m.sem("summed_step"), m.sem("summed_ready")
        log_step, rs_ready, n_step, x3_ready = m.sem("log_step"), m.sem("rstd_ready"), m.sem("normalise_step"), m.sem("x3_ready")
        xt_made, xt_ready, qv_made, qv_ready = m.sem("x3_T_made"), m.sem("x3_T_ready"), m.sem("qv_made"), m.sem("qv_ready")
        stored, part = m.sems("stored"), m.sem("tiles_moved")
        with nc.Block() as block:

            @block.sync
            def _(sp):
                def body(s, q, on):
                    if on(0):
                        waits_apart(sp, sp_passed, [(r_ready, s - 3)])
                        own_rows(sp, tab, s, q, [(h_rows, H[:, q])], own, part, False)
                    if on(2):
                        t, tq = s - 2, (q - 2) % NRING
                        waits_apart(sp, sp_passed, [(u_ready, t - 3)])
                        own_rows(sp, tab, t, tq, [(x2, X[:, tq])], own_x, part, False)
                    if on(7):
                        t, tq = s - 7, (q - 7) % NRING
                        waits_apart(sp, sp_passed, [(qv_ready, 2 * t + 2)])
                        own_rows(sp, tab, t, tq, [(x3_out, X3[:, tq]), (qv_out, QV[:, tq % 2])], stored, part, True)

                def run(first, last):
                    turns(sp, first, last, 7, body)
                    all_stored(sp, stored, 32, last)
                both_ranges(sp, tab["total"][0:1, 0:1], run)

            @block.gpsimd
            def _(pool):
                def body(s, q, on):
                    gather_rows(pool, tab, s, q, h_rows, idx, G, HW, idx_ready, gathered, r_ready, s - 3, passed)
                both_ranges(pool, tab["total"][0:1, 0:1], lambda a, b: turns(pool, a, b, 0, body))

            @block.vector
            def _(dve):
                dve.memset(EE[:, :, :, :, :], 0.0)
                dve.memset(ES[:, :, :, :, :], 0.0)
                for ring in (TOP, AM, A):
                    dve.memset(ring[:, NRING - 1, B - 1, :], 0.0)
                dve.tensor_copy(F[:, 0], const["eye"][0:NT, 0:NT].unsqueeze(1).broadcast_to([NT, B, NT]))
                dve.tensor_copy(F[:, 1], const["eye"][0:NT, 0:NT].unsqueeze(1).broadcast_to([NT, B, NT])).then_inc(ready, 1)
                dve.wait_ge(ready, 1)

                def body(s, q, on):
                    if on(2):
                        t, r = s - 2, q % 2
                        st = Steps(dve, a_step, 1)
                        st.begin(t)
                        dve.wait_ge(l2_made, t + 1)
                        wait(dve, p_ready, t)
                        st.mark(dve.scalar_tensor_tensor(arg[:, :, :], pL[:, 1, 0:B * HEADS].rearrange("p (j h) -> p j h", j=B),
                                                         -1.0, LG[:, r], ALU.mult, ALU.add))
                        st.sync()
                        dve.tensor_scalar(arg[:, :, :], arg[:, :, :], 0.0, None, ALU.min).then_inc(a_ready, 1)
                    if on(1):
                        t, r, tq = s - 1, (q - 1) % 2, (q - 1) % NRING
                        st = Steps(dve, v_step, 1)
                        st.begin(t)
                        dve.wait_ge(l1_made, t + 1)
                        dve.wait_ge(gathered[tq], 16 * B * lap(t))
                        wait(dve, v_ready, t)
                        looked = pL[:, 0, 0:B * 2 * HEADS].rearrange("p (j h) -> p j h", j=B)
                        dve.tensor_tensor(dif[:, :, :], G[:, tq, :, D:RW], looked[:, :, 0:HEADS], ALU.subtract)
                        st.mark(dve.tensor_tensor(lin[:, :, :], G[:, tq, :, D:RW], looked[:, :, HEADS:], ALU.add))
                        st.sync()
                        leaky(dve, LG[:, r], lin[:, :, :])
                        wait(dve, vt_made, B * t)
                        dve.tensor_tensor(V[:, :, :, :], S[:, tq].unsqueeze(2).broadcast_to([W, B, HEADS, NT]),
                                          dif[:, :, :].unsqueeze(3).broadcast_to([W, B, HEADS, NT]), ALU.mult).then_inc(v_ready, 1)
                    if on(0):
                        wait(dve, pa_made, s - 3)
                        one_hot(dve, const, tab, s, S[:, q]).then_inc(s_ready, 1)
                    if on(5):
                        t, r, tq = s - 5, (q - 5) % 2, (q - 5) % NRING
                        nstep = Steps(dve, n_step, 1)
                        nstep.begin(t)
                        dve.wait_ge(rs_ready, t + 1)
                        wait(dve, stored[tq], 32 * (lap(t) - 1))
                        wait(dve, x3_ready, t)
                        normalise(dve, nstep, U[:, r], mv[:, r], rs[:, r], shift[:, :], X3[:, tq]).then_inc(x3_ready, 1)
                    if on(2):
                        t, r, tq = s - 2, q % 2, (q - 2) % NRING
                        mark_firsts(dve, const, tab, t, F[:, r], pa_made, t - 1)
                        dve.wait_ge(p_ready, t + 1)
                        dve.wait_ge(e_ready, t + 1)
                        wait(dve, pa_made, t - 1)
                        dve.tensor_tensor(by_head(R[:, r, :, 0:D]), by_head(G[:, tq, :, 0:D]),
                                          per_channel(R[:, r, :, D:], W), ALU.mult)
                        dve.tensor_tensor(by_head(HS[:, r, :, 0:D]), by_head(H[:, tq, :, 0:D]),
                                          per_channel(EE[:, tq, 0], NT), ALU.mult)
                        dve.tensor_copy(HS[:, r, :, D:], EE[:, tq, 0]).then_inc(r_ready, 1)
                    if on(1):
                        t, r, tq = s - 1, (q - 1) % 2, (q - 1) % NRING
                        st = Steps(dve, m_step, 4)
                        st.begin(t)
                        dve.wait_ge(own[tq], 16 * lap(t))
                        wait(dve, am_ready, t)
                        wait(dve, e_ready, t - 1)
                        wait(dve, l2_made, t - 3)
                        st.mark(dve.tensor_tensor(own_lin[:, :, :], H[:, tq, :, D:RW], H[:, tq, :, RW:], ALU.add))
                        st.sync()
                        leaky(dve, own_lg[:, :, :], own_lin[:, :, :])
                        for j in range(B):
                            dve.wait_ge(vt_made, B * t + j + 1)
                            dve.tensor_reduce(TOP[:, tq, j, :], pV[j % 2][:, :, :], AX.X, ALU.max).then_inc(vt_read, 1)
                        dve.wait_ge(vt_read, B * t + B)
                        st.mark(dve.tensor_scalar(TOP[:, tq], TOP[:, tq], 0.0, None, ALU.max))
                        waits_apart(dve, ready, [(m_step, st.base + st.n)])

                        def top_before():
                            dve.tensor_copy(keep4[:, :], tab["keep"][0:NT, bass.ds(t * B, B)])
                            dve.drain()
                            for j in range(B):
                                before = TOP[:, tq, j - 1] if j else TOP[:, (tq - 1) % NRING, B - 1]
                                dve.scalar_tensor_tensor(TOP[:, tq, j], before, keep4[:, j:j + 1], TOP[:, tq, j], ALU.mult, ALU.max)
                                dve.drain()
                        if_set(dve, tab["carry"], t, top_before)
                        st.mark(dve.tensor_tensor(own_lin[:, :, :], own_lin[:, :, :], TOP[:, tq], ALU.add))
                        st.sync()
                        st.mark(leaky(dve, AM[:, tq], own_lin[:, :, :]))
                        waits_apart(dve, ready, [(m_step, st.base + st.n)])

                        def max_before():
                            for j in range(B):
                                before = AM[:, tq, j - 1] if j else AM[:, (tq - 1) % NRING, B - 1]
                                dve.tensor_tensor(ES[:, r, 1, j], before, AM[:, tq, j], ALU.subtract)
                                dve.drain()
                                dve.tensor_scalar(ES[:, r, 1, j], ES[:, r, 1, j], keep4[:, j:j + 1], None, ALU.mult)
                                dve.drain()
                        if_set(dve, tab["carry"], t, max_before)
                        dve.tensor_tensor(ES[:, r, 0], own_lg[:, :, :], AM[:, tq], ALU.subtract).then_inc(am_ready, 1)
                    if on(4):
                        t, r, tq = s - 4, q % 2, q
                        st = Steps(dve, u_step, 6)
                        st.begin(t)
                        waits_apart(dve, ready, [(pa_ready, t + 1), (u_ready, t)])

                        def add_before():
                            dve.tensor_copy(keep4e[:, :], tab["keep"][0:NT, bass.ds(t * B, B)])
                            dve.drain()
                            for j in range(B):
                                before = A[:, tq, j - 1] if j else A[:, (tq - 1) % NRING, B - 1]
                                fade = EE[:, tq, 1, j]
                                dve.tensor_tensor(tmp[:, 0:D].rearrange("p (h c) -> p h c", h=HEADS),
                                                  before[:, 0:D].rearrange("p (h c) -> p h c", h=HEADS),
                                                  fade.unsqueeze(2).broadcast_to([NT, HEADS, HC]), ALU.mult)
                                dve.tensor_tensor(tmp[:, D:], before[:, D:], fade, ALU.mult)
                                dve.drain()
                                dve.scalar_tensor_tensor(A[:, tq, j], tmp[:, :], keep4e[:, j:j + 1], A[:, tq, j], ALU.mult, ALU.add)
                                dve.drain()
                        if_set(dve, tab["carry"], t, add_before)
                        st.mark(dve.tensor_scalar(den[:, :, :], A[:, tq, :, D:], 1e-16, None, ALU.add))
                        st.sync()
                        st.mark(dve.reciprocal(den[:, :, :], den[:, :, :]))
                        st.sync()
                        st.mark(dve.tensor_tensor(by_head(T[:, :, :]), by_head(A[:, tq, :, 0:D]), per_channel(den[:, :, :], NT), ALU.mult))
                        st.sync()
                        st.mark(dve.tensor_tensor(TB[:, :, :], T[:, :, :], w["row_L2_gnn_bias"][0:NT, :].unsqueeze(1).broadcast_to([NT, B, D]), ALU.add))
                        dve.wait_ge(own_x[tq], 16 * lap(t))
                        wait(dve, x3_ready, t - 1)
                        st.sync()
                        st.mark(dve.tensor_tensor(U[:, r], TB[:, :, :], X[:, tq], ALU.add))
                        st.sync()
                        norm_stats(dve, ready, st, U[:, r], stats, mv[:, r]).then_inc(u_ready, 1)
                        st.end()
                both_ranges(dve, tab["total"][0:1, 0:1], lambda a, b: turns(dve, a, b, 5, body))

            @block.scalar
            def _(act):
                def body(s, q, on):
                    if on(5):
                        t, r = s - 5, (q - 5) % 2
                        act.wait_ge(u_ready, t + 1)
                        wait(act, x3_ready, t - 1)
                        wait(act, rs_ready, t)
                        rstd(act, mv[:, r, :, 1], lg[:, :], rs[:, r], w["eps"][0:NT, :], log_step, t).then_inc(rs_ready, 1)
                    if on(2):
                        t, r = s - 2, q % 2
                        act.wait_ge(a_ready, t + 1)
                        wait(act, pa_made, t - 1)
                        act.activation(R[:, r, :, D:], arg[:, :, :], ACT.Exp).then_inc(p_ready, 1)
                    if on(3):
                        t, tq = s - 3, (q - 3) % NRING
                        act.wait_ge(pa_made, t + 1)
                        wait(act, u_ready, t - 2)
                        act.activation(A[:, tq], pA[:, :, 0:RW], ACT.Copy).then_inc(pa_ready, 1)
                    if on(0):
                        act.wait_ge(st_made, s + 1)
                        wait(act, l2_made, s - 3)
                        act.activation(ST[:, q], pST[:, :, :], ACT.Copy).then_inc(st_ready, 1)
                    if on(6):
                        t, r = s - 6, q % 2
                        act.wait_ge(xt_made, t + 1)
                        wait(act, qv_made, 2 * (t - 1))
                        act.activation(XT[:, r], pXT[:, :, :], ACT.Copy).then_inc(xt_ready, 1)
                    if on(1):
                        t, r, tq = s - 1, (q - 1) % 2, (q - 1) % NRING
                        act.wait_ge(am_ready, t + 1)
                        wait(act, u_ready, t - 3)
                        act.activation(EE[:, tq], ES[:, r], ACT.Exp).then_inc(e_ready, 1)
                    if on(6):
                        t, r, tq = s - 6, q % 2, (q - 6) % NRING
                        wait(act, stored[tq - 2], 32 * lap(t - 2))
                        for i in range(2):
                            act.wait_ge(qv_made, 2 * t + i + 1)
                            act.activation(QV[:, r, 2 * i:2 * i + 2, :], pQV[:, :, :], ACT.Copy).then_inc(qv_ready, 1)
                both_ranges(act, tab["total"][0:1, 0:1], lambda a, b: turns(act, a, b, 6, body))

            @block.tensor
            def _(pe):
                eye = const["eye"]
                bias = w["parts"][:, D:3 * D].unsqueeze(1).broadcast_to([3, 2, 2 * D])

                def body(s, q, on):
                    if on(1):
                        t, tq = s - 1, (q - 1) % NRING
                        pe.wait_ge(st_ready, t + 1)
                        pe.wait_ge(own[tq], 16 * lap(t))
                        wait(pe, v_ready, t)
                        for j in range(B):
                            last = pe.matmul(pL[:, 0, j * 2 * HEADS:(j + 1) * 2 * HEADS], ST[:, tq, j, :], H[:, tq, j, D:],
                                             start=True, stop=True)
                        last.then_inc(l1_made, 1)
                    if on(2):
                        t, tq = s - 2, (q - 2) % NRING
                        pe.wait_ge(am_ready, t + 1)
                        wait(pe, a_ready, t)
                        for j in range(B):
                            last = pe.matmul(pL[:, 1, j * HEADS:(j + 1) * HEADS], ST[:, tq, j, :], AM[:, tq, j, :],
                                             start=True, stop=True)
                        last.then_inc(l2_made, 1)
                    if on(3):
                        t, r, tq = s - 3, (q - 3) % 2, (q - 3) % NRING
                        pe.wait_ge(r_ready, t + 1)
                        wait(pe, pa_ready, t)
                        for j in range(B):
                            pe.matmul(pA[:, j, 0:RW], S[:, tq, j, :], R[:, r, j, :], start=True, stop=False)
                            last = pe.matmul(pA[:, j, 0:RW], F[:, r, j, :], HS[:, r, j, :], start=False, stop=True)
                        last.then_inc(pa_made, 1)
                    if on(6):
                        t, tq = s - 6, (q - 6) % NRING
                        pe.wait_ge(x3_ready, t + 1)
                        wait(pe, xt_ready, t)
                        for j in range(B):
                            last = pe.transpose(pXT[:, j, :], X3[:, tq, j, :], eye[0:NT, 0:NT])
                        last.then_inc(xt_made, 1)
                    if on(0):
                        pe.wait_ge(s_ready, s + 1)
                        wait(pe, st_ready, s)
                        for j in range(B):
                            last = pe.transpose(pST[:, j, :], S[:, q, j, :], eye[:, :])
                        last.then_inc(st_made, 1)
                    if on(1):
                        t = s - 1
                        pe.wait_ge(v_ready, t + 1)
                        for j in range(B):
                            wait(pe, vt_read, B * t + j - 1)
                            for h in range(HEADS):
                                last = pe.transpose(pV[j % 2][:, h, :], V[:, j, h, :], eye[:, :])
                            last.then_inc(vt_made, 1)
                    if on(6):
                        t, r = s - 6, q % 2
                        pe.wait_ge(xt_ready, t + 1)
                        for i in range(2):
                            wait(pe, qv_ready, 2 * t + i)
                            pe.matmul(pQV[:, :, :], w["ones3"][:, :], bias, start=True, stop=False)
                            for j in range(2):
                                last = pe.matmul(pQV[:, j, :], XT[:, r, 2 * i + j, :], w["qv"][:, :], start=False, stop=(j == 1))
                            last.then_inc(qv_made, 1)
                both_ranges(pe, tab["total"][0:1, 0:1], lambda a, b: turns(pe, a, b, 6, body))



def attention_layer(nc, tab, const, w, qv, x3, out):
    with ExitStack() as ctx:
        m = Mem(nc, ctx, "att")
        idx = m.sb("idx", [W, 2, B], I32)
        G = m.sb("gathered", [W, NRING, B, 2 * D])
        Q = m.sb("own_q", [NT, NRING, B, D])
        X = m.sb("own_x", [NT, NRING, B, D])
        S = m.sb("one_hot", [W, NRING, B, NT])
        ST = m.sb("one_hot_T", [NT, 2, B, W])
        junk = m.sb("junk", [W, B, D])
        sc = m.sb("score", [W, 2, B])
        EX = m.sb("exp_score", [W, 2, B])
        SW = m.sb("weighted_one_hot", [W, 2, B, NT])
        ones = m.sb("ones", [W, 1])
        AT = m.sb("sums_T", [D, NRING, B, NT])
        DN = m.sb("denominators", [NT, NRING, B, 1])
        rd = m.sb("reciprocals", [NT, B])
        XB = m.sb("x_bo", [NT, B, D])
        U = m.sb("summed", [NT, 2, B, D])
        stats = m.sb("stats", [NT, B, 6])
        mv = m.sb("mean_var", [NT, 2, B, 2])
        lg = m.sb("logs", [NT, 2, B])
        rs = m.sb("rstd", [NT, 2, B])
        shift = m.sb("shift", [NT, 2, B])
        Z = m.sb("normalised", [NT, 2, B, D])
        XC = m.sb("x_beta", [NT, B, D])
        ZG = m.sb("scaled", [NT, B, D])
        U2 = m.sb("summed2", [NT, 2, B, D])
        stats2 = m.sb("stats2", [NT, B, 6])
        mv2 = m.sb("mean_var2", [NT, 2, B, 2])
        rs2 = m.sb("rstd2", [NT, 2, B])
        shift2 = m.sb("shift2", [NT, 2, B])
        O = m.sb("out", [NT, 2, B, D])
        keep4 = m.sb("keep4", [D, B])
        keep4d = m.sb("keep4_den", [NT, B])
        pST = m.ps("one_hot_T", [NT, B, W])
        pQ = m.ps("centre_q", [W, B, D])
        pT = m.ps("sums_T", [D, B, NT])
        pD = m.ps("denominators", [NT, B])
        pZ = m.ps("product", [NT, B, D])
        ready, passed, sp_passed = m.sem("constants_set"), m.sem("waits_passed"), m.sem("sync_waits_passed")
        own, own_x, idx_ready, gathered = (m.sems("own_loaded"), m.sems("own_x_loaded"), m.sem("indices_ready"),
                                           m.sems("gathered"))
        s_ready, st_made, st_ready, q_made = (m.sem("one_hot_ready"), m.sem("one_hot_T_made"), m.sem("one_hot_T_ready"),
                                              m.sem("centre_q_made"))
        c_step, sc_ready, e_ready, sw_ready = m.sem("score_step"), m.sem("score_ready"), m.sem("exp_ready"), m.sem("weighted_ready")
        t_made, t_copied, t_ready, z_made = m.sem("sums_made"), m.sem("sums_copied"), m.sem("sums_ready"), m.sem("product_made")
        u_step, u_ready, log_step, rs_ready = m.sem("summed_step"), m.sem("summed_ready"), m.sem("log_step"), m.sem("rstd_ready")
        sh_ready, n_ready, z_read = m.sem("shift_ready"), m.sem("normalised_ready"), m.sem("product_read")
        u2_step, u2_ready, log2_step, rs2_ready = m.sem("summed2_step"), m.sem("summed2_ready"), m.sem("log2_step"), m.sem("rstd2_ready")
        sh2_ready, o_ready = m.sem("shift2_ready"), m.sem("out_ready")
        stored, part = m.sems("stored"), m.sem("tiles_moved")
        with nc.Block() as block:

            @block.sync
            def _(sp):
                def body(s, q, on):
                    if on(0):
                        waits_apart(sp, sp_passed, [(q_made, s - 3)])
                        own_rows(sp, tab, s, q, [(qv[:, 0:D], Q[:, q])], own, part, False)
                    if on(2):
                        t, tq = s - 2, (q - 2) % NRING
                        waits_apart(sp, sp_passed, [(u2_ready, t - 3)])
                        own_rows(sp, tab, t, tq, [(x3, X[:, tq])], own_x, part, False)
                    if on(6):
                        t, tq = s - 6, (q - 6) % NRING
                        waits_apart(sp, sp_passed, [(o_ready, t + 1)])
                        own_rows(sp, tab, t, tq, [(out, O[:, tq % 2])], stored, part, True)

                def run(first, last):
                    turns(sp, first, last, 6, body)
                    all_stored(sp, stored, 16, last)
                both_ranges(sp, tab["total"][0:1, 0:1], run)

            @block.gpsimd
            def _(pool):
                def body(s, q, on):
                    gather_rows(pool, tab, s, q, qv, idx, G, 2 * D, idx_ready, gathered, t_made, s - 3, passed)
                both_ranges(pool, tab["total"][0:1, 0:1], lambda a, b: turns(pool, a, b, 0, body))

            @block.vector
            def _(dve):
                dve.memset(DN[:, NRING - 1, B - 1, :], 0.0)
                dve.memset(AT[:, NRING - 1, B - 1, :], 0.0)
                dve.memset(ones[:, :], 1.0).then_inc(ready, 1)
                dve.wait_ge(ready, 1)

                def body(s, q, on):
                    if on(0):
                        wait(dve, t_made, s - 3)
                        one_hot(dve, const, tab, s, S[:, q]).then_inc(s_ready, 1)
                    if on(1):
                        t, r, tq = s - 1, (q - 1) % 2, (q - 1) % NRING
                        st = Steps(dve, c_step, 2)
                        st.begin(t)
                        dve.wait_ge(q_made, t + 1)
                        dve.wait_ge(gathered[tq], 16 * B * lap(t))
                        wait(dve, e_ready, t - 1)
                        wait(dve, sc_ready, t)
                        st.mark(dve.tensor_tensor(junk[:, :, :], pQ[:, :, :], G[:, tq, :, 0:D], ALU.mult))
                        st.sync()
                        st.mark(dve.tensor_reduce(sc[:, r], junk[:, :, :], AX.X, ALU.add))
                        st.sync()
                        dve.tensor_scalar(sc[:, r], sc[:, r], 5.0 * D ** 0.5, -5.0 * D ** 0.5, ALU.min, ALU.max).then_inc(sc_ready, 1)
                    if on(3):
                        t, tq = s - 3, (q - 3) % NRING
                        waits_apart(dve, ready, [(t_copied, t + 1)])
                        pass_on(dve, tab, t, AT, tq, keep4[:, :])
                        pass_on(dve, tab, t, DN, tq, keep4d[:, :])
                        dve.sem_inc(t_ready, 1)
                    if on(3):
                        t, tq = s - 3, (q - 3) % NRING
                        st = Steps(dve, u_step, 4)
                        st.begin(t)
                        dve.wait_ge(own_x[tq], 16 * lap(t))
                        wait(dve, u_ready, t)
                        st.mark(dve.tensor_tensor(XB[:, :, :], X[:, tq], w["row_L3_gnn_bo"][0:NT, :].unsqueeze(1).broadcast_to([NT, B, D]), ALU.add))
                        st.mark(dve.tensor_scalar(rd[:, :], DN[:, tq, :, 0], 1e-30, None, ALU.max))
                        st.sync()
                        st.mark(dve.reciprocal(rd[:, :], rd[:, :]))
                    if on(5):
                        t, r, tq = s - 5, (q - 5) % 2, (q - 5) % NRING
                        st2 = Steps(dve, u2_step, 4)
                        st2.begin(t)
                        wait(dve, u2_ready, t)
                        st2.mark(dve.tensor_tensor(XC[:, :, :], X[:, tq], w["row_L3_gnn_beta"][0:NT, :].unsqueeze(1).broadcast_to([NT, B, D]), ALU.add))
                        dve.wait_ge(n_ready, t + 1)
                        st2.mark(dve.tensor_tensor(ZG[:, :, :], Z[:, r], w["row_L3_gnn_gamma"][0:NT, :].unsqueeze(1).broadcast_to([NT, B, D]), ALU.mult))
                        wait(dve, o_ready, t - 1)
                        st2.sync()
                        st2.mark(dve.tensor_tensor(U2[:, r], ZG[:, :, :], XC[:, :, :], ALU.add))
                        st2.sync()
                        norm_stats(dve, ready, st2, U2[:, r], stats2, mv2[:, r]).then_inc(u2_ready, 1)
                        st2.end()
                    if on(1):
                        t, r, tq = s - 1, (q - 1) % 2, (q - 1) % NRING
                        dve.wait_ge(e_ready, t + 1)
                        wait(dve, t_made, t - 1)
                        dve.tensor_tensor(SW[:, r], S[:, tq], EX[:, r].unsqueeze(2).broadcast_to([W, B, NT]), ALU.mult).then_inc(sw_ready, 1)
                    if on(3):
                        t, r = s - 3, (q - 3) % 2
                        dve.wait_ge(z_made, t + 1)
                        wait(dve, n_ready, t - 1)
                        st.sync()
                        for j in range(B):
                            last = dve.scalar_tensor_tensor(U[:, r, j, :], pZ[:, j, :], rd[:, j:j + 1], XB[:, j, :], ALU.mult, ALU.add)
                        last.then_inc(z_read, 1)
                        dve.wait_ge(z_read, t + 1)
                        norm_stats(dve, ready, st, U[:, r], stats, mv[:, r]).then_inc(u_ready, 1)
                        st.end()
                    if on(4):
                        t, r = s - 4, q % 2
                        dve.wait_ge(rs_ready, t + 1)
                        wait(dve, n_ready, t - 1)
                        dve.scalar_tensor_tensor(shift[:, r], mv[:, r, :, 0], -1.0, rs[:, r], ALU.mult, ALU.mult).then_inc(sh_ready, 1)
                    if on(6):
                        t, r = s - 6, q % 2
                        dve.wait_ge(rs2_ready, t + 1)
                        wait(dve, o_ready, t - 1)
                        dve.scalar_tensor_tensor(shift2[:, r], mv2[:, r, :, 0], -1.0, rs2[:, r], ALU.mult, ALU.mult).then_inc(sh2_ready, 1)
                both_ranges(dve, tab["total"][0:1, 0:1], lambda a, b: turns(dve, a, b, 6, body))

            @block.scalar
            def _(act):
                def body(s, q, on):
                    if on(6):
                        t, r = s - 6, q % 2
                        act.wait_ge(u2_ready, t + 1)
                        wait(act, sh2_ready, t - 1)
                        wait(act, o_ready, t - 1)
                        act.activation(lg[:, 1], mv2[:, r, :, 1], ACT.Ln, bias=w["eps"][0:NT, :]).then_inc(log2_step, 1)
                    if on(4):
                        t, r = s - 4, q % 2
                        act.wait_ge(u_ready, t + 1)
                        wait(act, sh_ready, t - 1)
                        wait(act, n_ready, t - 1)
                        rstd(act, mv[:, r, :, 1], lg[:, 0], rs[:, r], w["eps"][0:NT, :], log_step, t).then_inc(rs_ready, 1)
                    if on(6):
                        t, r = s - 6, q % 2
                        act.wait_ge(log2_step, t + 1)
                        act.activation(rs2[:, r], lg[:, 1], ACT.Exp, scale=-0.5).then_inc(rs2_ready, 1)
                    if on(0):
                        act.wait_ge(st_made, s + 1)
                        wait(act, q_made, s - 1)
                        act.activation(ST[:, q % 2], pST[:, :, :], ACT.Copy).then_inc(st_ready, 1)
                    if on(2):
                        t, tq = s - 2, (q - 2) % NRING
                        act.wait_ge(t_made, t + 1)
                        wait(act, z_made, t - 3)
                        wait(act, u_ready, t - 2)
                        act.activation(DN[:, tq, :, 0], pD[:, :], ACT.Copy)
                        act.activation(AT[:, tq], pT[:, :, :], ACT.Copy).then_inc(t_copied, 1)
                    if on(1):
                        t, r = s - 1, (q - 1) % 2
                        act.wait_ge(sc_ready, t + 1)
                        wait(act, sw_ready, t - 1)
                        act.activation(EX[:, r], sc[:, r], ACT.Exp, scale=D ** -0.5).then_inc(e_ready, 1)
                    if on(4):
                        t, r = s - 4, q % 2
                        act.wait_ge(sh_ready, t + 1)
                        wait(act, u2_ready, t - 1)
                        for j in range(B):
                            last = act.activation(Z[:, r, j, :], U[:, r, j, :], ACT.Identity, scale=rs[:, r, j:j + 1], bias=shift[:, r, j:j + 1])
                        last.then_inc(n_ready, 1)
                    if on(6):
                        t, r, tq = s - 6, q % 2, (q - 6) % NRING
                        act.wait_ge(sh2_ready, t + 1)
                        wait(act, stored[tq - 2], 16 * lap(t - 2))
                        for j in range(B):
                            last = act.activation(O[:, r, j, :], U2[:, r, j, :], ACT.Identity, scale=rs2[:, r, j:j + 1], bias=shift2[:, r, j:j + 1])
                        last.then_inc(o_ready, 1)
                both_ranges(act, tab["total"][0:1, 0:1], lambda a, b: turns(act, a, b, 6, body))

            @block.tensor
            def _(pe):
                def body(s, q, on):
                    if on(2):
                        t, r, tq = s - 2, q % 2, (q - 2) % NRING
                        pe.wait_ge(sw_ready, t + 1)
                        wait(pe, t_copied, t)
                        for j in range(B):
                            pe.matmul(pT[:, j, :], G[:, tq, j, D:], SW[:, r, j, :], start=True, stop=True)
                            last = pe.matmul(pD[:, j:j + 1], SW[:, r, j, :], ones[:, :], start=True, stop=True)
                        last.then_inc(t_made, 1)
                    if on(1):
                        t, r, tq = s - 1, (q - 1) % 2, (q - 1) % NRING
                        pe.wait_ge(st_ready, t + 1)
                        pe.wait_ge(own[tq], 16 * lap(t))
                        wait(pe, sc_ready, t)
                        for j in range(B):
                            last = pe.matmul(pQ[:, j, :], ST[:, r, j, :], Q[:, tq, j, :], start=True, stop=True)
                        last.then_inc(q_made, 1)
                    if on(0):
                        pe.wait_ge(s_ready, s + 1)
                        wait(pe, st_ready, s)
                        for j in range(B):
                            last = pe.transpose(pST[:, j, :], S[:, q, j, :], const["eye"][:, :])
                        last.then_inc(st_made, 1)
                    if on(3):
                        t, tq = s - 3, (q - 3) % NRING
                        pe.wait_ge(t_ready, t + 1)
                        wait(pe, z_read, t)
                        for j in range(B):
                            last = pe.matmul(pZ[:, j, :], AT[:, tq, j, :], w["L3_gnn_Wo"][:, :], start=True, stop=True)
                        last.then_inc(z_made, 1)
                both_ranges(pe, tab["total"][0:1, 0:1], lambda a, b: turns(pe, a, b, 3, body))



def four_graph_layers(nc, ins, out):
    def scratch(name, shape):
        return nc.dram_tensor(name, shape, F32, kind="Internal").ap()

    hist = {k: scratch(f"hist_{k}", [TILES]) for k in KEYS}
    item_rows = {k: scratch(f"item_rows_{k}", [3, MAXI]) for k in KEYS}
    x1, x2, x3 = (scratch(f"x{i}", [N, D]) for i in (1, 2, 3))
    y1, y2 = scratch("y1", [N, D]), scratch("y2", [N, D])
    h = scratch("gat_rows", [N, D + 2 * HEADS])
    qv = scratch("qv", [N, 2 * D])
    with ExitStack() as ctx:
        keep = Mem(nc, ctx, "keep")
        const = dict(eye=keep.sb("eye", [128, 128]), neg_eye=keep.sb("neg_eye", [128, 128]), iota=keep.sb("iota", [128, NT]))
        tab = sort_edges(nc, keep, {k: ins[k] for k in KEYS}, hist, item_rows, const)
        w = load_weights(nc, keep, ins, const)
        dis = keep.sb("inverse_root_degree", [NT, MAXI])
        gated_layer(nc, tab["dst"], const, w, dis, ins["x"], x1, y1)
        convolution(nc, tab["dst"], const, w, dis, "conv1", "L1_gnn_W1", "L1_gnn_b1", y1, y_out=y2)
        convolution(nc, tab["dst"], const, w, dis, "conv2", "L1_gnn_W2", "L1_gnn_b2", y2, x_in=x1, x_out=x2, gat=h)
        gat_layer(nc, tab["src"], const, w, h, x2, x3, qv)
        attention_layer(nc, tab["dst"], const, w, qv, x3, out)


_INS = ['x', 'src', 'dst', 'L0_gnn_W1', 'L0_gnn_b1', 'L0_gnn_W2', 'L0_gnn_b2', 'L0_gnn_W4', 'L0_gnn_b4',
        'L1_gnn_W1', 'L1_gnn_b1', 'L1_gnn_W2', 'L1_gnn_b2', 'L2_gnn_weight', 'L2_gnn_att', 'L2_gnn_bias',
        'L3_gnn_Wqk', 'L3_gnn_bqk', 'L3_gnn_Wv', 'L3_gnn_bv', 'L3_gnn_Wo', 'L3_gnn_bo', 'L3_gnn_gamma', 'L3_gnn_beta']
_OUTS = [((50000, 128), 'float32')]


def kernel(**inputs):
    import numpy as _np
    import concourse.bacc as _bacc
    from concourse import mybir as _mybir
    from concourse.bass_utils import run_bass_kernel_spmd as _run

    nc = _bacc.Bacc("TRN2", target_bir_lowering=False, num_devices=1)
    arrays, ins, outs = {}, {}, []
    for name in _INS:
        a = _np.ascontiguousarray(inputs[name])
        arrays[f"in_{name}_dram"] = a
        ins[name] = nc.dram_tensor(f"in_{name}_dram", a.shape, _mybir.dt.from_np(a.dtype), kind="ExternalInput").ap()
    for i, (shape, dtype) in enumerate(_OUTS):
        dt = _mybir.dt.from_np(_np.dtype(dtype))
        outs.append(nc.dram_tensor(f"out_{i}_dram", shape, dt, kind="ExternalOutput").ap())
    four_graph_layers(nc, ins, outs[0])
    r = _run(nc, [arrays], core_ids=[0])
    return r.results[0]["out_0_dram"]
```

```python
from contextlib import ExitStack

import numpy as np
import concourse.bass as bass
from concourse import mybir
from concourse.alu_op_type import AluOpType as ALU

F32, I32 = mybir.dt.float32, mybir.dt.int32
F16, BF16 = mybir.dt.float16, mybir.dt.bfloat16
ACT = mybir.ActivationFunctionType
AX = mybir.AxisListType

N = 50000
E = 50000
D = 128
HEADS, HC = 4, 32
NT = 100
TILES = N // NT
W = 128
EP = 125
CH = E // EP
B = 4
MAIN = 504
PLACE = 512
MAXI = 896
MAGIC = 12582912.0
BIG = 131072.0
HI, LO = 25, 20
SPLIT = 2048
NRING = 4
GROUPS = MAXI // B // NRING
HEAD = 4 * NRING
KEYS = ("dst", "src")
EPS = 1e-5
TABLES = "natural_log_exp_and_others"


def wait(eng, sem, value):
    if not isinstance(value, int) or value > 0:
        eng.wait_ge(sem, value)


def turns(eng, first, last, lag, body, either=None):
    head = first + max(lag, NRING) + NRING
    head += (-head) % NRING
    tail = head + (last - 1 - head) // NRING * NRING
    assert lag <= 2 * NRING
    if either is None:
        def either(part, where, r):
            part(None)

    def peeled(lo, hi):
        def part(quiet):
            for s in range(lo, hi):
                body(s, s % NRING, lambda k: first <= s - k < last, quiet)
        return part

    either(peeled(first, head), "head", head)
    with eng.Fori(head // NRING, tail // NRING) as r:
        def part(quiet):
            for q in range(NRING):
                body(r * NRING + q, q, lambda k: True, quiet)
        either(part, "middle", r)
    either(peeled(tail, last + lag), "tail", tail)


def lap(t):
    return t // NRING + 1


def waits_apart(eng, passed, pairs):
    for sem, value in pairs:
        wait(eng, sem, value)
    eng.sem_inc(passed, 1)


class Steps:

    def __init__(self, eng, sem, per):
        self.eng, self.sem, self.per = eng, sem, per

    def begin(self, t):
        self.base, self.n = t * self.per, 0

    def mark(self, ins):
        self.n += 1
        assert self.n <= self.per
        return ins.then_inc(self.sem, 1)

    def sync(self):
        self.eng.wait_ge(self.sem, self.base + self.n)

    def end(self):
        assert self.n == self.per, (self.n, self.per)


def both_ranges(eng, tab, run):
    run(0, MAIN // B)
    total = eng.value_load(tab["total"][0:1, 0:1], min_val=0, max_val=MAXI)
    with eng.If(total > MAIN):
        run(MAIN // B, MAXI // B)
    with eng.Else():
        pass


def sweep(eng, tab, lag, body):
    both_ranges(eng, tab, lambda first, last: turns(eng, first, last, lag, body))


def quiet_sweep(eng, tab, lag, body):
    def either(part, where, r):
        flags = {"head": tab["quiet_head"][0:1, 0:1], "tail": tab["quiet_tail"][0:1, 0:1]}
        flag = eng.value_load(tab["quiet"][0:1, bass.ds(r, 1)] if where == "middle" else flags[where], min_val=0, max_val=1)
        with eng.If(flag > 0):
            part(True)
        with eng.Else():
            part(False)

    def run(first, last):
        turns(eng, first, last, lag, body, either if first == 0 else None)
    both_ranges(eng, tab, run)


class Mem:

    def __init__(self, nc, ctx, tag):
        self.nc, self.ctx, self.tag, self.held = nc, ctx, tag, []
        ctx.callback(self.release)

    def release(self):
        if self.held:
            self.nc.clear_and_free_semaphores(self.held)
            self.nc.all_engine_barrier()

    def sb(self, name, shape, dt=F32):
        return self.ctx.enter_context(self.nc.sbuf_tensor(f"{self.tag}_{name}", shape, dt))

    def ps(self, name, shape, dt=F32):
        return self.ctx.enter_context(self.nc.psum_tensor(f"{self.tag}_bank_{name}", shape, dt))

    def sems(self, name):
        return [self.sem(f"{name}_{q}") for q in range(NRING)]

    def sem(self, name):
        self.held.append(self.nc.alloc_semaphore(f"{self.tag}_{name}"))
        return self.held[-1]



def sort_edges(nc, keep, key_dram, hist_dram, rows_dram, const):
    tab = {k: {} for k in KEYS}
    for k in KEYS:
        t = tab[k]
        t["other"] = keep.sb(f"other_{k}", [W, MAXI], I32)
        t["local"] = keep.sb(f"local_{k}", [W, MAXI])
        t["total"] = keep.sb(f"total_{k}", [1, 1], I32)
        t["keep"] = keep.sb(f"keep_{k}", [128, MAXI])
        t["first"] = keep.sb(f"first_{k}", [128, MAXI])
        t["row"] = keep.sb(f"row_{k}", [1, MAXI], I32)
        t["last"] = keep.sb(f"last_{k}", [1, MAXI], I32)
        t["plain"] = keep.sb(f"plain_{k}", [1, MAXI // B], I32)
        t["carry"] = keep.sb(f"carry_{k}", [1, MAXI // B], I32)
        t["quiet"] = keep.sb(f"quiet_{k}", [1, GROUPS], I32)
        t["quiet_head"] = keep.sb(f"quiet_head_{k}", [1, 1], I32)
        t["quiet_tail"] = keep.sb(f"quiet_tail_{k}", [1, 1], I32)
        t["straight"] = keep.sb(f"straight_{k}", [1, GROUPS], I32)
        t["straight_head"] = keep.sb(f"straight_head_{k}", [1, 1], I32)
        t["again"] = keep.sb(f"again_{k}", [1, MAXI // B], I32)

    with ExitStack() as outer:
        m = Mem(nc, outer, "sort")
        iota_i = m.sb("iota_i", [128, MAXI], I32)
        iota_h = m.sb("iota_h", [128, MAXI], F16)
        iota_f = m.sb("iota_f", [128, HI])
        item_no = m.sb("item_no", [128, MAXI // 128])
        item_no_i = m.sb("item_no_i", [128, MAXI // 128], I32)
        diff_i = m.sb("diff_i", [128, 128], I32)
        earlier = m.sb("earlier", [EP, EP], F16)
        not_earlier = m.sb("not_earlier", [EP, EP], F16)
        big_eye = m.sb("big_eye", [EP, EP], BF16)
        neg_big_eye = m.sb("neg_big_eye", [EP, EP], BF16)
        ones_row = m.sb("ones_row", [1, EP])
        neg_big = m.sb("neg_big", [128, 1])
        node_i = {k: m.sb(f"node_i_{k}", [EP, CH], I32) for k in KEYS}
        node = {k: m.sb(f"node_{k}", [EP, CH]) for k in KEYS}
        tile = {k: m.sb(f"tile_{k}", [EP, CH]) for k in KEYS}
        low = {k: m.sb(f"low_{k}", [EP, CH]) for k in KEYS}
        high = {k: m.sb(f"high_{k}", [EP, CH]) for k in KEYS}
        pos = {k: m.sb(f"pos_{k}", [EP, CH]) for k in KEYS}
        item = {k: m.sb(f"item_{k}", [EP, CH]) for k in KEYS}
        start = {k: m.sb(f"start_{k}", [128, TILES]) for k in KEYS}
        end = {k: m.sb(f"end_{k}", [128, TILES]) for k in KEYS}
        base = {k: m.sb(f"base_{k}", [128, TILES]) for k in KEYS}

        G = 20
        with ExitStack() as inner:
            p = Mem(nc, inner, "hist")
            thi = {k: p.sb(f"thi_{k}", [EP, CH]) for k in KEYS}
            tlo = {k: p.sb(f"tlo_{k}", [EP, CH]) for k in KEYS}
            hot_hi = {k: p.sb(f"hot_hi_{k}", [EP, 2, G, HI]) for k in KEYS}
            hot_lo = {k: p.sb(f"hot_lo_{k}", [EP, 2, G, LO]) for k in KEYS}
            hist = {k: p.ps(f"hist_{k}", [HI, LO]) for k in KEYS}
            hist_sb = p.sb("hist_sb", [HI, 2, LO])
            iotas, loaded, step = p.sem("iotas_ready"), p.sem("edges_loaded"), p.sem("vector_step")
            hot_ready, counted = p.sem("one_hots_ready"), p.sem("chunks_counted")
            hist_ready, stored, spread = p.sem("histogram_ready"), p.sem("histogram_stored"), p.sem("histogram_spread")
            with nc.Block() as block:

                @block.sync
                def _(sp):
                    for k in KEYS:
                        sp.dma_start(node_i[k][:, :], key_dram[k].rearrange("(p c) -> p c", c=CH)).then_inc(loaded, 16)
                    sp.wait_ge(hist_ready, 1)
                    for n, k in enumerate(KEYS):
                        sp.dma_start(hist_dram[k].rearrange("(h l) -> h l", l=LO), hist_sb[:, n, :]).then_inc(stored, 16)
                    sp.wait_ge(stored, 32)
                    for k in KEYS:
                        row = hist_dram[k].rearrange("(a t) -> a t", a=1)
                        sp.dma_start(base[k][:, :], row.broadcast_to([128, TILES])).then_inc(spread, 16)

                @block.gpsimd
                def _(pool):
                    pool.iota(iota_i[:, :], [[1, MAXI]], base=0, channel_multiplier=0)
                    pool.iota(item_no_i[:, :], [[128, MAXI // 128]], base=0, channel_multiplier=1)
                    pool.iota(diff_i[:, :], [[1, 128]], base=0, channel_multiplier=-1).then_inc(iotas, 1)

                @block.vector
                def _(dve):
                    c = Steps(dve, step, 10 ** 6)
                    c.begin(0)

                    def do(ins):
                        c.mark(ins)
                        c.sync()

                    def rounded(out, in_, scale, shift):
                        do(dve.tensor_scalar(out, in_, scale, shift, ALU.mult, ALU.add))
                        do(dve.tensor_scalar(out, out, MAGIC, MAGIC, ALU.add, ALU.subtract))

                    dve.wait_ge(iotas, 1)
                    dve.tensor_copy(iota_h[:, :], iota_i[:, :])
                    dve.tensor_copy(iota_f[:, :], iota_i[:, 0:HI])
                    dve.tensor_copy(item_no[:, :], item_no_i[:, :])
                    below = diff_i[0:EP, 0:EP]
                    dve.tensor_scalar(earlier[:, :], below, 0.0, None, ALU.is_gt)
                    dve.tensor_scalar(not_earlier[:, :], below, 0.0, None, ALU.is_le)
                    dve.tensor_scalar(big_eye[:, :], below, 0.0, BIG, ALU.is_equal, ALU.mult)
                    dve.tensor_scalar(neg_big_eye[:, :], below, 0.0, -BIG, ALU.is_equal, ALU.mult)
                    dve.tensor_scalar(const["eye"][:, :], diff_i[:, :], 0.0, None, ALU.is_equal)
                    dve.tensor_scalar(const["neg_eye"][:, :], diff_i[:, :], 0.0, -1.0, ALU.is_equal, ALU.mult)
                    dve.tensor_copy(const["iota"][:, :], iota_i[:, 0:NT])
                    dve.memset(neg_big[:, :], -BIG)
                    do(dve.memset(ones_row[:, :], 1.0))
                    dve.wait_ge(loaded, 32)
                    for k in KEYS:
                        do(dve.tensor_copy(node[k][:, :], node_i[k][:, :]))
                    for k, o in zip(KEYS, reversed(KEYS)):
                        rounded(tile[k][:, :], node[k][:, :], 1.0 / NT, -0.495)
                        rounded(thi[k][:, :], tile[k][:, :], 1.0 / LO, -0.475)
                        do(dve.scalar_tensor_tensor(tlo[k][:, :], thi[k][:, :], -float(LO), tile[k][:, :], ALU.mult, ALU.add))
                        rounded(item[k][:, :], node[o][:, :], 1.0 / SPLIT, -0.49975)
                        do(dve.scalar_tensor_tensor(low[k][:, :], item[k][:, :], -float(SPLIT), node[o][:, :], ALU.mult, ALU.add))
                        do(dve.tensor_scalar(low[k][:, :], low[k][:, :], 1.0, None, ALU.add))
                        do(dve.scalar_tensor_tensor(pos[k][:, :], tile[k][:, :], -float(NT), node[k][:, :], ALU.mult, ALU.add))
                        do(dve.tensor_scalar(pos[k][:, :], pos[k][:, :], NT / 2.0, float(HI), ALU.subtract, ALU.mult))
                        do(dve.tensor_tensor(high[k][:, :], pos[k][:, :], item[k][:, :], ALU.add))
                    for s in range(CH // G):
                        wait(dve, counted, 2 * (s - 1))
                        for k in KEYS:
                            at = slice(s * G, (s + 1) * G)
                            dve.tensor_tensor(hot_hi[k][:, s % 2], iota_f[0:EP, :].unsqueeze(1).broadcast_to([EP, G, HI]),
                                              thi[k][:, at].unsqueeze(2).broadcast_to([EP, G, HI]), ALU.is_equal)
                            dve.tensor_tensor(hot_lo[k][:, s % 2], iota_f[0:EP, 0:LO].unsqueeze(1).broadcast_to([EP, G, LO]),
                                              tlo[k][:, at].unsqueeze(2).broadcast_to([EP, G, LO]), ALU.is_equal).then_inc(hot_ready, 1)
                    dve.wait_ge(counted, 2 * (CH // G))
                    dve.tensor_copy(hist_sb[:, 0, :], hist["dst"][:, :])
                    dve.tensor_copy(hist_sb[:, 1, :], hist["src"][:, :]).then_inc(hist_ready, 1)

                    dve.wait_ge(spread, 32)
                    for n, k in enumerate(KEYS):
                        rounded(start[k][:, :], base[k][:, :], 1.0 / W, (W - 1) / W - 0.498)
                        do(dve.tensor_scalar(start[k][:, :], start[k][:, :], 1.0, None, ALU.max))
                        do(dve.tensor_tensor_scan(end[k][:, :], start[k][:, :], start[k][:, :], 0.0, ALU.add, ALU.bypass))
                        do(dve.tensor_tensor(start[k][:, :], end[k][:, :], start[k][:, :], ALU.subtract))
                        do(dve.tensor_scalar(base[k][:, :], start[k][:, :], float(W), None, ALU.mult))
                        do(dve.tensor_copy(tab[k]["total"][:, :], end[k][0:1, TILES - 1:TILES]))

                @block.tensor
                def _(pe):
                    for s in range(CH // G):
                        for n, k in enumerate(KEYS):
                            pe.wait_ge(hot_ready, 2 * s + n + 1)
                            for g in range(G):
                                last = pe.matmul(hist[k][:, :], hot_hi[k][:, s % 2, g, :], hot_lo[k][:, s % 2, g, :],
                                                 start=(s == 0 and g == 0), stop=(s == CH // G - 1 and g == G - 1))
                            last.then_inc(counted, 1)

        with ExitStack() as inner:
            p = Mem(nc, inner, "flags")
            NG = MAXI // 128
            junk = p.sb("junk", [128, TILES])
            col = {k: p.sb(f"col_{k}", [128, 3, NG]) for k in KEYS}
            tiles = {k: p.sb(f"tiles_{k}", [1, MAXI]) for k in KEYS}
            lasts = {k: p.sb(f"lasts_{k}", [1, MAXI]) for k in KEYS}
            f1 = p.sb("f1", [1, MAXI // B])
            f2 = p.sb("f2", [1, MAXI // B])
            idle = p.sb("idle", [128, MAXI])
            g1 = p.sb("g1", [1, GROUPS])
            g2 = p.sb("g2", [1, GROUPS])
            step, cols, stored, spread = p.sem("vector_step"), p.sem("columns_ready"), p.sem("stored"), p.sem("spread")
            with nc.Block() as block:

                @block.sync
                def _(sp):
                    for n, k in enumerate(KEYS):
                        sp.wait_ge(cols, n + 1)
                        for w in range(3):
                            sp.dma_start(rows_dram[k][w].rearrange("(g p) -> p g", p=128), col[k][:, w, :],
                                         allow_slow_non_contiguous=True).then_inc(stored, 16)
                    sp.wait_ge(stored, 96)
                    for k in KEYS:
                        row = [rows_dram[k][w].rearrange("(a t) -> a t", a=1) for w in range(3)]
                        sp.dma_start(tiles[k][:, :], row[0]).then_inc(spread, 16)
                        sp.dma_start(tab[k]["first"][:, :], row[1].broadcast_to([128, MAXI])).then_inc(spread, 16)
                        sp.dma_start(lasts[k][:, :], row[2]).then_inc(spread, 16)

                @block.vector
                def _(dve):
                    c = Steps(dve, step, 10 ** 6)
                    c.begin(0)

                    def do(ins):
                        c.mark(ins)
                        c.sync()

                    for k in KEYS:
                        do(dve.tensor_scalar(end[k][:, :], end[k][:, :], 1.0, None, ALU.subtract))
                        for g in range(NG):
                            for w, (row, op) in enumerate(((start, ALU.is_le), (start, ALU.is_equal), (end, ALU.is_equal))):
                                do(dve.tensor_scalar(junk[:, :], row[k][:, :], item_no[:, g:g + 1], 0.0, op, ALU.add,
                                                     accum_out=col[k][:, w, g:g + 1]))
                        do(dve.tensor_scalar(col[k][:, 0, :], col[k][:, 0, :], 1.0, None, ALU.subtract))
                        dve.sem_inc(cols, 1)
                    dve.wait_ge(spread, 96)
                    for k in KEYS:
                        t = tab[k]
                        by4 = tiles[k][:, :].rearrange("a (b j) -> a b j", j=B)
                        last4 = lasts[k][:, :].rearrange("a (b j) -> a b j", j=B)
                        do(dve.tensor_scalar(idle[:, :], iota_h[:, :], end[k][:, TILES - 1:TILES], None, ALU.is_gt))
                        do(dve.tensor_tensor(t["first"][:, :], t["first"][:, :], idle[:, :], ALU.max))
                        do(dve.tensor_scalar(t["keep"][:, :], t["first"][:, :], -1.0, 1.0, ALU.mult, ALU.add))
                        do(dve.tensor_scalar(t["row"][:, :], tiles[k][:, :], float(NT), None, ALU.mult))
                        do(dve.tensor_copy(t["last"][:, :], lasts[k][:, :]))
                        do(dve.tensor_tensor(f1[:, :], by4[:, :, B - 1], by4[:, :, 0], ALU.subtract))
                        do(dve.scalar_tensor_tensor(f1[:, :], f1[:, :], float(B - 1), last4[:, :, B - 1], ALU.is_equal, ALU.mult))
                        do(dve.tensor_copy(t["plain"][:, :], f1[:, :]))
                        keep4 = t["keep"][0:1, :].rearrange("a (b j) -> a b j", j=B)
                        do(dve.tensor_reduce(f1[:, :], keep4, AX.X, ALU.max))
                        do(dve.tensor_copy(t["carry"][:, :], f1[:, :]))
                        do(dve.tensor_copy(f2[:, 0:2], f1[:, 0:2]))
                        do(dve.tensor_tensor(f2[:, 2:], f1[:, 2:], f1[:, :MAXI // B - 2], ALU.max))
                        do(dve.tensor_copy(t["again"][:, :], f2[:, :]))
                        GI = NRING * B
                        group = keep4.rearrange("a b j -> a (b j)").rearrange("a (g i) -> a g i", i=GI)
                        do(dve.tensor_reduce(g1[:, :], group, AX.X, ALU.max))
                        do(dve.tensor_copy(g2[:, 0:2], g1[:, 0:2]))
                        do(dve.tensor_tensor(g2[:, 2:], g1[:, 2:], g1[:, 1:GROUPS - 1], ALU.max))
                        do(dve.tensor_tensor(g2[:, 2:], g2[:, 2:], g1[:, 0:GROUPS - 2], ALU.max))
                        do(dve.tensor_scalar(t["quiet"][:, :], g2[:, :], 0.0, None, ALU.is_equal))
                        for flag, span in ((t["quiet_head"], t["keep"][0:1, 0:HEAD * B]),
                                           (t["quiet_tail"], t["keep"][0:1, MAIN - 3 * GI:MAIN])):
                            do(dve.tensor_reduce(g1[:, 0:1], span, AX.X, ALU.max))
                            do(dve.tensor_scalar(flag[:, :], g1[:, 0:1], 0.0, None, ALU.is_equal))
                        tile_g = tiles[k][:, :].rearrange("a (g i) -> a g i", i=GI)
                        last_g = lasts[k][:, :].rearrange("a (g i) -> a g i", i=GI)
                        first_g = t["first"][0:1, :].rearrange("a (g i) -> a g i", i=GI)
                        do(dve.memset(g1[:, 0:2], 0.0))
                        do(dve.tensor_tensor(g1[:, 2:], tile_g[:, 2:, GI - 1], tile_g[:, 0:GROUPS - 2, 0], ALU.subtract))
                        do(dve.scalar_tensor_tensor(g1[:, 2:], g1[:, 2:], float(3 * GI - 1), last_g[:, 2:, GI - 1], ALU.is_equal, ALU.mult))
                        do(dve.tensor_tensor(g1[:, 2:], g1[:, 2:], first_g[:, 0:GROUPS - 2, 0], ALU.mult))
                        do(dve.tensor_copy(t["straight"][:, :], g1[:, :]))
                        do(dve.scalar_tensor_tensor(g1[:, 0:1], tiles[k][:, HEAD * B - 1:HEAD * B], float(HEAD * B - 1),
                                                    lasts[k][:, HEAD * B - 1:HEAD * B], ALU.is_equal, ALU.mult))
                        do(dve.tensor_copy(t["straight_head"][:, :], g1[:, 0:1]))

        with ExitStack() as inner:
            p = Mem(nc, inner, "rank")
            hot = {k: p.sb(f"hot_{k}", [EP, NRING, TILES], F16) for k in KEYS}
            rank = {k: p.ps(f"rank_{k}", [EP, TILES]) for k in KEYS}
            junk = {k: p.sb(f"junk_{k}", [EP, TILES], F16 if k == "dst" else F32) for k in KEYS}
            got = {k: p.sb(f"got_{k}", [EP, 2, NRING]) for k in KEYS}
            hot_ready = p.sem("one_hots_ready")
            added = {k: p.sem(f"earlier_added_{k}") for k in KEYS}
            picked = {k: p.sem(f"position_picked_{k}") for k in KEYS}
            moved = {k: p.sem(f"positions_moved_{k}") for k in KEYS}
            counted = p.sem("chunk_counted")
            with nc.Block() as block:

                @block.vector
                def _(dve):
                    def body(s, q, on, quiet):
                        if on(0):
                            wait(dve, counted, 2 * (s - NRING + 1))
                            for k in KEYS:
                                last = dve.tensor_scalar(hot[k][:, q], iota_h[0:EP, 0:TILES], tile[k][:, bass.ds(s, 1)],
                                                         None, ALU.is_equal)
                            last.then_inc(hot_ready, 1)
                        if on(2):
                            t, r = s - 2, (q - 2) % NRING
                            dve.wait_ge(added["dst"], t + 1)
                            dve.tensor_tensor_reduce(out=junk["dst"][:, :], in0=rank["dst"][:, :], in1=hot["dst"][:, r],
                                                     scale=1.0, scalar=0.0, op0=ALU.mult, op1=ALU.add,
                                                     accum_out=got["dst"][:, 0, r:r + 1]).then_inc(picked["dst"], 1)
                            if r == NRING - 1:
                                dve.wait_ge(picked["dst"], t + 1)
                                dve.tensor_copy(pos["dst"][:, bass.ds(t - (NRING - 1), NRING)], got["dst"][:, 0]).then_inc(moved["dst"], 1)
                                dve.wait_ge(moved["dst"], (t + 1) // NRING)
                    turns(dve, 0, CH, 2, body)

                @block.scalar
                def _(act):
                    def body(s, q, on, quiet):
                        if on(0):
                            act.wait_ge(added["src"], s + 1)
                            act.activation(junk["src"][:, :], rank["src"][:, :], ACT.Relu, bias=neg_big[0:EP, :],
                                           accum_out=got["src"][:, 0, q:q + 1]).then_inc(picked["src"], 1)
                            if q == NRING - 1:
                                act.wait_ge(picked["src"], s + 1)
                                act.activation(pos["src"][:, bass.ds(s - (NRING - 1), NRING)], got["src"][:, 0], ACT.Copy).then_inc(moved["src"], 1)
                                act.wait_ge(moved["src"], (s + 1) // NRING)
                    turns(act, 0, CH, 0, body)

                @block.tensor
                def _(pe):
                    for k in KEYS:
                        pe.matmul(rank[k][:, :], ones_row[:, :], base[k][0:1, :], start=True, stop=True)

                    def body(s, q, on, quiet):
                        if on(0):
                            pe.wait_ge(hot_ready, s + 1)
                        for k in KEYS:
                            if on(1):
                                r = (q - 1) % NRING
                                pe.wait_ge(picked[k], s)
                                last = pe.matmul(rank[k][:, :], not_earlier[:, :], hot[k][:, r], start=False, stop=True, skip_group_check=True)
                                if k == "src":
                                    last = pe.matmul(rank[k][:, :], neg_big_eye[:, :], hot[k][:, r], start=False, stop=True, skip_group_check=True)
                                last.then_inc(counted, 1)
                            if on(0):
                                last = pe.matmul(rank[k][:, :], earlier[:, :], hot[k][:, q], start=False, stop=True, skip_group_check=True)
                                if k == "src":
                                    last = pe.matmul(rank[k][:, :], big_eye[:, :], hot[k][:, q], start=False, stop=True, skip_group_check=True)
                                last.then_inc(added[k], 1)
                    turns(pe, 0, CH, 1, body)
                    pe.wait_ge(counted, 2 * CH)

        with ExitStack() as inner:
            p = Mem(nc, inner, "place")
            in_item = {k: p.sb(f"in_item_{k}", [EP, NRING, PLACE], F16) for k in KEYS}
            in_slot = {k: p.sb(f"in_slot_{k}", [EP, NRING, 2, W], F16) for k in KEYS}
            plane = {k: [p.ps(f"plane{n}_{k}", [W, PLACE]) for n in range(2)] for k in KEYS}
            v1 = p.sb("v1", [W, PLACE])
            v2 = p.sb("v2", [W, PLACE])
            v3 = p.sb("v3", [W, PLACE])
            v4 = p.sb("v4", [W, PLACE])
            step, hot_ready, placed = p.sem("vector_step"), p.sem("one_hots_ready"), p.sem("chunk_placed")
            filled, tstep = p.sem("empty_slots_set"), p.sem("table_step")
            with nc.Block() as block:

                @block.vector
                def _(dve):
                    c = Steps(dve, step, 10 ** 6)
                    c.begin(0)

                    def do(ins):
                        c.mark(ins)
                        c.sync()

                    for k in KEYS:
                        t = tab[k]
                        dve.memset(t["other"][:, MAIN:], 0)
                        dve.memset(t["local"][:, MAIN:], -1.0)
                        do(dve.tensor_scalar(item[k][:, :], pos[k][:, :], 1.0 / W, -0.496, ALU.mult, ALU.add))
                        do(dve.tensor_scalar(item[k][:, :], item[k][:, :], MAGIC, MAGIC, ALU.add, ALU.subtract))
                        do(dve.scalar_tensor_tensor(pos[k][:, :], item[k][:, :], -float(W), pos[k][:, :], ALU.mult, ALU.add))

                    def place(n, lo, width):
                        def body(s, q, on, quiet):
                            wait(dve, placed, n * CH + s - NRING + 1 if n else s - NRING + 1)
                            at = bass.ds(s, 1)
                            for k in KEYS:
                                for w, pay in enumerate((low[k], high[k])):
                                    dve.tensor_scalar(in_slot[k][:, q, w, :], iota_h[0:EP, 0:W], pos[k][:, at], pay[:, at],
                                                      ALU.is_equal, ALU.mult)
                                last = dve.tensor_scalar(in_item[k][:, q, 0:width], iota_h[0:EP, lo:lo + width], item[k][:, at],
                                                         None, ALU.is_equal)
                            last.then_inc(hot_ready, 1)
                        turns(dve, 0, CH, 0, body)
                        dve.wait_ge(placed, (n + 1) * CH)
                        for i, k in enumerate(KEYS):
                            t = tab[k]
                            o = t["other"][:, lo:lo + width]
                            l = t["local"][:, lo:lo + width]
                            a, b, used, hi = v1[:, 0:width], v2[:, 0:width], v3[:, 0:width], v4[:, 0:width]
                            do(dve.tensor_copy(a, plane[k][0][:, 0:width]))
                            do(dve.tensor_copy(b, plane[k][1][:, 0:width]))
                            do(dve.tensor_scalar(used, a, 0.0, None, ALU.is_gt))
                            do(dve.tensor_scalar(b, b, NT / 2.0 * HI, None, ALU.add))
                            do(dve.tensor_scalar(hi, b, 1.0 / HI, -0.48, ALU.mult, ALU.add))
                            do(dve.tensor_scalar(hi, hi, MAGIC, MAGIC, ALU.add, ALU.subtract))
                            do(dve.scalar_tensor_tensor(b, hi, -float(HI), b, ALU.mult, ALU.add))
                            do(dve.tensor_scalar(hi, hi, 1.0, None, ALU.add))
                            do(dve.tensor_tensor(hi, hi, used, ALU.mult))
                            do(dve.tensor_scalar(l, hi, 1.0, None, ALU.subtract))
                            do(dve.scalar_tensor_tensor(b, b, float(SPLIT), a, ALU.mult, ALU.add))
                            do(dve.tensor_scalar(b, b, 1.0, 0.0, ALU.subtract, ALU.max))
                            do(dve.tensor_copy(o, b))
                        dve.sem_inc(filled, 1)

                    dve.drain()
                    place(0, 0, PLACE)
                    total = {k: dve.value_load(tab[k]["total"][0:1, 0:1], min_val=0, max_val=MAXI) for k in KEYS}
                    with dve.If((total["dst"] > PLACE) | (total["src"] > PLACE)):
                        place(1, PLACE, MAXI - PLACE)
                    with dve.Else():
                        pass

                @block.tensor
                def _(pe):
                    def place(n, width):
                        def chunk(s, q, start, stop):
                            pe.wait_ge(hot_ready, n * CH + s + 1)
                            for k in KEYS:
                                for w in range(2):
                                    last = pe.matmul(plane[k][w][:, 0:width], in_slot[k][:, q, w, :], in_item[k][:, q, 0:width],
                                                     start=start, stop=stop)
                            last.then_inc(placed, 1)
                        turns(pe, 0, CH, 0, lambda s, q, on, quiet: chunk(s, q, isinstance(s, int) and s == 0,
                                                                     isinstance(s, int) and s == CH - 1))
                    place(0, PLACE)
                    total = {k: pe.value_load(tab[k]["total"][0:1, 0:1], min_val=0, max_val=MAXI) for k in KEYS}
                    with pe.If((total["dst"] > PLACE) | (total["src"] > PLACE)):
                        pe.wait_ge(filled, 1)
                        place(1, MAXI - PLACE)
                    with pe.Else():
                        pass
    return tab



def rows_sweep(sp, tab, lag, body, stored, each):
    def either(part, where, r):
        if where == "tail":
            part(None)
            return
        flag = sp.value_load(tab["straight"][0:1, bass.ds(r, 1)] if where == "middle" else tab["straight_head"][0:1, 0:1],
                             min_val=0, max_val=1)
        with sp.If(flag > 0):
            if where == "head":
                assert r <= HEAD
                part(lambda s, q, k: (s - k) * B * NT)
            else:
                lo, hi = 2 * NRING * B * NT, N - NRING * B * NT
                base = sp.value_load(tab["row"][0:1, bass.ds(r * NRING * B, 1)], min_val=lo, max_val=hi)
                part(lambda s, q, k: base + (q - k) * B * NT)
        with sp.Else():
            part(None)

    def run(first, last):
        turns(sp, first, last, lag, body, either if first == 0 else None)
        for q in range(NRING):
            sp.wait_ge(stored[q], each * len(range(q, last, NRING)))
    both_ranges(sp, tab, run)


def own_rows(sp, tab, t, q, pairs, sems, part, store, row):
    sem = sems[q]

    def in_one(row):
        for dram, buf in pairs:
            rows = dram[bass.ds(row, B * NT), :].rearrange("(j n) f -> n j f", n=NT)
            src, dst = (buf, rows) if store else (rows, buf)
            sp.dma_start(dst, src).then_inc(sem, 16)

    if row is not None:
        in_one(row)
        return
    plain = sp.value_load(tab["plain"][0:1, bass.ds(t, 1)], min_val=0, max_val=1)
    with sp.If(plain > 0):
        in_one(sp.value_load(tab["row"][0:1, bass.ds(t * B, 1)], min_val=0, max_val=N - B * NT))
    with sp.Else():
        wait(sp, sem, 16 * len(pairs) * (lap(t) - 1))
        for j in range(B):
            last = sp.value_load(tab["last"][0:1, bass.ds(t * B + j, 1)], min_val=0, max_val=1) if store else 1
            row = sp.value_load(tab["row"][0:1, bass.ds(t * B + j, 1)], min_val=0, max_val=N - NT)

            def move():
                for dram, buf in pairs:
                    src, dst = dram[bass.ds(row, NT), :], buf[:, j, :]
                    src, dst = (dst, src) if store else (src, dst)
                    sp.dma_start(dst, src).then_inc(part, 16)
            if store:
                with sp.If(last > 0):
                    move()
                with sp.Else():
                    sp.sem_inc(part, 16 * len(pairs))
            else:
                move()
        sp.wait_ge(part, 16 * B * len(pairs))
        sp.sem_clear(part)
        sp.sem_inc(sem, 16 * len(pairs))


def gather_rows(pool, tab, t, q, table, idx, rows, width, idx_ready, gathered, free, free_at, ready):
    par = q % 2
    wait(pool, gathered[(q - 2) % NRING], 16 * B * lap(t - 2))
    pool.tensor_copy(idx[:, par, :], tab["other"][:, bass.ds(t * B, B)]).then_inc(idx_ready, 1)
    wait(pool, free, free_at)
    pool.wait_ge(idx_ready, t + 1)
    pool.sem_inc(ready, 1)
    for j in range(B):
        pool.indirect_dma_start(rows[:, q, j, 0:width], None, table,
                                bass.IndirectOffsetOnAxis(idx[:, par, j:j + 1], 0)).then_inc(gathered[q], 16)


def one_hot(dve, const, tab, t, out):
    return dve.tensor_tensor(out, const["iota"][:, :].unsqueeze(1).broadcast_to([W, B, NT]),
                             tab["local"][:, bass.ds(t * B, B)].unsqueeze(2).broadcast_to([W, B, NT]), ALU.is_equal)


def if_set(eng, flags, t, then):
    flag = eng.value_load(flags[0:1, bass.ds(t, 1)], min_val=0, max_val=1)
    with eng.If(flag > 0):
        then()
    with eng.Else():
        pass


def mark_firsts(dve, const, tab, t, out, used, used_at, quiet):
    def build():
        wait(dve, used, used_at)
        dve.tensor_tensor(out, const["eye"][0:NT, 0:NT].unsqueeze(1).broadcast_to([NT, B, NT]),
                          tab["first"][0:NT, bass.ds(t * B, B)].unsqueeze(2).broadcast_to([NT, B, NT]), ALU.mult)
        dve.drain()
    if not quiet:
        if_set(dve, tab["again"], t, build)


def pass_on(dve, tab, t, acc, q, keep, quiet):
    def add():
        dve.tensor_copy(keep, tab["keep"][:keep.shape[0], bass.ds(t * B, B)])
        dve.drain()
        for j in range(B):
            before = acc[:, q, j - 1] if j else acc[:, (q - 1) % NRING, B - 1]
            dve.scalar_tensor_tensor(acc[:, q, j], before, keep[:, j:j + 1], acc[:, q, j], ALU.mult, ALU.add)
            dve.drain()
    if not quiet:
        if_set(dve, tab["carry"], t, add)


def norm_stats(dve, settled, c, u, stats, mv):
    for j in range(B):
        last = dve.bn_stats(stats[:, j, :], u[:, j, :])
    c.mark(last)
    waits_apart(dve, settled, [(c.sem, c.base + c.n)])
    for j in range(B):
        last = dve.bn_aggr(mv[:, j, :], stats[:, j, :])
    return last


def rstd(act, var, logs, out, eps, log_step, t):
    act.activation(logs, var, ACT.Ln, bias=eps).then_inc(log_step, 1)
    act.wait_ge(log_step, t + 1)
    return act.activation(out, logs, ACT.Exp, scale=-0.5)


def normalise(dve, c, u, mv, rs, shift, out):
    c.mark(dve.scalar_tensor_tensor(shift, mv[:, :, 0], -1.0, rs, ALU.mult, ALU.mult))
    c.sync()
    for j in range(B):
        last = dve.tensor_scalar(out[:, j, :], u[:, j, :], rs[:, j:j + 1], shift[:, j:j + 1], ALU.mult, ALU.add)
    return last


def col(v):
    return v.rearrange("(p a) -> p a", a=1)


def row(v):
    return v.rearrange("(a p) -> a p", a=1)



def load_weights(nc, keep, ins, const):
    w = {n: keep.sb(n, [D, D]) for n in ("L0_gnn_W1", "L0_gnn_W4", "L1_gnn_W1", "L1_gnn_W2", "L3_gnn_Wo")}
    w["W2"] = keep.sb("W2", [D, 1])
    w["b1"] = keep.sb("b1", [D, 1])
    w["neg_b2"] = keep.sb("neg_b2", [W, 1])
    w["gat"] = keep.sb("gat", [D, D + 2 * HEADS])
    w["qv"] = keep.sb("qv", [D, 2 * D])
    rows = ("L1_gnn_b1", "L1_gnn_b2", "L2_gnn_bias", "L3_gnn_bo", "L3_gnn_gamma", "L3_gnn_beta")
    for n in rows:
        w["row_" + n] = keep.sb("row_" + n, [128, D])
    parts = ("L0_gnn_b4", "L3_gnn_bqk", "L3_gnn_bv")
    w["parts"] = keep.sb("parts", [3, len(parts) * D], BF16)
    w["ones3"] = keep.sb("ones3", [3, NT], BF16)
    w["eps"] = keep.sb("eps", [128, 1])
    with ExitStack() as ctx:
        p = Mem(nc, ctx, "load")
        att = p.sb("att", [128, HEADS, 2 * HC])
        prod = p.sb("prod", [D, 2, D])
        full = p.sb("full", [1, len(parts) * D])
        left = p.sb("left", [1, len(parts) * D])
        piece = p.sb("piece", [1, 3, len(parts) * D], BF16)
        loaded, step, split, spread = p.sem("loaded"), p.sem("vector_step"), p.sem("split"), p.sem("spread")
        with nc.Block() as block:

            @block.sync
            def _(sp):
                loads = [(w[n][:, :], ins[n]) for n in ("L0_gnn_W1", "L0_gnn_W4", "L1_gnn_W1", "L1_gnn_W2", "L3_gnn_Wo")]
                loads += [(w["W2"][:, :], ins["L0_gnn_W2"]), (w["b1"][:, :], col(ins["L0_gnn_b1"])),
                          (w["neg_b2"][:, :], row(ins["L0_gnn_b2"]).broadcast_to([W, 1])),
                          (w["gat"][:, 0:D], ins["L2_gnn_weight"]), (w["qv"][:, 0:D], ins["L3_gnn_Wqk"]),
                          (w["qv"][:, D:], ins["L3_gnn_Wv"]),
                          (att[:, :, :], ins["L2_gnn_att"].broadcast_to([128, HEADS, 2 * HC]))]
                loads += [(w["row_" + n][:, :], row(ins[n]).broadcast_to([128, D])) for n in rows]
                loads += [(full[:, i * D:(i + 1) * D], row(ins[n])) for i, n in enumerate(parts)]
                for dst, src in loads:
                    sp.dma_start(dst, src).then_inc(loaded, 16)
                sp.wait_ge(split, 1)
                for i in range(3):
                    sp.dma_start(w["parts"][i:i + 1, :], piece[:, i, :]).then_inc(spread, 16)
                sp.wait_ge(spread, 48)
                sp.wait_ge(loaded, 16 * len(loads))

            @block.vector
            def _(dve):
                c = Steps(dve, step, 10 ** 6)
                c.begin(0)

                def do(ins_):
                    c.mark(ins_)
                    c.sync()
                dve.memset(w["ones3"][:, :], 1.0)
                dve.memset(w["eps"][:, :], EPS)
                dve.wait_ge(loaded, 16 * 21)
                do(dve.tensor_scalar(w["neg_b2"][:, :], w["neg_b2"][:, :], -1.0, None, ALU.mult))
                wt = w["gat"][:, 0:D].rearrange("p (h c) -> p h c", h=HEADS)
                for i, half in enumerate((slice(HC, 2 * HC), slice(0, HC))):
                    pr = prod[:, i, :].rearrange("p (h c) -> p h c", h=HEADS)
                    do(dve.tensor_tensor(pr, wt, att[:, :, half], ALU.mult))
                    do(dve.tensor_reduce(w["gat"][:, D + i * HEADS:D + (i + 1) * HEADS], pr, AX.X, ALU.add))
                do(dve.tensor_copy(piece[:, 0, :], full[:, :]))
                do(dve.tensor_tensor(left[:, :], full[:, :], piece[:, 0, :], ALU.subtract))
                do(dve.tensor_copy(piece[:, 1, :], left[:, :]))
                do(dve.tensor_tensor(left[:, :], left[:, :], piece[:, 1, :], ALU.subtract))
                dve.tensor_copy(piece[:, 2, :], left[:, :]).then_inc(split, 1)
    return w



def gated_layer(nc, tab, const, w, dis, x, x1, y1):
    with ExitStack() as ctx:
        m = Mem(nc, ctx, "l0")
        idx = m.sb("idx", [W, 2, B], I32)
        G = m.sb("gathered", [W, NRING, B, D + 1])
        X = m.sb("own", [NT, NRING, B, D])
        S = m.sb("one_hot", [W, NRING, B, NT])
        ST = m.sb("one_hot_T", [NT, 2, B, W])
        XT = m.sb("own_T", [D, NRING, B, NT])
        TH = m.sb("theta_T", [D, 2, B * W])
        R = m.sb("hidden_T", [D, 2, B * W])
        EX = m.sb("exp_logit", [W, 2, B])
        WE = m.sb("edge_weight", [W, 2, B])
        SW = m.sb("weighted_one_hot", [W, 2, B, NT])
        A = m.sb("sums", [NT, NRING, B, D + 2])
        W1 = m.sb("weight_sum_plus_1", [NT, B])
        V = m.sb("partial", [NT, B, D])
        U = m.sb("summed", [NT, 2, B, D])
        stats = m.sb("stats", [NT, B, 6])
        mv = m.sb("mean_var", [NT, 2, 2, B, 2])
        lg = m.sb("logs", [NT, 2, B])
        rs = m.sb("rstd", [NT, 2, 2, B])
        shift = m.sb("shift", [NT, B])
        keep4 = m.sb("keep4", [NT, B])
        X1 = m.sb("x1", [NT, NRING, B, D])
        Y1 = m.sb("y1", [NT, 2, B, D])
        pST = m.ps("one_hot_T", [NT, B, W])
        pX = m.ps("own_T", [D, B, NT])
        pTH = m.ps("theta_T", [D, B, W])
        pH = m.ps("hidden_T", [D, B * W])
        pZ = m.ps("logit", [W, B])
        pA = m.ps("sums", [NT, B, 256])
        pW = m.ps("x_W4", [NT, B, D])
        ready, passed, sp_passed = m.sem("constants_set"), m.sem("waits_passed"), m.sem("sync_waits_passed")
        own, idx_ready, gathered = m.sems("own_loaded"), m.sem("indices_ready"), m.sems("gathered")
        s_ready, st_made, st_ready = m.sem("one_hot_ready"), m.sem("one_hot_T_made"), m.sem("one_hot_T_ready")
        xt_made, xt_ready = m.sem("own_T_made"), m.sem("own_T_ready")
        th_made, th_ready = m.sem("theta_made"), m.sem("theta_ready")
        h_made, h_ready = m.sem("hidden_made"), m.sem("hidden_ready")
        z_made, e_ready, w_step, sw_ready = m.sem("logit_made"), m.sem("exp_ready"), m.sem("weight_step"), m.sem("weighted_ready")
        a_made, a_ready, w4_made, u_step, u_ready = (m.sem("sums_made"), m.sem("sums_ready"), m.sem("x_W4_made"),
                                                     m.sem("epilogue_step"), m.sem("summed_ready"))
        log_step, rs_ready, n_step, x1_ready, y1_ready = (m.sem("log_step"), m.sem("rstd_ready"), m.sem("normalise_step"),
                                                          m.sem("x1_ready"), m.sem("y1_ready"))
        stored, part, stat_step = m.sems("stored"), m.sem("tiles_moved"), m.sem("stat_step")
        with nc.Block() as block:

            @block.sync
            def _(sp):
                def body(s, q, on, rows):
                    if on(0):
                        waits_apart(sp, sp_passed, [(u_ready, s - 3)])
                        own_rows(sp, tab, s, q, [(x, X[:, q])], own, part, False, rows and rows(s, q, 0))
                    if on(7):
                        t, tq = s - 7, (q - 7) % NRING
                        waits_apart(sp, sp_passed, [(x1_ready, t + 1), (y1_ready, t + 1)])
                        own_rows(sp, tab, t, tq, [(x1, X1[:, tq]), (y1, Y1[:, tq % 2])], stored, part, True, rows and rows(s, q, 7))
                rows_sweep(sp, tab, 7, body, stored, 32)

            @block.gpsimd
            def _(pool):
                def body(s, q, on, quiet):
                    gather_rows(pool, tab, s, q, x, idx, G, D, idx_ready, gathered, a_made, s - 3, passed)
                sweep(pool, tab, 0, body)

            @block.vector
            def _(dve):
                wstep, ustep, nstep = Steps(dve, w_step, 2), Steps(dve, u_step, 3), Steps(dve, n_step, 1)
                dve.memset(mv[:, :, :, :, :], 1.0)
                dve.memset(A[:, NRING - 1, B - 1, :], 0.0)
                dve.memset(G[:, :, :, D:D + 1], 1.0).then_inc(ready, 1)
                dve.wait_ge(ready, 1)

                def body(s, q, on, quiet):
                    if on(0):
                        wait(dve, a_made, s - 3)
                        one_hot(dve, const, tab, s, S[:, q]).then_inc(s_ready, 1)
                    if on(4):
                        t, r, rq = s - 4, q % 2, q
                        dve.wait_ge(a_ready, t + 1)
                        wait(dve, x1_ready, t - 1)
                        wait(dve, u_ready, t)
                        pass_on(dve, tab, t, A, rq, keep4[:, :], quiet)
                        ustep.begin(t)
                        dve.tensor_scalar(mv[:, r, 1, :, 1], A[:, rq, :, D + 1], 1.0, None, ALU.add)
                        ustep.mark(dve.tensor_scalar(W1[:, :], A[:, rq, :, D], 1.0, None, ALU.add))
                        ustep.sync()
                        for j in range(B):
                            last = dve.scalar_tensor_tensor(V[:, j, :], X[:, rq, j, :], W1[:, j:j + 1], A[:, rq, j, 0:D],
                                                            ALU.mult, ALU.subtract)
                        ustep.mark(last)
                        dve.wait_ge(w4_made, t + 1)
                        ustep.sync()
                        for j in range(B):
                            last = dve.scalar_tensor_tensor(U[:, r, j, :], pW[:, j, :], A[:, rq, j, D + 1:D + 2], V[:, j, :],
                                                            ALU.mult, ALU.add)
                        ustep.mark(last)
                        ustep.sync()
                        ustep.end()
                        sstep = Steps(dve, stat_step, 1)
                        sstep.begin(t)
                        norm_stats(dve, ready, sstep, U[:, r], stats, mv[:, r, 0]).then_inc(u_ready, 1)
                    if on(5):
                        t, r, tq = s - 5, (q - 5) % 2, (q - 5) % NRING
                        dve.wait_ge(rs_ready, t + 1)
                        wait(dve, stored[tq], 32 * (lap(t) - 1))
                        wait(dve, x1_ready, t)
                        nstep.begin(t)
                        dve.tensor_copy(dis[:, bass.ds(t * B, B)], rs[:, r, 1])
                        normalise(dve, nstep, U[:, r], mv[:, r, 0], rs[:, r, 0], shift[:, :], X1[:, tq]).then_inc(x1_ready, 1)
                        nstep.end()
                    if on(2):
                        t, r, rq = s - 2, q % 2, (q - 2) % NRING
                        dve.wait_ge(e_ready, t + 1)
                        wait(dve, a_made, t - 1)
                        wstep.begin(t)
                        wstep.mark(dve.tensor_scalar(EX[:, r], EX[:, r], 1.0, None, ALU.add))
                        wstep.sync()
                        wstep.mark(dve.reciprocal(WE[:, r], EX[:, r]))
                        wstep.sync()
                        wstep.end()
                        dve.tensor_tensor(SW[:, r], S[:, rq], WE[:, r].unsqueeze(2).broadcast_to([W, B, NT]),
                                          ALU.mult).then_inc(sw_ready, 1)
                quiet_sweep(dve, tab, 5, body)

            @block.scalar
            def _(act):
                act.preload_act_table_set(TABLES)

                def body(s, q, on, quiet):
                    if on(6):
                        t, r, tq = s - 6, q % 2, (q - 6) % NRING
                        act.wait_ge(x1_ready, t + 1)
                        wait(act, stored[tq - 2], 32 * lap(t - 2))
                        for j in range(B):
                            last = act.activation(Y1[:, r, j, :], X1[:, tq, j, :], ACT.Copy, scale=rs[:, r, 1, j:j + 1])
                        last.then_inc(y1_ready, 1)
                    if on(1):
                        t, r = s - 1, (q - 1) % 2
                        act.wait_ge(st_made, t + 1)
                        wait(act, th_made, t - 1)
                        act.activation(ST[:, r], pST[:, :, :], ACT.Copy).then_inc(st_ready, 1)
                    if on(2):
                        t, r = s - 2, q % 2
                        act.wait_ge(h_made, t + 1)
                        wait(act, z_made, t - 1)
                        act.activation(R[:, r], pH[:, :], ACT.Relu, bias=w["b1"][:, :]).then_inc(h_ready, 1)
                    if on(5):
                        t, r = s - 5, (q - 5) % 2
                        act.wait_ge(u_ready, t + 1)
                        wait(act, x1_ready, t - 1)
                        wait(act, y1_ready, t - 1)
                        wait(act, rs_ready, t)
                        act.activation(lg[:, 0], mv[:, r, 0, :, 1], ACT.Ln, bias=w["eps"][0:NT, :])
                        act.activation(lg[:, 1], mv[:, r, 1, :, 1], ACT.Ln).then_inc(log_step, 1)
                        act.wait_ge(log_step, t + 1)
                        act.activation(rs[:, r], lg[:, :, :], ACT.Exp, scale=-0.5).then_inc(rs_ready, 1)
                    if on(3):
                        t, tq = s - 3, (q - 3) % NRING
                        act.wait_ge(a_made, t + 1)
                        wait(act, u_ready, t - 2)
                        act.activation(A[:, tq], pA[:, :, 0:D + 2], ACT.Copy).then_inc(a_ready, 1)
                    if on(2):
                        t, r = s - 2, q % 2
                        act.wait_ge(z_made, t + 1)
                        wait(act, sw_ready, t - 1)
                        act.activation(EX[:, r], pZ[:, :], ACT.Exp, bias=w["neg_b2"][:, :], scale=-1.0).then_inc(e_ready, 1)
                    if on(1):
                        t, r = s - 1, (q - 1) % 2
                        act.wait_ge(th_made, t + 1)
                        wait(act, h_made, t - 1)
                        act.activation(TH[:, r], pTH[:, :, :], ACT.Copy).then_inc(th_ready, 1)
                    if on(2):
                        t, tq = s - 2, (q - 2) % NRING
                        act.wait_ge(xt_made, t + 1)
                        wait(act, w4_made, t - 3)
                        act.activation(XT[:, tq], pX[:, :, :], ACT.Copy).then_inc(xt_ready, 1)
                sweep(act, tab, 6, body)

            @block.tensor
            def _(pe):
                eye, neg_eye = const["eye"], const["neg_eye"]
                b4 = w["parts"][:, 0:D].unsqueeze(1).broadcast_to([3, B, D])

                def body(s, q, on, quiet):
                    if on(1):
                        t, tq = s - 1, (q - 1) % NRING
                        pe.wait_ge(s_ready, t + 1)
                        wait(pe, st_ready, t)
                        for j in range(B):
                            last = pe.transpose(pST[:, j, :], S[:, tq, j, :], eye[:, :])
                        last.then_inc(st_made, 1)
                    if on(2):
                        t, r = s - 2, q % 2
                        pe.wait_ge(th_ready, t + 1)
                        wait(pe, h_ready, t)
                        pe.matmul(pH[:, :], w["L0_gnn_W1"][:, :], TH[:, r], start=True, stop=True).then_inc(h_made, 1)
                    if on(3):
                        t, r, tq = s - 3, (q - 3) % 2, (q - 3) % NRING
                        pe.wait_ge(xt_ready, t + 1)
                        wait(pe, u_ready, t)
                        pe.matmul(pW[:, :, :], w["ones3"][:, :], b4, start=True, stop=False)
                        for j in range(B):
                            last = pe.matmul(pW[:, j, :], XT[:, tq, j, :], w["L0_gnn_W4"][:, :], start=False, stop=(j == B - 1))
                        last.then_inc(w4_made, 1)
                        pe.wait_ge(sw_ready, t + 1)
                        wait(pe, a_ready, t)
                        for j in range(B):
                            pe.matmul(pA[:, j, 0:D + 1], SW[:, r, j, :], G[:, tq, j, :], start=True, stop=True)
                            last = pe.matmul(pA[:, j, D + 1:D + 2], S[:, tq, j, :], G[:, tq, j, D:D + 1], start=True, stop=True)
                        last.then_inc(a_made, 1)
                    if on(2):
                        t, r = s - 2, q % 2
                        pe.wait_ge(h_ready, t + 1)
                        wait(pe, e_ready, t)
                        for j in range(B):
                            last = pe.matmul(pZ[:, j:j + 1], R[:, r, j * W:(j + 1) * W], w["W2"][:, :], start=True, stop=True)
                        last.then_inc(z_made, 1)
                    if on(1):
                        t, r, tq = s - 1, (q - 1) % 2, (q - 1) % NRING
                        pe.wait_ge(st_ready, t + 1)
                        pe.wait_ge(own[tq], 16 * lap(t))
                        pe.wait_ge(gathered[tq], 16 * B * lap(t))
                        wait(pe, th_ready, t)
                        for j in range(B):
                            pe.matmul(pTH[:, j, :], X[:, tq, j, :], ST[:, r, j, :], start=True, stop=False)
                            last = pe.matmul(pTH[:, j, :], G[:, tq, j, 0:D], neg_eye[:, :], start=False, stop=True)
                        last.then_inc(th_made, 1)
                    if on(2):
                        t, tq = s - 2, (q - 2) % NRING
                        wait(pe, xt_ready, t)
                        for j in range(B):
                            last = pe.transpose(pX[:, j, :], X[:, tq, j, :], eye[0:NT, 0:NT])
                        last.then_inc(xt_made, 1)
                sweep(pe, tab, 3, body)



def convolution(nc, tab, const, w, dis, tag, weight, bias, y_in, y_out=None, x_in=None, x_out=None, gat=None):
    second = x_in is not None
    HW = D + 2 * HEADS
    with ExitStack() as ctx:
        m = Mem(nc, ctx, tag)
        idx = m.sb("idx", [W, 2, B], I32)
        G = m.sb("gathered", [W, NRING, B, D])
        Y = m.sb("own", [NT, NRING, B, D])
        S = m.sb("one_hot", [W, NRING, B, NT])
        F = m.sb("firsts", [NT, 2, B, NT])
        AT = m.sb("sums_T", [D, NRING, B, NT])
        dl = m.sb("dis", [NT, NRING, B])
        keep4 = m.sb("keep4", [D, B])
        T = m.sb("before_relu", [NT, 2, B, D])
        O = m.sb("out", [NT, NRING, B, D])
        pT = m.ps("sums_T", [D, B, NT])
        pZ = m.ps("product", [NT, B, D])
        ready, passed, sp_passed = m.sem("constants_set"), m.sem("waits_passed"), m.sem("sync_waits_passed")
        own, idx_ready, gathered = m.sems("own_loaded"), m.sem("indices_ready"), m.sems("gathered")
        s_ready, t_made, t_copied, t_ready = (m.sem("one_hot_ready"), m.sem("sums_made"), m.sem("sums_copied"),
                                              m.sem("sums_ready"))
        z_made, b_ready, o_ready = m.sem("product_made"), m.sem("biased_ready"), m.sem("out_ready")
        d_ready, stored, part = m.sem("dis_ready"), m.sems("stored"), m.sem("tiles_moved")
        if second:
            X = m.sb("own_x", [NT, NRING, B, D])
            U = m.sb("summed", [NT, 2, B, D])
            stats = m.sb("stats", [NT, B, 6])
            mv = m.sb("mean_var", [NT, 2, B, 2])
            lg = m.sb("logs", [NT, B])
            rs = m.sb("rstd", [NT, 2, B])
            shift = m.sb("shift", [NT, B])
            OT = m.sb("out_T", [D, 2, B, NT])
            H = m.sb("gat_rows", [NT, 2, B, HW])
            pOT = m.ps("out_T", [D, B, NT])
            pH = m.ps("gat_rows", [NT, B, 256])
            own_x = m.sems("own_x_loaded")
            u_step, u_ready, log_step, rs_ready, n_step = (m.sem("summed_step"), m.sem("summed_ready"), m.sem("log_step"),
                                                           m.sem("rstd_ready"), m.sem("normalise_step"))
            ot_made, ot_ready, h_made, h_ready = (m.sem("out_T_made"), m.sem("out_T_ready"), m.sem("gat_made"),
                                                  m.sem("gat_ready"))
        with nc.Block() as block:

            @block.sync
            def _(sp):
                def body(s, q, on, rows):
                    if on(0):
                        waits_apart(sp, sp_passed, [(t_made, s - 3)])
                        own_rows(sp, tab, s, q, [(y_in, Y[:, q])], own, part, False, rows and rows(s, q, 0))
                        if second:
                            waits_apart(sp, sp_passed, [(u_ready, s - 3)])
                            own_rows(sp, tab, s, q, [(x_in, X[:, q])], own_x, part, False, rows and rows(s, q, 0))
                    if second and on(7):
                        t, tq = s - 7, (q - 7) % NRING
                        waits_apart(sp, sp_passed, [(o_ready, t + 1), (h_ready, t + 1)])
                        own_rows(sp, tab, t, tq, [(x_out, O[:, tq]), (gat, H[:, tq % 2])], stored, part, True, rows and rows(s, q, 7))
                    if not second and on(5):
                        t, tq = s - 5, (q - 5) % NRING
                        waits_apart(sp, sp_passed, [(o_ready, t + 1)])
                        own_rows(sp, tab, t, tq, [(y_out, O[:, tq])], stored, part, True, rows and rows(s, q, 5))
                rows_sweep(sp, tab, 7 if second else 5, body, stored, 32 if second else 16)

            @block.gpsimd
            def _(pool):
                def body(s, q, on, quiet):
                    gather_rows(pool, tab, s, q, y_in, idx, G, D, idx_ready, gathered, t_made, s - 3, passed)
                sweep(pool, tab, 0, body)

            @block.vector
            def _(dve):
                dve.memset(AT[:, NRING - 1, B - 1, :], 0.0)
                dve.tensor_copy(F[:, 0], const["eye"][0:NT, 0:NT].unsqueeze(1).broadcast_to([NT, B, NT]))
                dve.tensor_copy(F[:, 1], const["eye"][0:NT, 0:NT].unsqueeze(1).broadcast_to([NT, B, NT])).then_inc(ready, 1)
                dve.wait_ge(ready, 1)

                def body(s, q, on, quiet):
                    if on(0):
                        mark_firsts(dve, const, tab, s, F[:, q % 2], t_made, s - 1, quiet)
                        wait(dve, t_made, s - 3)
                        one_hot(dve, const, tab, s, S[:, q]).then_inc(s_ready, 1)
                    if on(2):
                        t, tq = s - 2, (q - 2) % NRING
                        wait(dve, b_ready, t - 3)
                        dve.tensor_copy(dl[:, tq], dis[:, bass.ds(t * B, B)]).then_inc(d_ready, 1)
                        dve.wait_ge(t_copied, t + 1)
                        if quiet:
                            dve.sem_inc(t_ready, 1)
                        else:
                            pass_on(dve, tab, t, AT, tq, keep4[:, :], quiet)
                            dve.sem_inc(t_ready, 1)
                    if on(3):
                        t, r, tq = s - 3, (q - 3) % 2, (q - 3) % NRING
                        dve.wait_ge(z_made, t + 1)
                        dve.wait_ge(d_ready, t + 1)
                        wait(dve, u_ready if second else o_ready, t - 1)
                        for j in range(B):
                            last = dve.scalar_tensor_tensor(T[:, r, j, :], pZ[:, j, :], dl[:, tq, j:j + 1],
                                                            w["row_" + bias][0:NT, :], ALU.mult, ALU.add)
                        last.then_inc(b_ready, 1)
                        if second:
                            ustep = Steps(dve, u_step, 2)
                            ustep.begin(t)
                            dve.wait_ge(b_ready, t + 1)
                            dve.wait_ge(own_x[tq], 16 * lap(t))
                            wait(dve, o_ready, t - 1)
                            wait(dve, u_ready, t)
                            ustep.mark(dve.scalar_tensor_tensor(U[:, r], T[:, r], 0.0, X[:, tq], ALU.max, ALU.add))
                            ustep.sync()
                            norm_stats(dve, ready, ustep, U[:, r], stats, mv[:, r]).then_inc(u_ready, 1)
                            ustep.end()
                    if second and on(4):
                        t, r, tq = s - 4, q % 2, q
                        dve.wait_ge(rs_ready, t + 1)
                        wait(dve, stored[tq], 32 * (lap(t) - 1))
                        wait(dve, ot_made, t - 3)
                        wait(dve, o_ready, t)
                        nstep = Steps(dve, n_step, 1)
                        nstep.begin(t)
                        normalise(dve, nstep, U[:, r], mv[:, r], rs[:, r], shift[:, :], O[:, tq]).then_inc(o_ready, 1)
                quiet_sweep(dve, tab, 4 if second else 3, body)

            @block.scalar
            def _(act):
                act.preload_act_table_set(TABLES)

                def body(s, q, on, quiet):
                    if second and on(4):
                        t, r = s - 4, q % 2
                        act.wait_ge(u_ready, t + 1)
                        wait(act, o_ready, t - 1)
                        wait(act, rs_ready, t)
                        rstd(act, mv[:, r, :, 1], lg[:, :], rs[:, r], w["eps"][0:NT, :], log_step, t).then_inc(rs_ready, 1)
                    if second and on(6):
                        t, r, tq = s - 6, q % 2, (q - 6) % NRING
                        act.wait_ge(h_made, t + 1)
                        wait(act, stored[tq - 2], 32 * lap(t - 2))
                        act.activation(H[:, r], pH[:, :, 0:HW], ACT.Copy).then_inc(h_ready, 1)
                    if second and on(5):
                        t, r = s - 5, (q - 5) % 2
                        act.wait_ge(ot_made, t + 1)
                        wait(act, h_made, t - 1)
                        act.activation(OT[:, r], pOT[:, :, :], ACT.Copy).then_inc(ot_ready, 1)
                    if not second and on(4):
                        t, r, tq = s - 4, q % 2, q
                        act.wait_ge(b_ready, t + 1)
                        wait(act, stored[tq], 16 * (lap(t) - 1))
                        for j in range(B):
                            last = act.activation(O[:, tq, j, :], T[:, r, j, :], ACT.Relu, scale=dl[:, tq, j:j + 1])
                        last.then_inc(o_ready, 1)
                    if on(1):
                        t, tq = s - 1, (q - 1) % NRING
                        act.wait_ge(t_made, t + 1)
                        wait(act, z_made, t - 3)
                        wait(act, t_ready, t - 2)
                        act.activation(AT[:, tq], pT[:, :, :], ACT.Copy).then_inc(t_copied, 1)
                sweep(act, tab, 6 if second else 4, body)

            @block.tensor
            def _(pe):
                def body(s, q, on, quiet):
                    if on(3):
                        t, tq = s - 3, (q - 3) % NRING
                        pe.wait_ge(t_ready, t + 1)
                        wait(pe, b_ready, t)
                        for j in range(B):
                            last = pe.matmul(pZ[:, j, :], AT[:, tq, j, :], w[weight][:, :], start=True, stop=True)
                        last.then_inc(z_made, 1)
                    if second and on(6):
                        t, r = s - 6, q % 2
                        pe.wait_ge(ot_ready, t + 1)
                        wait(pe, h_ready, t)
                        for j in range(B):
                            last = pe.matmul(pH[:, j, 0:HW], OT[:, r, j, :], w["gat"][:, :], start=True, stop=True)
                        last.then_inc(h_made, 1)
                    if second and on(5):
                        t, tq = s - 5, (q - 5) % NRING
                        pe.wait_ge(o_ready, t + 1)
                        wait(pe, ot_ready, t)
                        for j in range(B):
                            last = pe.transpose(pOT[:, j, :], O[:, tq, j, :], const["eye"][0:NT, 0:NT])
                        last.then_inc(ot_made, 1)
                    if on(1):
                        t, r, tq = s - 1, (q - 1) % 2, (q - 1) % NRING
                        pe.wait_ge(s_ready, t + 1)
                        pe.wait_ge(own[tq], 16 * lap(t))
                        pe.wait_ge(gathered[tq], 16 * B * lap(t))
                        wait(pe, t_copied, t)
                        for j in range(B):
                            pe.matmul(pT[:, j, :], G[:, tq, j, :], S[:, tq, j, :], start=True, stop=False)
                            last = pe.matmul(pT[:, j, :], Y[:, tq, j, :], F[:, r, j, :], start=False, stop=True)
                        last.then_inc(t_made, 1)
                sweep(pe, tab, 6 if second else 3, body)



def leaky(dve, out, in_):
    return dve.scalar_tensor_tensor(out, in_, 0.2, in_, ALU.mult, ALU.max)


def by_head(rows):
    return rows.rearrange("p j (h c) -> p j h c", h=HEADS)


def per_channel(heads, parts):
    return heads.unsqueeze(3).broadcast_to([parts, B, HEADS, HC])


def gat_layer(nc, tab, const, w, h_rows, x2, x3_out, qv_out):
    HW = D + 2 * HEADS
    RW = D + HEADS
    with ExitStack() as ctx:
        m = Mem(nc, ctx, "gat")
        idx = m.sb("idx", [W, 2, B], I32)
        G = m.sb("gathered", [W, NRING, B, HW])
        H = m.sb("own", [NT, NRING, B, HW])
        X = m.sb("own_x", [NT, NRING, B, D])
        S = m.sb("one_hot", [W, NRING, B, NT])
        F = m.sb("firsts", [NT, 2, B, NT])
        ST = m.sb("one_hot_T", [NT, NRING, B, W])
        dif = m.sb("ar_above_own", [W, B, HEADS])
        lin = m.sb("logit_linear", [W, B, HEADS])
        LG = m.sb("logit", [W, 2, B, HEADS])
        arg = m.sb("exp_argument", [W, B, HEADS])
        V = m.sb("values_by_node", [W, B, HEADS, NT])
        TOP = m.sb("top_above_own", [NT, NRING, B, HEADS])
        own_lin = m.sb("own_linear", [NT, B, HEADS])
        own_lg = m.sb("own_logit", [NT, B, HEADS])
        AM = m.sb("logit_max", [NT, NRING, B, HEADS])
        ES = m.sb("own_arguments", [NT, 2, 2, B, HEADS])
        EE = m.sb("own_exp", [NT, NRING, 2, B, HEADS])
        R = m.sb("weighted", [W, 2, B, RW])
        HS = m.sb("own_weighted", [NT, 2, B, RW])
        A = m.sb("sums", [NT, NRING, B, RW])
        tmp = m.sb("before_scaled", [NT, RW])
        den = m.sb("denominator", [NT, B, HEADS])
        T = m.sb("mean_by_head", [NT, B, D])
        U = m.sb("summed", [NT, 2, B, D])
        stats = m.sb("stats", [NT, B, 6])
        mv = m.sb("mean_var", [NT, 2, B, 2])
        lg = m.sb("logs", [NT, B])
        rs = m.sb("rstd", [NT, 2, B])
        shift = m.sb("shift", [NT, B])
        keep4 = m.sb("keep4", [NT, B])
        keep4e = m.sb("keep4_late", [NT, B])
        X3 = m.sb("x3", [NT, NRING, B, D])
        XT = m.sb("x3_T", [D, 2, B, NT])
        QV = m.sb("qv", [NT, 2, B, 2 * D])
        pST = m.ps("one_hot_T", [NT, B, W])
        pL = m.ps("looked_up", [W, 2, 256])
        pV = [m.ps(f"values_T_{i}", [NT, HEADS, W]) for i in range(2)]
        pA = m.ps("sums", [NT, B, 256])
        pXT = m.ps("x3_T", [D, B, NT])
        pQV = m.ps("qv", [NT, 2, 2 * D])
        ready, passed, sp_passed = m.sem("constants_set"), m.sem("waits_passed"), m.sem("sync_waits_passed")
        own, own_x, idx_ready, gathered = (m.sems("own_loaded"), m.sems("own_x_loaded"), m.sem("indices_ready"),
                                           m.sems("gathered"))
        s_ready, st_made, st_ready, l1_made, l2_made = (m.sem("one_hot_ready"), m.sem("one_hot_T_made"),
                                                        m.sem("one_hot_T_ready"), m.sem("centre_looked_up"),
                                                        m.sem("max_looked_up"))
        v_step, v_ready, vt_made, vt_read = m.sem("logit_step"), m.sem("values_ready"), m.sem("values_T_made"), m.sem("values_T_read")
        m_step, am_ready, e_ready = m.sem("max_step"), m.sem("max_ready"), m.sem("own_exp_ready")
        a_step, a_ready, p_ready, r_ready = m.sem("argument_step"), m.sem("argument_ready"), m.sem("exp_ready"), m.sem("weighted_ready")
        pa_made, pa_ready, u_step, u_ready = m.sem("sums_made"), m.sem("sums_ready"), m.sem("summed_step"), m.sem("summed_ready")
        log_step, rs_ready, n_step, x3_ready = m.sem("log_step"), m.sem("rstd_ready"), m.sem("normalise_step"), m.sem("x3_ready")
        xt_made, xt_ready, qv_made, qv_ready = m.sem("x3_T_made"), m.sem("x3_T_ready"), m.sem("qv_made"), m.sem("qv_ready")
        xb_ready, stored, part = m.sem("x_bias_ready"), m.sems("stored"), m.sem("tiles_moved")
        with nc.Block() as block:

            @block.sync
            def _(sp):
                def body(s, q, on, rows):
                    if on(0):
                        waits_apart(sp, sp_passed, [(r_ready, s - 3)])
                        own_rows(sp, tab, s, q, [(h_rows, H[:, q])], own, part, False, rows and rows(s, q, 0))
                    if on(1):
                        t, tq = s - 1, (q - 1) % NRING
                        waits_apart(sp, sp_passed, [(u_ready, t - 3)])
                        own_rows(sp, tab, t, tq, [(x2, X[:, tq])], own_x, part, False, rows and rows(s, q, 1))
                    if on(7):
                        t, tq = s - 7, (q - 7) % NRING
                        waits_apart(sp, sp_passed, [(qv_ready, 2 * t + 2)])
                        own_rows(sp, tab, t, tq, [(x3_out, X3[:, tq]), (qv_out, QV[:, tq % 2])], stored, part, True, rows and rows(s, q, 7))
                rows_sweep(sp, tab, 7, body, stored, 32)

            @block.gpsimd
            def _(pool):
                bias = w["row_L2_gnn_bias"][0:NT, :].unsqueeze(1).broadcast_to([NT, B, D])

                def body(s, q, on, quiet):
                    if on(0):
                        gather_rows(pool, tab, s, q, h_rows, idx, G, HW, idx_ready, gathered, r_ready, s - 3, passed)
                    if on(2):
                        t, tq = s - 2, (q - 2) % NRING
                        pool.wait_ge(own_x[tq], 16 * lap(t))
                        pool.tensor_tensor(X[:, tq], X[:, tq], bias, ALU.add).then_inc(xb_ready, 1)
                sweep(pool, tab, 2, body)

            @block.vector
            def _(dve):
                dve.memset(EE[:, :, :, :, :], 0.0)
                dve.memset(ES[:, :, :, :, :], 0.0)
                for ring in (TOP, AM, A):
                    dve.memset(ring[:, NRING - 1, B - 1, :], 0.0)
                dve.tensor_copy(F[:, 0], const["eye"][0:NT, 0:NT].unsqueeze(1).broadcast_to([NT, B, NT]))
                dve.tensor_copy(F[:, 1], const["eye"][0:NT, 0:NT].unsqueeze(1).broadcast_to([NT, B, NT])).then_inc(ready, 1)
                dve.wait_ge(ready, 1)

                def body(s, q, on, quiet):
                    if on(2):
                        t, r = s - 2, q % 2
                        st = Steps(dve, a_step, 1)
                        st.begin(t)
                        dve.wait_ge(l2_made, t + 1)
                        wait(dve, p_ready, t)
                        st.mark(dve.scalar_tensor_tensor(arg[:, :, :], pL[:, 1, 0:B * HEADS].rearrange("p (j h) -> p j h", j=B),
                                                         -1.0, LG[:, r], ALU.mult, ALU.add))
                        st.sync()
                        dve.tensor_scalar(arg[:, :, :], arg[:, :, :], 0.0, None, ALU.min).then_inc(a_ready, 1)
                    if on(1):
                        t, r, tq = s - 1, (q - 1) % 2, (q - 1) % NRING
                        st = Steps(dve, v_step, 1)
                        st.begin(t)
                        dve.wait_ge(l1_made, t + 1)
                        dve.wait_ge(gathered[tq], 16 * B * lap(t))
                        wait(dve, v_ready, t)
                        looked = pL[:, 0, 0:B * 2 * HEADS].rearrange("p (j h) -> p j h", j=B)
                        dve.tensor_tensor(dif[:, :, :], G[:, tq, :, D:RW], looked[:, :, 0:HEADS], ALU.subtract)
                        st.mark(dve.tensor_tensor(lin[:, :, :], G[:, tq, :, D:RW], looked[:, :, HEADS:], ALU.add))
                        st.sync()
                        leaky(dve, LG[:, r], lin[:, :, :])
                        wait(dve, vt_made, B * t)
                        dve.tensor_tensor(V[:, :, :, :], S[:, tq].unsqueeze(2).broadcast_to([W, B, HEADS, NT]),
                                          dif[:, :, :].unsqueeze(3).broadcast_to([W, B, HEADS, NT]), ALU.mult).then_inc(v_ready, 1)
                    if on(0):
                        wait(dve, pa_made, s - 3)
                        one_hot(dve, const, tab, s, S[:, q]).then_inc(s_ready, 1)
                    if on(5):
                        t, r, tq = s - 5, (q - 5) % 2, (q - 5) % NRING
                        nstep = Steps(dve, n_step, 1)
                        nstep.begin(t)
                        dve.wait_ge(rs_ready, t + 1)
                        wait(dve, stored[tq], 32 * (lap(t) - 1))
                        wait(dve, x3_ready, t)
                        normalise(dve, nstep, U[:, r], mv[:, r], rs[:, r], shift[:, :], X3[:, tq]).then_inc(x3_ready, 1)
                    if on(2):
                        t, r, tq = s - 2, q % 2, (q - 2) % NRING
                        mark_firsts(dve, const, tab, t, F[:, r], pa_made, t - 1, quiet)
                        dve.wait_ge(p_ready, t + 1)
                        dve.wait_ge(e_ready, t + 1)
                        wait(dve, pa_made, t - 1)
                        dve.tensor_tensor(by_head(R[:, r, :, 0:D]), by_head(G[:, tq, :, 0:D]),
                                          per_channel(R[:, r, :, D:], W), ALU.mult)
                        dve.tensor_tensor(by_head(HS[:, r, :, 0:D]), by_head(H[:, tq, :, 0:D]),
                                          per_channel(EE[:, tq, 0], NT), ALU.mult)
                        dve.tensor_copy(HS[:, r, :, D:], EE[:, tq, 0]).then_inc(r_ready, 1)
                    if on(1):
                        t, r, tq = s - 1, (q - 1) % 2, (q - 1) % NRING
                        st = Steps(dve, m_step, 4)
                        st.begin(t)
                        dve.wait_ge(own[tq], 16 * lap(t))
                        wait(dve, am_ready, t)
                        wait(dve, e_ready, t - 1)
                        wait(dve, l2_made, t - 3)
                        st.mark(dve.tensor_tensor(own_lin[:, :, :], H[:, tq, :, D:RW], H[:, tq, :, RW:], ALU.add))
                        st.sync()
                        leaky(dve, own_lg[:, :, :], own_lin[:, :, :])
                        for j in range(B):
                            dve.wait_ge(vt_made, B * t + j + 1)
                            dve.tensor_reduce(TOP[:, tq, j, :], pV[j % 2][:, :, :], AX.X, ALU.max).then_inc(vt_read, 1)
                        dve.wait_ge(vt_read, B * t + B)
                        st.mark(dve.tensor_scalar(TOP[:, tq], TOP[:, tq], 0.0, None, ALU.max))
                        if quiet:
                            st.sync()
                        else:
                            waits_apart(dve, ready, [(m_step, st.base + st.n)])

                        def top_before():
                            dve.tensor_copy(keep4[:, :], tab["keep"][0:NT, bass.ds(t * B, B)])
                            dve.drain()
                            for j in range(B):
                                before = TOP[:, tq, j - 1] if j else TOP[:, (tq - 1) % NRING, B - 1]
                                dve.scalar_tensor_tensor(TOP[:, tq, j], before, keep4[:, j:j + 1], TOP[:, tq, j], ALU.mult, ALU.max)
                                dve.drain()
                        if not quiet:
                            if_set(dve, tab["carry"], t, top_before)
                        st.mark(dve.tensor_tensor(own_lin[:, :, :], own_lin[:, :, :], TOP[:, tq], ALU.add))
                        st.sync()
                        st.mark(leaky(dve, AM[:, tq], own_lin[:, :, :]))
                        if quiet:
                            st.sync()
                        else:
                            waits_apart(dve, ready, [(m_step, st.base + st.n)])

                        def max_before():
                            for j in range(B):
                                before = AM[:, tq, j - 1] if j else AM[:, (tq - 1) % NRING, B - 1]
                                dve.tensor_tensor(ES[:, r, 1, j], before, AM[:, tq, j], ALU.subtract)
                                dve.drain()
                                dve.tensor_scalar(ES[:, r, 1, j], ES[:, r, 1, j], keep4[:, j:j + 1], None, ALU.mult)
                                dve.drain()
                        if not quiet:
                            if_set(dve, tab["carry"], t, max_before)
                        dve.tensor_tensor(ES[:, r, 0], own_lg[:, :, :], AM[:, tq], ALU.subtract).then_inc(am_ready, 1)
                    if on(4):
                        t, r, tq = s - 4, q % 2, q
                        st = Steps(dve, u_step, 5)
                        st.begin(t)
                        waits_apart(dve, ready, [(pa_ready, t + 1), (u_ready, t)])

                        def add_before():
                            dve.tensor_copy(keep4e[:, :], tab["keep"][0:NT, bass.ds(t * B, B)])
                            dve.drain()
                            for j in range(B):
                                before = A[:, tq, j - 1] if j else A[:, (tq - 1) % NRING, B - 1]
                                fade = EE[:, tq, 1, j]
                                dve.tensor_tensor(tmp[:, 0:D].rearrange("p (h c) -> p h c", h=HEADS),
                                                  before[:, 0:D].rearrange("p (h c) -> p h c", h=HEADS),
                                                  fade.unsqueeze(2).broadcast_to([NT, HEADS, HC]), ALU.mult)
                                dve.tensor_tensor(tmp[:, D:], before[:, D:], fade, ALU.mult)
                                dve.drain()
                                dve.scalar_tensor_tensor(A[:, tq, j], tmp[:, :], keep4e[:, j:j + 1], A[:, tq, j], ALU.mult, ALU.add)
                                dve.drain()
                        if not quiet:
                            if_set(dve, tab["carry"], t, add_before)
                        st.mark(dve.tensor_scalar(den[:, :, :], A[:, tq, :, D:], 1e-16, None, ALU.add))
                        st.sync()
                        st.mark(dve.reciprocal(den[:, :, :], den[:, :, :]))
                        st.sync()
                        st.mark(dve.tensor_tensor(by_head(T[:, :, :]), by_head(A[:, tq, :, 0:D]), per_channel(den[:, :, :], NT), ALU.mult))
                        st.sync()
                        dve.wait_ge(xb_ready, t + 1)
                        wait(dve, x3_ready, t - 1)
                        st.mark(dve.tensor_tensor(U[:, r], T[:, :, :], X[:, tq], ALU.add))
                        st.sync()
                        norm_stats(dve, ready, st, U[:, r], stats, mv[:, r]).then_inc(u_ready, 1)
                        st.end()
                quiet_sweep(dve, tab, 5, body)

            @block.scalar
            def _(act):
                act.preload_act_table_set(TABLES)

                def body(s, q, on, quiet):
                    if on(5):
                        t, r = s - 5, (q - 5) % 2
                        act.wait_ge(u_ready, t + 1)
                        wait(act, x3_ready, t - 1)
                        wait(act, rs_ready, t)
                        rstd(act, mv[:, r, :, 1], lg[:, :], rs[:, r], w["eps"][0:NT, :], log_step, t).then_inc(rs_ready, 1)
                    if on(2):
                        t, r = s - 2, q % 2
                        act.wait_ge(a_ready, t + 1)
                        wait(act, pa_made, t - 1)
                        act.activation(R[:, r, :, D:], arg[:, :, :], ACT.Exp).then_inc(p_ready, 1)
                    if on(3):
                        t, tq = s - 3, (q - 3) % NRING
                        act.wait_ge(pa_made, t + 1)
                        wait(act, u_ready, t - 2)
                        act.activation(A[:, tq], pA[:, :, 0:RW], ACT.Copy).then_inc(pa_ready, 1)
                    if on(0):
                        act.wait_ge(st_made, s + 1)
                        wait(act, l2_made, s - 3)
                        act.activation(ST[:, q], pST[:, :, :], ACT.Copy).then_inc(st_ready, 1)
                    if on(6):
                        t, r = s - 6, q % 2
                        act.wait_ge(xt_made, t + 1)
                        wait(act, qv_made, 2 * (t - 1))
                        act.activation(XT[:, r], pXT[:, :, :], ACT.Copy).then_inc(xt_ready, 1)
                    if on(1):
                        t, r, tq = s - 1, (q - 1) % 2, (q - 1) % NRING
                        act.wait_ge(am_ready, t + 1)
                        wait(act, u_ready, t - 3)
                        act.activation(EE[:, tq], ES[:, r], ACT.Exp).then_inc(e_ready, 1)
                    if on(6):
                        t, r, tq = s - 6, q % 2, (q - 6) % NRING
                        wait(act, stored[tq - 2], 32 * lap(t - 2))
                        for i in range(2):
                            act.wait_ge(qv_made, 2 * t + i + 1)
                            act.activation(QV[:, r, 2 * i:2 * i + 2, :], pQV[:, :, :], ACT.Copy).then_inc(qv_ready, 1)
                sweep(act, tab, 6, body)

            @block.tensor
            def _(pe):
                eye = const["eye"]
                bias = w["parts"][:, D:3 * D].unsqueeze(1).broadcast_to([3, 2, 2 * D])

                def body(s, q, on, quiet):
                    if on(1):
                        t, tq = s - 1, (q - 1) % NRING
                        pe.wait_ge(st_ready, t + 1)
                        pe.wait_ge(own[tq], 16 * lap(t))
                        wait(pe, v_ready, t)
                        for j in range(B):
                            last = pe.matmul(pL[:, 0, j * 2 * HEADS:(j + 1) * 2 * HEADS], ST[:, tq, j, :], H[:, tq, j, D:],
                                             start=True, stop=True)
                        last.then_inc(l1_made, 1)
                    if on(2):
                        t, tq = s - 2, (q - 2) % NRING
                        pe.wait_ge(am_ready, t + 1)
                        wait(pe, a_ready, t)
                        for j in range(B):
                            last = pe.matmul(pL[:, 1, j * HEADS:(j + 1) * HEADS], ST[:, tq, j, :], AM[:, tq, j, :],
                                             start=True, stop=True)
                        last.then_inc(l2_made, 1)
                    if on(3):
                        t, r, tq = s - 3, (q - 3) % 2, (q - 3) % NRING
                        pe.wait_ge(r_ready, t + 1)
                        wait(pe, pa_ready, t)
                        for j in range(B):
                            pe.matmul(pA[:, j, 0:RW], S[:, tq, j, :], R[:, r, j, :], start=True, stop=False)
                            last = pe.matmul(pA[:, j, 0:RW], F[:, r, j, :], HS[:, r, j, :], start=False, stop=True)
                        last.then_inc(pa_made, 1)
                    if on(6):
                        t, tq = s - 6, (q - 6) % NRING
                        pe.wait_ge(x3_ready, t + 1)
                        wait(pe, xt_ready, t)
                        for j in range(B):
                            last = pe.transpose(pXT[:, j, :], X3[:, tq, j, :], eye[0:NT, 0:NT])
                        last.then_inc(xt_made, 1)
                    if on(0):
                        pe.wait_ge(s_ready, s + 1)
                        wait(pe, st_ready, s)
                        for j in range(B):
                            last = pe.transpose(pST[:, j, :], S[:, q, j, :], eye[:, :])
                        last.then_inc(st_made, 1)
                    if on(1):
                        t = s - 1
                        pe.wait_ge(v_ready, t + 1)
                        for j in range(B):
                            wait(pe, vt_read, B * t + j - 1)
                            for h in range(HEADS):
                                last = pe.transpose(pV[j % 2][:, h, :], V[:, j, h, :], eye[:, :])
                            last.then_inc(vt_made, 1)
                    if on(6):
                        t, r = s - 6, q % 2
                        pe.wait_ge(xt_ready, t + 1)
                        for i in range(2):
                            wait(pe, qv_ready, 2 * t + i)
                            pe.matmul(pQV[:, :, :], w["ones3"][:, :], bias, start=True, stop=False)
                            for j in range(2):
                                last = pe.matmul(pQV[:, j, :], XT[:, r, 2 * i + j, :], w["qv"][:, :], start=False, stop=(j == 1))
                            last.then_inc(qv_made, 1)
                sweep(pe, tab, 6, body)



def attention_layer(nc, tab, const, w, qv, x3, out):
    with ExitStack() as ctx:
        m = Mem(nc, ctx, "att")
        idx = m.sb("idx", [W, 2, B], I32)
        G = m.sb("gathered", [W, NRING, B, 2 * D])
        Q = m.sb("own_q", [NT, NRING, B, D])
        X = m.sb("own_x", [NT, NRING, B, D])
        S = m.sb("one_hot", [W, NRING, B, NT])
        ST = m.sb("one_hot_T", [NT, 2, B, W])
        junk = m.sb("junk", [W, B, D])
        sc = m.sb("score", [W, 2, B])
        EX = m.sb("exp_score", [W, 2, B])
        SW = m.sb("weighted_one_hot", [W, 2, B, NT])
        ones = m.sb("ones", [W, 1])
        AT = m.sb("sums_T", [D, NRING, B, NT])
        DN = m.sb("denominators", [NT, NRING, B, 1])
        rd = m.sb("reciprocals", [NT, B])
        XB = m.sb("x_bo", [NT, NRING, B, D])
        U = m.sb("summed", [NT, 2, B, D])
        stats = m.sb("stats", [NT, B, 6])
        mv = m.sb("mean_var", [NT, 2, B, 2])
        lg = m.sb("logs", [NT, 2, B])
        rs = m.sb("rstd", [NT, 2, B])
        shift = m.sb("shift", [NT, 2, B])
        Z = m.sb("normalised", [NT, 2, B, D])
        ZG = m.sb("scaled", [NT, B, D])
        U2 = m.sb("summed2", [NT, 2, B, D])
        stats2 = m.sb("stats2", [NT, B, 6])
        mv2 = m.sb("mean_var2", [NT, 2, B, 2])
        rs2 = m.sb("rstd2", [NT, 2, B])
        shift2 = m.sb("shift2", [NT, 2, B])
        O = m.sb("out", [NT, 2, B, D])
        keep4 = m.sb("keep4", [D, B])
        keep4d = m.sb("keep4_den", [NT, B])
        pST = m.ps("one_hot_T", [NT, B, W])
        pQ = m.ps("centre_q", [W, B, D])
        pT = m.ps("sums_T", [D, B, NT])
        pD = m.ps("denominators", [NT, B])
        pZ = m.ps("product", [NT, B, D])
        ready, passed, sp_passed = m.sem("constants_set"), m.sem("waits_passed"), m.sem("sync_waits_passed")
        own, own_x, idx_ready, gathered = (m.sems("own_loaded"), m.sems("own_x_loaded"), m.sem("indices_ready"),
                                           m.sems("gathered"))
        s_ready, st_made, st_ready, q_made = (m.sem("one_hot_ready"), m.sem("one_hot_T_made"), m.sem("one_hot_T_ready"),
                                              m.sem("centre_q_made"))
        c_step, sc_ready, e_ready, sw_ready = m.sem("score_step"), m.sem("score_ready"), m.sem("exp_ready"), m.sem("weighted_ready")
        t_made, t_copied, t_ready, z_made = m.sem("sums_made"), m.sem("sums_copied"), m.sem("sums_ready"), m.sem("product_made")
        u_step, u_ready, log_step, rs_ready = m.sem("summed_step"), m.sem("summed_ready"), m.sem("log_step"), m.sem("rstd_ready")
        sh_ready, n_ready, z_read = m.sem("shift_ready"), m.sem("normalised_ready"), m.sem("product_read")
        u2_step, u2_ready, log2_step, rs2_ready = m.sem("summed2_step"), m.sem("summed2_ready"), m.sem("log2_step"), m.sem("rstd2_ready")
        sh2_ready, o_ready = m.sem("shift2_ready"), m.sem("out_ready")
        xb_ready, xc_ready, stored, part = m.sem("x_bo_ready"), m.sem("x_beta_ready"), m.sems("stored"), m.sem("tiles_moved")
        with nc.Block() as block:

            @block.sync
            def _(sp):
                def body(s, q, on, rows):
                    if on(0):
                        waits_apart(sp, sp_passed, [(q_made, s - 3)])
                        own_rows(sp, tab, s, q, [(qv[:, 0:D], Q[:, q])], own, part, False, rows and rows(s, q, 0))
                    if on(1):
                        t, tq = s - 1, (q - 1) % NRING
                        waits_apart(sp, sp_passed, [(u2_ready, t - 3)])
                        own_rows(sp, tab, t, tq, [(x3, X[:, tq])], own_x, part, False, rows and rows(s, q, 1))
                    if on(7):
                        t, tq = s - 7, (q - 7) % NRING
                        waits_apart(sp, sp_passed, [(o_ready, t + 1)])
                        own_rows(sp, tab, t, tq, [(out, O[:, tq % 2])], stored, part, True, rows and rows(s, q, 7))
                rows_sweep(sp, tab, 7, body, stored, 16)

            @block.gpsimd
            def _(pool):
                bo = w["row_L3_gnn_bo"][0:NT, :].unsqueeze(1).broadcast_to([NT, B, D])
                beta = w["row_L3_gnn_beta"][0:NT, :].unsqueeze(1).broadcast_to([NT, B, D])

                def body(s, q, on, quiet):
                    if on(0):
                        gather_rows(pool, tab, s, q, qv, idx, G, 2 * D, idx_ready, gathered, t_made, s - 3, passed)
                    if on(2):
                        t, tq = s - 2, (q - 2) % NRING
                        pool.wait_ge(own_x[tq], 16 * lap(t))
                        wait(pool, u_ready, t - 3)
                        pool.tensor_tensor(XB[:, tq], X[:, tq], bo, ALU.add).then_inc(xb_ready, 1)
                        pool.wait_ge(xb_ready, t + 1)
                        pool.tensor_tensor(X[:, tq], X[:, tq], beta, ALU.add).then_inc(xc_ready, 1)
                sweep(pool, tab, 2, body)

            @block.vector
            def _(dve):
                dve.memset(DN[:, NRING - 1, B - 1, :], 0.0)
                dve.memset(AT[:, NRING - 1, B - 1, :], 0.0)
                dve.memset(ones[:, :], 1.0).then_inc(ready, 1)
                dve.wait_ge(ready, 1)

                def body(s, q, on, quiet):
                    if on(0):
                        wait(dve, t_made, s - 3)
                        one_hot(dve, const, tab, s, S[:, q]).then_inc(s_ready, 1)
                    if on(1):
                        t, r, tq = s - 1, (q - 1) % 2, (q - 1) % NRING
                        st = Steps(dve, c_step, 2)
                        st.begin(t)
                        dve.wait_ge(q_made, t + 1)
                        dve.wait_ge(gathered[tq], 16 * B * lap(t))
                        wait(dve, e_ready, t - 1)
                        wait(dve, sc_ready, t)
                        st.mark(dve.tensor_tensor(junk[:, :, :], pQ[:, :, :], G[:, tq, :, 0:D], ALU.mult))
                        st.sync()
                        st.mark(dve.tensor_reduce(sc[:, r], junk[:, :, :], AX.X, ALU.add))
                        st.sync()
                        dve.tensor_scalar(sc[:, r], sc[:, r], 5.0 * D ** 0.5, -5.0 * D ** 0.5, ALU.min, ALU.max).then_inc(sc_ready, 1)
                    if on(4):
                        t, r = s - 4, q % 2
                        dve.wait_ge(rs_ready, t + 1)
                        wait(dve, n_ready, t - 1)
                        dve.scalar_tensor_tensor(shift[:, r], mv[:, r, :, 0], -1.0, rs[:, r], ALU.mult, ALU.mult).then_inc(sh_ready, 1)
                    if on(6):
                        t, r = s - 6, q % 2
                        dve.wait_ge(rs2_ready, t + 1)
                        wait(dve, o_ready, t - 1)
                        dve.scalar_tensor_tensor(shift2[:, r], mv2[:, r, :, 0], -1.0, rs2[:, r], ALU.mult, ALU.mult).then_inc(sh2_ready, 1)
                    if on(3):
                        t, tq = s - 3, (q - 3) % NRING
                        waits_apart(dve, ready, [(t_copied, t + 1)])
                        pass_on(dve, tab, t, AT, tq, keep4[:, :], quiet)
                        pass_on(dve, tab, t, DN, tq, keep4d[:, :], quiet)
                        dve.sem_inc(t_ready, 1)
                        st = Steps(dve, u_step, 3)
                        st.begin(t)
                        wait(dve, u_ready, t)
                        st.mark(dve.tensor_scalar(rd[:, :], DN[:, tq, :, 0], 1e-30, None, ALU.max))
                        st.sync()
                        st.mark(dve.reciprocal(rd[:, :], rd[:, :]))
                    if on(5):
                        t, r, tq = s - 5, (q - 5) % 2, (q - 5) % NRING
                        st2 = Steps(dve, u2_step, 3)
                        st2.begin(t)
                        wait(dve, u2_ready, t)
                        dve.wait_ge(n_ready, t + 1)
                        st2.mark(dve.tensor_tensor(ZG[:, :, :], Z[:, r], w["row_L3_gnn_gamma"][0:NT, :].unsqueeze(1).broadcast_to([NT, B, D]), ALU.mult))
                        wait(dve, o_ready, t - 1)
                        dve.wait_ge(xc_ready, t + 1)
                        st2.sync()
                        st2.mark(dve.tensor_tensor(U2[:, r], ZG[:, :, :], X[:, tq], ALU.add))
                        st2.sync()
                        norm_stats(dve, ready, st2, U2[:, r], stats2, mv2[:, r]).then_inc(u2_ready, 1)
                        st2.end()
                    if on(1):
                        t, r, tq = s - 1, (q - 1) % 2, (q - 1) % NRING
                        dve.wait_ge(e_ready, t + 1)
                        wait(dve, t_made, t - 1)
                        dve.tensor_tensor(SW[:, r], S[:, tq], EX[:, r].unsqueeze(2).broadcast_to([W, B, NT]), ALU.mult).then_inc(sw_ready, 1)
                    if on(3):
                        t, r, tq = s - 3, (q - 3) % 2, (q - 3) % NRING
                        dve.wait_ge(z_made, t + 1)
                        dve.wait_ge(xb_ready, t + 1)
                        wait(dve, n_ready, t - 1)
                        st.sync()
                        for j in range(B):
                            last = dve.scalar_tensor_tensor(U[:, r, j, :], pZ[:, j, :], rd[:, j:j + 1], XB[:, tq, j, :], ALU.mult, ALU.add)
                        last.then_inc(z_read, 1)
                        dve.wait_ge(z_read, t + 1)
                        norm_stats(dve, ready, st, U[:, r], stats, mv[:, r]).then_inc(u_ready, 1)
                        st.end()
                quiet_sweep(dve, tab, 6, body)

            @block.scalar
            def _(act):
                act.preload_act_table_set(TABLES)

                def body(s, q, on, quiet):
                    if on(6):
                        t, r = s - 6, q % 2
                        act.wait_ge(u2_ready, t + 1)
                        wait(act, sh2_ready, t - 1)
                        wait(act, o_ready, t - 1)
                        act.activation(lg[:, 1], mv2[:, r, :, 1], ACT.Ln, bias=w["eps"][0:NT, :]).then_inc(log2_step, 1)
                    if on(4):
                        t, r = s - 4, q % 2
                        act.wait_ge(u_ready, t + 1)
                        wait(act, sh_ready, t - 1)
                        wait(act, n_ready, t - 1)
                        rstd(act, mv[:, r, :, 1], lg[:, 0], rs[:, r], w["eps"][0:NT, :], log_step, t).then_inc(rs_ready, 1)
                    if on(6):
                        t, r = s - 6, q % 2
                        act.wait_ge(log2_step, t + 1)
                        act.activation(rs2[:, r], lg[:, 1], ACT.Exp, scale=-0.5).then_inc(rs2_ready, 1)
                    if on(0):
                        act.wait_ge(st_made, s + 1)
                        wait(act, q_made, s - 1)
                        act.activation(ST[:, q % 2], pST[:, :, :], ACT.Copy).then_inc(st_ready, 1)
                    if on(2):
                        t, tq = s - 2, (q - 2) % NRING
                        act.wait_ge(t_made, t + 1)
                        wait(act, z_made, t - 3)
                        wait(act, u_ready, t - 2)
                        act.activation(DN[:, tq, :, 0], pD[:, :], ACT.Copy)
                        act.activation(AT[:, tq], pT[:, :, :], ACT.Copy).then_inc(t_copied, 1)
                    if on(1):
                        t, r = s - 1, (q - 1) % 2
                        act.wait_ge(sc_ready, t + 1)
                        wait(act, sw_ready, t - 1)
                        act.activation(EX[:, r], sc[:, r], ACT.Exp, scale=D ** -0.5).then_inc(e_ready, 1)
                    if on(4):
                        t, r = s - 4, q % 2
                        act.wait_ge(sh_ready, t + 1)
                        wait(act, u2_ready, t - 1)
                        for j in range(B):
                            last = act.activation(Z[:, r, j, :], U[:, r, j, :], ACT.Identity, scale=rs[:, r, j:j + 1], bias=shift[:, r, j:j + 1])
                        last.then_inc(n_ready, 1)
                    if on(6):
                        t, r, tq = s - 6, q % 2, (q - 6) % NRING
                        act.wait_ge(sh2_ready, t + 1)
                        wait(act, stored[tq - 2], 16 * lap(t - 2))
                        for j in range(B):
                            last = act.activation(O[:, r, j, :], U2[:, r, j, :], ACT.Identity, scale=rs2[:, r, j:j + 1], bias=shift2[:, r, j:j + 1])
                        last.then_inc(o_ready, 1)
                sweep(act, tab, 6, body)

            @block.tensor
            def _(pe):
                def body(s, q, on, quiet):
                    if on(2):
                        t, r, tq = s - 2, q % 2, (q - 2) % NRING
                        pe.wait_ge(sw_ready, t + 1)
                        wait(pe, t_copied, t)
                        for j in range(B):
                            pe.matmul(pT[:, j, :], G[:, tq, j, D:], SW[:, r, j, :], start=True, stop=True)
                            last = pe.matmul(pD[:, j:j + 1], SW[:, r, j, :], ones[:, :], start=True, stop=True)
                        last.then_inc(t_made, 1)
                    if on(1):
                        t, r, tq = s - 1, (q - 1) % 2, (q - 1) % NRING
                        pe.wait_ge(st_ready, t + 1)
                        pe.wait_ge(own[tq], 16 * lap(t))
                        wait(pe, sc_ready, t)
                        for j in range(B):
                            last = pe.matmul(pQ[:, j, :], ST[:, r, j, :], Q[:, tq, j, :], start=True, stop=True)
                        last.then_inc(q_made, 1)
                    if on(0):
                        pe.wait_ge(s_ready, s + 1)
                        wait(pe, st_ready, s)
                        for j in range(B):
                            last = pe.transpose(pST[:, j, :], S[:, q, j, :], const["eye"][:, :])
                        last.then_inc(st_made, 1)
                    if on(3):
                        t, tq = s - 3, (q - 3) % NRING
                        pe.wait_ge(t_ready, t + 1)
                        wait(pe, z_read, t)
                        for j in range(B):
                            last = pe.matmul(pZ[:, j, :], AT[:, tq, j, :], w["L3_gnn_Wo"][:, :], start=True, stop=True)
                        last.then_inc(z_made, 1)
                sweep(pe, tab, 3, body)



def four_graph_layers(nc, ins, out):
    def scratch(name, shape):
        return nc.dram_tensor(name, shape, F32, kind="Internal").ap()

    hist = {k: scratch(f"hist_{k}", [TILES]) for k in KEYS}
    item_rows = {k: scratch(f"item_rows_{k}", [3, MAXI]) for k in KEYS}
    x1, x2, x3 = (scratch(f"x{i}", [N, D]) for i in (1, 2, 3))
    y1, y2 = scratch("y1", [N, D]), scratch("y2", [N, D])
    h = scratch("gat_rows", [N, D + 2 * HEADS])
    qv = scratch("qv", [N, 2 * D])
    with ExitStack() as ctx:
        keep = Mem(nc, ctx, "keep")
        const = dict(eye=keep.sb("eye", [128, 128]), neg_eye=keep.sb("neg_eye", [128, 128]), iota=keep.sb("iota", [128, NT]))
        tab = sort_edges(nc, keep, {k: ins[k] for k in KEYS}, hist, item_rows, const)
        w = load_weights(nc, keep, ins, const)
        dis = keep.sb("inverse_root_degree", [NT, MAXI])
        gated_layer(nc, tab["dst"], const, w, dis, ins["x"], x1, y1)
        convolution(nc, tab["dst"], const, w, dis, "conv1", "L1_gnn_W1", "L1_gnn_b1", y1, y_out=y2)
        convolution(nc, tab["dst"], const, w, dis, "conv2", "L1_gnn_W2", "L1_gnn_b2", y2, x_in=x1, x_out=x2, gat=h)
        gat_layer(nc, tab["src"], const, w, h, x2, x3, qv)
        attention_layer(nc, tab["dst"], const, w, qv, x3, out)


_INS = ['x', 'src', 'dst', 'L0_gnn_W1', 'L0_gnn_b1', 'L0_gnn_W2', 'L0_gnn_b2', 'L0_gnn_W4', 'L0_gnn_b4',
        'L1_gnn_W1', 'L1_gnn_b1', 'L1_gnn_W2', 'L1_gnn_b2', 'L2_gnn_weight', 'L2_gnn_att', 'L2_gnn_bias',
        'L3_gnn_Wqk', 'L3_gnn_bqk', 'L3_gnn_Wv', 'L3_gnn_bv', 'L3_gnn_Wo', 'L3_gnn_bo', 'L3_gnn_gamma', 'L3_gnn_beta']
_OUTS = [((50000, 128), 'float32')]


def kernel(**inputs):
    import numpy as _np
    import concourse.bacc as _bacc
    from concourse import mybir as _mybir
    from concourse.bass_utils import run_bass_kernel_spmd as _run

    nc = _bacc.Bacc("TRN2", target_bir_lowering=False, num_devices=1)
    arrays, ins, outs = {}, {}, []
    for name in _INS:
        a = _np.ascontiguousarray(inputs[name])
        arrays[f"in_{name}_dram"] = a
        ins[name] = nc.dram_tensor(f"in_{name}_dram", a.shape, _mybir.dt.from_np(a.dtype), kind="ExternalInput").ap()
    for i, (shape, dtype) in enumerate(_OUTS):
        dt = _mybir.dt.from_np(_np.dtype(dtype))
        outs.append(nc.dram_tensor(f"out_{i}_dram", shape, dt, kind="ExternalOutput").ap())
    four_graph_layers(nc, ins, outs[0])
    r = _run(nc, [arrays], core_ids=[0])
    return r.results[0]["out_0_dram"]
```
